# Optimizing a Trainium2 kernel written in Bass

```python
import numpy as np
import jax
import jax.numpy as jnp

def _softmax(x, axis=-1):
    return jax.nn.softmax(x, axis=axis)

def _gelu(x):
    return jax.nn.gelu(x, approximate=True)

def _silu(x):
    return jax.nn.silu(x)

def _sigmoid(x):
    return jax.nn.sigmoid(x)

def _layernorm(x, axis=-1, eps=1e-05):
    m = jnp.mean(x, axis=axis, keepdims=True)
    v = jnp.var(x, axis=axis, keepdims=True)
    return (x - m) / jnp.sqrt(v + eps)

def _scatter_add(tgt, idx, src, axis=0):
    return tgt.at[idx].add(src)

def _segment_sum(src, seg, n):
    return jax.ops.segment_sum(src, seg, n)
kernel_name = 'mk_seq_preln_d2_jaxref_r8_c1ba9e'

def setup_inputs(seed: int=0):
    np.random.seed(seed)
    _w = jnp.asarray

    def _L0_attn_setup():
        import jax, jax.numpy as jnp
        import numpy as np
        from jax import lax
        D_MODEL, D_STATE, D_CONV, D_INNER, DT_RANK = (128, 16, 4, 256, 64)
        B_SZ, SEQ = (2, 128)

        def silu(v):
            return v * jax.nn.sigmoid(v)

        def _mamba_fwd(x, W_in, conv_w, conv_b, W_x, W_dt, b_dt, A_log, D, W_out):
            b, l, _ = x.shape
            xz = x @ W_in
            x_e, z = jnp.split(xz, 2, axis=-1)
            xc = lax.conv_general_dilated(x_e.transpose(0, 2, 1), conv_w, window_strides=(1,), padding=[(D_CONV - 1, 0)], dimension_numbers=('NCH', 'OIH', 'NCH'), feature_group_count=D_INNER)
            xc = (xc + conv_b[None, :, None]).transpose(0, 2, 1)
            xc = silu(xc)
            x_dbl = xc @ W_x
            delta_r = x_dbl[..., :DT_RANK]
            Bmat = x_dbl[..., DT_RANK:DT_RANK + D_STATE]
            Cmat = x_dbl[..., DT_RANK + D_STATE:]
            delta = jax.nn.softplus(delta_r @ W_dt + b_dt)
            A = -jnp.exp(A_log)
            deltaA = jnp.exp(delta[..., None] * A[None, None])
            deltaB_x = delta[..., None] * Bmat[:, :, None, :] * xc[..., None]

            def combine(left, right):
                a_l, b_l = left
                a_r, b_r = right
                return (a_r * a_l, a_r * b_l + b_r)
            _, H = lax.associative_scan(combine, (deltaA, deltaB_x), axis=1)
            y = jnp.einsum('bldn,bln->bld', H, Cmat) + xc * D[None, None, :]
            y = y * silu(z)
            return y @ W_out
        key = jax.random.key(seed)
        ks = jax.random.split(key, 10)
        s = lambda fan: 1.0 / np.sqrt(fan)
        x = jax.random.normal(ks[0], (B_SZ, SEQ, D_MODEL), jnp.float32)
        W_in = jax.random.normal(ks[1], (D_MODEL, 2 * D_INNER), jnp.float32) * s(D_MODEL)
        conv_w = jax.random.normal(ks[2], (D_INNER, 1, D_CONV), jnp.float32) * s(D_CONV)
        conv_b = jax.random.normal(ks[3], (D_INNER,), jnp.float32) * 0.01
        W_x = jax.random.normal(ks[4], (D_INNER, DT_RANK + 2 * D_STATE), jnp.float32) * s(D_INNER)
        W_dt = jax.random.normal(ks[5], (DT_RANK, D_INNER), jnp.float32) * s(DT_RANK)
        b_dt = jax.random.normal(ks[6], (D_INNER,), jnp.float32) * 0.01
        A_log = jnp.log(jnp.tile(jnp.arange(1, D_STATE + 1, dtype=jnp.float32), (D_INNER, 1)))
        Dparam = jnp.ones((D_INNER,), jnp.float32)
        W_out = jax.random.normal(ks[7], (D_INNER, D_MODEL), jnp.float32) * s(D_INNER)
        return {'x': x, 'W_in': W_in, 'conv_w': conv_w, 'conv_b': conv_b, 'W_x': W_x, 'W_dt': W_dt, 'b_dt': b_dt, 'A_log': A_log, 'D': Dparam, 'W_out': W_out}
    _L0_attn_in = _L0_attn_setup()

    def _L0_ffn_setup():
        import jax, jax.numpy as jnp
        import numpy as np
        D, H, E, K = (128, 512, 8, 2)
        B, T = (2, 256)

        def _layernorm(x, g, b, eps=1e-05):
            mu = jnp.mean(x, axis=-1, keepdims=True)
            var = jnp.mean(jnp.square(x - mu), axis=-1, keepdims=True)
            return (x - mu) * jax.lax.rsqrt(var + eps) * g + b

        def _expert(x, g, b, W1, b1, W2, b2, Wo, bo):
            x = _layernorm(x, g, b)
            x1 = x @ W1 + b1
            x2 = jnp.clip(x @ W2 + b2, -20.0, 20.0)
            hidden = jnp.clip(x1 * (x2 * jax.nn.sigmoid(x2)), -10000.0, 10000.0)
            return jnp.clip(hidden @ Wo + bo, -10000.0, 10000.0)
        key = jax.random.key(seed)
        ks = jax.random.split(key, 6)
        s = 0.02
        return {'x': jax.random.normal(ks[0], (B, T, D), jnp.float32), 'ln_g': jnp.ones((D,), jnp.float32), 'ln_b': jnp.zeros((D,), jnp.float32), 'router_w': jax.random.normal(ks[1], (D, E), jnp.float32) * s, 'eg': jnp.ones((E, D), jnp.float32), 'eb': jnp.zeros((E, D), jnp.float32), 'W1': jax.random.normal(ks[2], (E, D, H), jnp.float32) * s, 'b1': jnp.zeros((E, H), jnp.float32), 'W2': jax.random.normal(ks[3], (E, D, H), jnp.float32) * s, 'b2': jnp.zeros((E, H), jnp.float32), 'Wo': jax.random.normal(ks[4], (E, H, D), jnp.float32) * s, 'bo': jnp.zeros((E, D), jnp.float32)}
    _L0_ffn_in = _L0_ffn_setup()

    def _L1_attn_setup():
        import jax, jax.numpy as jnp
        import numpy as np
        HIDDEN = 128
        NUM_HEADS = 16
        HEAD = HIDDEN // NUM_HEADS
        LEFT = 64
        RIGHT = 8
        NUM_POS = LEFT + RIGHT + 1
        key = jax.random.key(seed)
        ks = jax.random.split(key, 10)
        s = 1.0 / np.sqrt(HIDDEN)
        return {'hidden_states': jax.random.normal(ks[0], (4, 256, HIDDEN), jnp.float32), 'Wq': jax.random.normal(ks[1], (HIDDEN, HIDDEN), jnp.float32) * s, 'bq': jax.random.normal(ks[2], (HIDDEN,), jnp.float32) * 0.01, 'Wk': jax.random.normal(ks[3], (HIDDEN, HIDDEN), jnp.float32) * s, 'bk': jax.random.normal(ks[4], (HIDDEN,), jnp.float32) * 0.01, 'Wv': jax.random.normal(ks[5], (HIDDEN, HIDDEN), jnp.float32) * s, 'bv': jax.random.normal(ks[6], (HIDDEN,), jnp.float32) * 0.01, 'Wo': jax.random.normal(ks[7], (HIDDEN, HIDDEN), jnp.float32) * s, 'bo': jax.random.normal(ks[8], (HIDDEN,), jnp.float32) * 0.01, 'dist_emb': jax.random.normal(ks[9], (NUM_POS, HEAD), jnp.float32)}
    _L1_attn_in = _L1_attn_setup()

    def _L1_ffn_setup():
        import jax, jax.numpy as jnp
        import numpy as np
        DIM = 128
        HID = 352
        N_ROUTED = 7
        TOPK = 2
        B, S = (4, 256)

        def _expert(x, wg, wu, wd):
            return jax.nn.silu(x @ wg) * (x @ wu) @ wd
        key = jax.random.key(seed)
        ks = jax.random.split(key, 9)
        s = 0.02
        x = jax.random.normal(ks[0], (B, S, DIM), jnp.float32)
        shared_gate = jax.random.normal(ks[1], (DIM, HID), jnp.float32) * s
        shared_up = jax.random.normal(ks[2], (DIM, HID), jnp.float32) * s
        shared_down = jax.random.normal(ks[3], (HID, DIM), jnp.float32) * s
        routed_gate = jax.random.normal(ks[4], (N_ROUTED, DIM, HID), jnp.float32) * s
        routed_up = jax.random.normal(ks[5], (N_ROUTED, DIM, HID), jnp.float32) * s
        routed_down = jax.random.normal(ks[6], (N_ROUTED, HID, DIM), jnp.float32) * s
        Wr = jax.random.normal(ks[7], (DIM, N_ROUTED), jnp.float32) * s
        routing_bias = jax.random.normal(ks[8], (N_ROUTED,), jnp.float32)
        return dict(x=x, shared_gate=shared_gate, shared_up=shared_up, shared_down=shared_down, routed_gate=routed_gate, routed_up=routed_up, routed_down=routed_down, Wr=Wr, routing_bias=routing_bias)
    _L1_ffn_in = _L1_ffn_setup()
    _d = {'L0_attn_x': _L0_attn_in['x'], 'L0_attn_W_in': _L0_attn_in['W_in'], 'L0_attn_conv_w': _L0_attn_in['conv_w'], 'L0_attn_conv_b': _L0_attn_in['conv_b'], 'L0_attn_W_x': _L0_attn_in['W_x'], 'L0_attn_W_dt': _L0_attn_in['W_dt'], 'L0_attn_b_dt': _L0_attn_in['b_dt'], 'L0_attn_A_log': _L0_attn_in['A_log'], 'L0_attn_D': _L0_attn_in['D'], 'L0_attn_W_out': _L0_attn_in['W_out'], 'L0_ffn_ln_g': _L0_ffn_in['ln_g'], 'L0_ffn_ln_b': _L0_ffn_in['ln_b'], 'L0_ffn_router_w': _L0_ffn_in['router_w'], 'L0_ffn_eg': _L0_ffn_in['eg'], 'L0_ffn_eb': _L0_ffn_in['eb'], 'L0_ffn_W1': _L0_ffn_in['W1'], 'L0_ffn_b1': _L0_ffn_in['b1'], 'L0_ffn_W2': _L0_ffn_in['W2'], 'L0_ffn_b2': _L0_ffn_in['b2'], 'L0_ffn_Wo': _L0_ffn_in['Wo'], 'L0_ffn_bo': _L0_ffn_in['bo'], 'L1_attn_Wq': _L1_attn_in['Wq'], 'L1_attn_bq': _L1_attn_in['bq'], 'L1_attn_Wk': _L1_attn_in['Wk'], 'L1_attn_bk': _L1_attn_in['bk'], 'L1_attn_Wv': _L1_attn_in['Wv'], 'L1_attn_bv': _L1_attn_in['bv'], 'L1_attn_Wo': _L1_attn_in['Wo'], 'L1_attn_bo': _L1_attn_in['bo'], 'L1_attn_dist_emb': _L1_attn_in['dist_emb'], 'L1_ffn_shared_gate': _L1_ffn_in['shared_gate'], 'L1_ffn_shared_up': _L1_ffn_in['shared_up'], 'L1_ffn_shared_down': _L1_ffn_in['shared_down'], 'L1_ffn_routed_gate': _L1_ffn_in['routed_gate'], 'L1_ffn_routed_up': _L1_ffn_in['routed_up'], 'L1_ffn_routed_down': _L1_ffn_in['routed_down'], 'L1_ffn_Wr': _L1_ffn_in['Wr'], 'L1_ffn_routing_bias': _L1_ffn_in['routing_bias']}
    _x0 = _d['L0_attn_x']
    _d['L0_attn_x'] = jax.random.normal(jax.random.fold_in(jax.random.key(seed), 1), (4, 1024, 128), dtype=_x0.dtype)
    del _x0
    return _d

def reference(L0_attn_x, L0_attn_W_in, L0_attn_conv_w, L0_attn_conv_b, L0_attn_W_x, L0_attn_W_dt, L0_attn_b_dt, L0_attn_A_log, L0_attn_D, L0_attn_W_out, L0_ffn_ln_g, L0_ffn_ln_b, L0_ffn_router_w, L0_ffn_eg, L0_ffn_eb, L0_ffn_W1, L0_ffn_b1, L0_ffn_W2, L0_ffn_b2, L0_ffn_Wo, L0_ffn_bo, L1_attn_Wq, L1_attn_bq, L1_attn_Wk, L1_attn_bk, L1_attn_Wv, L1_attn_bv, L1_attn_Wo, L1_attn_bo, L1_attn_dist_emb, L1_ffn_shared_gate, L1_ffn_shared_up, L1_ffn_shared_down, L1_ffn_routed_gate, L1_ffn_routed_up, L1_ffn_routed_down, L1_ffn_Wr, L1_ffn_routing_bias):

    def _L0_attn_ref(x, W_in, conv_w, conv_b, W_x, W_dt, b_dt, A_log, D, W_out):
        import jax, jax.numpy as jnp
        import numpy as np
        from jax import lax
        D_MODEL, D_STATE, D_CONV, D_INNER, DT_RANK = (128, 16, 4, 256, 64)
        B_SZ, SEQ = (2, 128)

        def silu(v):
            return v * jax.nn.sigmoid(v)

        def _mamba_fwd(x, W_in, conv_w, conv_b, W_x, W_dt, b_dt, A_log, D, W_out):
            b, l, _ = x.shape
            xz = x @ W_in
            x_e, z = jnp.split(xz, 2, axis=-1)
            xc = lax.conv_general_dilated(x_e.transpose(0, 2, 1), conv_w, window_strides=(1,), padding=[(D_CONV - 1, 0)], dimension_numbers=('NCH', 'OIH', 'NCH'), feature_group_count=D_INNER)
            xc = (xc + conv_b[None, :, None]).transpose(0, 2, 1)
            xc = silu(xc)
            x_dbl = xc @ W_x
            delta_r = x_dbl[..., :DT_RANK]
            Bmat = x_dbl[..., DT_RANK:DT_RANK + D_STATE]
            Cmat = x_dbl[..., DT_RANK + D_STATE:]
            delta = jax.nn.softplus(delta_r @ W_dt + b_dt)
            A = -jnp.exp(A_log)
            deltaA = jnp.exp(delta[..., None] * A[None, None])
            deltaB_x = delta[..., None] * Bmat[:, :, None, :] * xc[..., None]

            def combine(left, right):
                a_l, b_l = left
                a_r, b_r = right
                return (a_r * a_l, a_r * b_l + b_r)
            _, H = lax.associative_scan(combine, (deltaA, deltaB_x), axis=1)
            y = jnp.einsum('bldn,bln->bld', H, Cmat) + xc * D[None, None, :]
            y = y * silu(z)
            return y @ W_out
        return _mamba_fwd(x, W_in, conv_w, conv_b, W_x, W_dt, b_dt, A_log, D, W_out)

    def _L0_ffn_ref(x, ln_g, ln_b, router_w, eg, eb, W1, b1, W2, b2, Wo, bo):
        import jax, jax.numpy as jnp
        import numpy as np
        D, H, E, K = (128, 512, 8, 2)
        B, T = (2, 256)

        def _layernorm(x, g, b, eps=1e-05):
            mu = jnp.mean(x, axis=-1, keepdims=True)
            var = jnp.mean(jnp.square(x - mu), axis=-1, keepdims=True)
            return (x - mu) * jax.lax.rsqrt(var + eps) * g + b

        def _expert(x, g, b, W1, b1, W2, b2, Wo, bo):
            x = _layernorm(x, g, b)
            x1 = x @ W1 + b1
            x2 = jnp.clip(x @ W2 + b2, -20.0, 20.0)
            hidden = jnp.clip(x1 * (x2 * jax.nn.sigmoid(x2)), -10000.0, 10000.0)
            return jnp.clip(hidden @ Wo + bo, -10000.0, 10000.0)
        Bb, Tt, Dd = x.shape
        xf = _layernorm(x.reshape(-1, Dd), ln_g, ln_b)
        N = xf.shape[0]
        logits = xf @ router_w
        scores, idx = jax.lax.top_k(logits, K)
        gate = jax.nn.softmax(scores, axis=-1)
        gates_e = jnp.zeros((N, E), xf.dtype).at[jnp.arange(N)[:, None], idx].add(gate)

        def body(acc, p):
            gcol, g, b, w1, bb1, w2, bb2, wo, bbo = p
            return (acc + gcol[:, None] * _expert(xf, g, b, w1, bb1, w2, bb2, wo, bbo), None)
        out, _ = jax.lax.scan(body, jnp.zeros_like(xf), (gates_e.T, eg, eb, W1, b1, W2, b2, Wo, bo))
        return out.reshape(Bb, Tt, Dd)

    def _L1_attn_ref(hidden_states, Wq, bq, Wk, bk, Wv, bv, Wo, bo, dist_emb):
        import jax, jax.numpy as jnp
        import numpy as np
        HIDDEN = 128
        NUM_HEADS = 16
        HEAD = HIDDEN // NUM_HEADS
        LEFT = 64
        RIGHT = 8
        NUM_POS = LEFT + RIGHT + 1
        B, L, H = hidden_states.shape
        scale = 1.0 / np.sqrt(HEAD)

        def proj(W, b):
            return (hidden_states @ W.T + b).reshape(B, L, NUM_HEADS, HEAD).transpose(0, 2, 1, 3)
        q = proj(Wq, bq)
        k = proj(Wk, bk)
        v = proj(Wv, bv)
        attn = jnp.einsum('bhld,bhrd->bhlr', q, k) * scale
        dist = jnp.arange(L)[None, :] - jnp.arange(L)[:, None]
        dist = jnp.clip(dist, -LEFT, RIGHT) + LEFT
        pos_emb = dist_emb[dist]
        rel = jnp.einsum('bhld,lrd->bhlr', q, pos_emb) * scale
        attn = jax.nn.softmax(attn + rel, axis=-1)
        out = jnp.einsum('bhlr,bhrd->bhld', attn, v)
        out = out.transpose(0, 2, 1, 3).reshape(B, L, H)
        return out @ Wo.T + bo

    def _L1_ffn_ref(x, shared_gate, shared_up, shared_down, routed_gate, routed_up, routed_down, Wr, routing_bias):
        import jax, jax.numpy as jnp
        import numpy as np
        DIM = 128
        HID = 352
        N_ROUTED = 7
        TOPK = 2
        B, S = (4, 256)

        def _expert(x, wg, wu, wd):
            return jax.nn.silu(x @ wg) * (x @ wu) @ wd
        b, s, d = x.shape
        n_exp = routed_gate.shape[0]
        shared_out = _expert(x, shared_gate, shared_up, shared_down)
        logits = x @ Wr * routing_bias
        probs = jax.nn.sigmoid(logits)
        scores, idx = jax.lax.top_k(probs, TOPK)
        scores = scores / scores.sum(-1, keepdims=True)
        t = b * s
        xf = x.reshape(t, d)
        weights = jnp.zeros((t, n_exp), x.dtype).at[jnp.arange(t)[:, None], idx.reshape(t, TOPK)].add(scores.reshape(t, TOPK))
        combined = jnp.zeros_like(xf)
        for e in range(n_exp):
            combined = combined + _expert(xf, routed_gate[e], routed_up[e], routed_down[e]) * weights[:, e:e + 1]
        return shared_out + combined.reshape(b, s, d)
    x = L0_attn_x
    x = x + _L0_attn_ref(_layernorm(x, axis=-1), L0_attn_W_in, L0_attn_conv_w, L0_attn_conv_b, L0_attn_W_x, L0_attn_W_dt, L0_attn_b_dt, L0_attn_A_log, L0_attn_D, L0_attn_W_out)
    x = x + _L0_ffn_ref(_layernorm(x, axis=-1), L0_ffn_ln_g, L0_ffn_ln_b, L0_ffn_router_w, L0_ffn_eg, L0_ffn_eb, L0_ffn_W1, L0_ffn_b1, L0_ffn_W2, L0_ffn_b2, L0_ffn_Wo, L0_ffn_bo)
    x = x + _L1_attn_ref(_layernorm(x, axis=-1), L1_attn_Wq, L1_attn_bq, L1_attn_Wk, L1_attn_bk, L1_attn_Wv, L1_attn_bv, L1_attn_Wo, L1_attn_bo, L1_attn_dist_emb)
    x = x + _L1_ffn_ref(_layernorm(x, axis=-1), L1_ffn_shared_gate, L1_ffn_shared_up, L1_ffn_shared_down, L1_ffn_routed_gate, L1_ffn_routed_up, L1_ffn_routed_down, L1_ffn_Wr, L1_ffn_routing_bias)
    return x

_drawn_inputs = setup_inputs


def setup_inputs(seed=0):
    import zlib

    import numpy as np

    out = dict(_drawn_inputs(seed))
    spreads = {'L0_attn_D': (1.0, 0.2),
     'L0_ffn_ln_g': (1.0, 0.6),
     'L0_ffn_ln_b': (0.0, 0.424),
     'L0_ffn_eg': (1.0, 0.6),
     'L0_ffn_eb': (0.0, 0.8),
     'L0_ffn_b1': (0.0, 0.8),
     'L0_ffn_b2': (0.0, 0.8),
     'L0_ffn_bo': (0.0, 0.385)}
    factors = {'L0_attn_conv_b': 6.35,
     'L0_attn_b_dt': 8.0,
     'L0_ffn_W1': 6.96,
     'L0_ffn_W2': 7.003,
     'L0_ffn_Wo': 6.417,
     'L1_attn_bq': 51.48,
     'L1_attn_bk': 64.0,
     'L1_attn_bv': 6.645,
     'L1_attn_bo': 18.41,
     'L1_ffn_shared_gate': 7.46,
     'L1_ffn_shared_up': 7.386,
     'L1_ffn_shared_down': 7.436,
     'L1_ffn_routed_gate': 8.0,
     'L1_ffn_routed_up': 8.0,
     'L1_ffn_routed_down': 8.0,
     'L1_ffn_Wr': 8.0,
     'L1_ffn_routing_bias': 8.0,
     'L1_attn_dist_emb': 3.881}
    for name, (base, spread) in spreads.items():
        noise = np.random.default_rng([zlib.crc32(name.encode()), seed]).standard_normal(out[name].shape)
        drawn = base * np.exp(spread * noise) if base else spread * noise
        out[name] = jnp.asarray(drawn.astype(out[name].dtype))
    for name, factor in factors.items():
        out[name] = (out[name] * factor).astype(out[name].dtype)
    return out
```

```python
from contextlib import ExitStack

import concourse.bass as bass
from concourse import mybir

P = 128
F32 = mybir.dt.float32
BF16 = mybir.dt.bfloat16
U32 = mybir.dt.uint32
I32 = mybir.dt.int32
ALU = mybir.AluOpType
ACT = mybir.ActivationFunctionType
AX = mybir.AxisListType.X
ds = bass.ds
EPS = 1e-5


class Steps:

    def __init__(self, eng, sem, base=0):
        self.eng, self.sem, self.base, self.n = eng, sem, base, 0

    def __call__(self, ins):
        ins.then_inc(self.sem, 1)
        self.n += 1
        self.eng.wait_ge(self.sem, self.base + self.n)


class Room:

    def __init__(self, nc, prefix):
        self.nc, self.prefix, self.ctx, self.sems = nc, prefix, ExitStack(), []

    def sb(self, name, shape, dt=F32):
        return self.ctx.enter_context(self.nc.sbuf_tensor(f"{self.prefix}_{name}", shape, dt))

    def ps(self, name, shape, dt=F32):
        return self.ctx.enter_context(self.nc.psum_tensor(f"{self.prefix}_{name}", shape, dt))

    def sem(self, name):
        self.sems.append(self.nc.alloc_semaphore(name=f"{self.prefix}_{name}"))
        return self.sems[-1]

    def __enter__(self):
        return self

    def __exit__(self, *a):
        self.nc.clear_and_free_semaphores(self.sems)
        self.nc.all_engine_barrier()
        self.ctx.close()


def load_constants(nc, x, X, ident):
    with Room(nc, "init") as room:
        loaded, built = room.sem("x_loaded"), room.sem("ident_built")
        with nc.Block() as block:
            @block.sync
            def _(sp):
                src = x.rearrange("b (t p) d -> p (b t) d", p=P)
                half = X.shape[1] // 2
                sp.dma_start(X[:, 0:half, :], src[:, 0:half, :]).then_inc(loaded, 16)
                sp.dma_start(X[:, half:, :], src[:, half:, :]).then_inc(loaded, 16)
                sp.wait_ge(loaded, 32)

            @block.gpsimd
            def _(pool):
                pool.memset(ident[:, :], 0.0).then_inc(built, 1)
                pool.wait_ge(built, 1)
                pool.affine_select(out=ident[:, :], in_=ident[:, :], compare_op=ALU.not_equal, fill=1.0,
                                   base=0, pattern=[[-1, P]], channel_multiplier=1).then_inc(built, 1)
                pool.wait_ge(built, 2)


def layernorm(nc, name, src, out, outT, ident, var_scale=1.0, var_bias=EPS, gb=None):
    T, D = src.shape[1], src.shape[2]
    with Room(nc, name) as room:
        sq = room.sb("sq", [P, T, D])
        mean, var, rstd = room.sb("mean", [P, T]), room.sb("var", [P, T]), room.sb("rstd", [P, T])
        tp = room.ps("tp", [P, 4, 4, P])
        dve_step, centred, squared, spread = (room.sem(s) for s in ("dve_step", "centred", "squared", "spread"))
        rooted, normed, turned, copied, epsed = (room.sem(s) for s in ("rooted", "normed", "turned", "copied", "epsed"))
        eps = room.sb("eps", [P, 1])

        def wide(m):
            return m[:, :].rearrange("p (t o) -> p t o", o=1).broadcast_to([P, T, D])

        with nc.Block() as block:
            @block.vector
            def _(dve):
                step = Steps(dve, dve_step)
                dve.memset(eps[:, :], var_bias).then_inc(epsed, 1)
                step(dve.tensor_reduce(mean[:, :], src[:, :, :], AX, ALU.add))
                step(dve.tensor_scalar(mean[:, :], mean[:, :], 1.0 / D, None, ALU.mult))
                dve.tensor_tensor(out[:, :, :], src[:, :, :], wide(mean), ALU.subtract).then_inc(centred, 1)
                dve.wait_ge(squared, 1)
                dve.tensor_reduce(var[:, :], sq[:, :, :], AX, ALU.add).then_inc(spread, 1)
                dve.wait_ge(rooted, 1)
                step(dve.reciprocal(rstd[:, :], rstd[:, :]))
                dve.wait_ge(centred, 1)
                last = dve.tensor_tensor(out[:, :, :], out[:, :, :], wide(rstd), ALU.mult)
                if gb is not None:
                    step(last)
                    for which, op in ((gb[0], ALU.mult), (gb[1], ALU.add)):
                        v = which[:, :].rearrange("p (o d) -> p o d", o=1).broadcast_to([P, T, D])
                        last = dve.tensor_tensor(out[:, :, :], out[:, :, :], v, op)
                        if op == ALU.mult:
                            step(last)
                last.then_inc(normed, 1)
                dve.wait_ge(normed, 1)

            @block.scalar
            def _(act):
                act.wait_ge(centred, 1)
                nc.scalar.activation(sq[:, :, :], out[:, :, :], ACT.Square).then_inc(squared, 1)
                act.wait_ge(spread, 1)
                act.wait_ge(epsed, 1)
                nc.scalar.activation(rstd[:, :], var[:, :], ACT.Sqrt, scale=var_scale / D,
                                     bias=eps[:, 0:1]).then_inc(rooted, 1)
                if outT is not None:
                    for g in range(T // 4):
                        act.wait_ge(turned, g + 1)
                        nc.scalar.copy(outT[:, 4 * P * g:4 * P * (g + 1)],
                                       tp[:, g % 4, :, :]).then_inc(copied, 1)

            if outT is not None:
                @block.tensor
                def _(pe):
                    pe.wait_ge(normed, 1)
                    for g in range(T // 4):
                        if g >= 4:
                            pe.wait_ge(copied, g - 3)
                        for j in range(4):
                            last = pe.transpose(tp[:, g % 4, j, :], out[:, 4 * g + j, :], ident[:, :])
                        last.then_inc(turned, 1)


def mamba(nc, X, XT, ident, W_in, conv_w, conv_b, W_x, W_dt, b_dt, A_log, D, W_out):
    DM, DI2 = W_in.shape
    DI, NS, R, TAPS = DI2 // 2, A_log.shape[1], W_dt.shape[0], conv_w.shape[2]
    C, L = DI // P, 1024
    NB, HALF = XT.shape[1] // L, L // 512
    with Room(nc, "mb") as room:
        win, wx, wdt, wout = (room.sb("win", [P, DI2]), room.sb("wx", [P, C, R + 2 * NS]),
                              room.sb("wdt", [R, DI]), room.sb("wout", [P, C, DM]))
        cw, cb, bdt = room.sb("cw", [P, C, TAPS]), room.sb("cb", [P, C]), room.sb("bdt", [P, C])
        Aneg, Dv = room.sb("Aneg", [P, C, NS]), room.sb("Dv", [P, C])
        Ddiag = room.sb("Ddiag", [P, C, P])
        sel = room.sb("sel", [3 * 2 * NS, 2 * NS * P], BF16)
        xe, conv, xc, sz = (room.sb("xe", [P, C, L + TAPS - 1]), room.sb("conv", [P, C, L]),
                            room.sb("xc", [P, C, L]), room.sb("sz", [P, C, L]))
        dR = room.sb("dR", [R, L])
        bc_rest, bc_mid, bc3 = (room.sb("bc_rest", [2 * NS, L]), room.sb("bc_mid", [2 * NS, L], BF16),
                                room.sb("bc3", [3 * 2 * NS, L], BF16))
        delta, u, soft = room.sb("delta", [P, C, L]), room.sb("u", [P, C, L]), room.sb("soft", [P, C, L])
        decay = room.sb("decay", [P, 2, C, L])
        drive = room.sb("drive", [P, 2, C, L])
        h, hc, Cb = room.sb("h", [P, 2, C, L]), room.sb("hc", [P, 2, C, L]), room.sb("Cb", [P, 2, L])
        credit = room.sb("credit", [P, 1])
        G = room.ps("G", [P, 8, 512])
        names = ("loaded", "consts", "dve_step", "xz", "xe_ok", "sz_ok", "conv_ok", "xc_ok", "dbl", "dR_ok", "bc_ok",
                 "dt_ok", "abs_ok", "exp_ok", "log_ok", "u_ok", "B_ready", "C_ready", "B_free", "Cb_ready", "decay_ok",
                 "drive_ok", "h_ok", "hc_ok", "y_add", "y_init", "gated", "proj", "added", "r_ok")
        s = {n: room.sem(n) for n in names}

        with nc.Block() as block:
            @block.sync
            def _(sp):
                for dst, src in ((win[:, :], W_in), (wx[:, :, :], W_x.rearrange("(c p) m -> p c m", p=P)),
                                 (wdt[:, :], W_dt), (wout[:, :, :], W_out.rearrange("(c p) m -> p c m", p=P)),
                                 (cw[:, :, :], conv_w.rearrange("(c p) o k -> p c (o k)", p=P)),
                                 (cb[:, :], conv_b.rearrange("(c p) -> p c", p=P)),
                                 (bdt[:, :], b_dt.rearrange("(c p) -> p c", p=P)),
                                 (Aneg[:, :, :], A_log.rearrange("(c p) n -> p c n", p=P)),
                                 (Dv[:, :], D.rearrange("(c p) -> p c", p=P))):
                    with nc.allow_non_contiguous_dma(reason="a few small vectors"):
                        sp.dma_start(dst, src).then_inc(s["loaded"], 16)
                sp.wait_ge(s["loaded"], 9 * 16)

            @block.gpsimd
            def _(pool):
                pool.memset(sel[:, :], 0.0).then_inc(s["consts"], 1)
                for k in range(3):
                    pool.wait_ge(s["consts"], k + 1)
                    v = sel[:, :].rearrange("k (j m) -> k j m", m=P)
                    pool.affine_select(out=v, in_=v, compare_op=ALU.not_equal, fill=1.0, base=-2 * NS * k,
                                       pattern=[[-1, 2 * NS], [0, P]], channel_multiplier=1).then_inc(s["consts"], 1)
                pool.wait_ge(s["consts"], 4)
                pool.memset(credit[:, :], 0.0).then_inc(s["y_add"], 1)
                with pool.Fori(0, NB) as b:
                    with pool.Fori(0, NS // 2) as j:
                        for q in range(2):
                            it = b * NS + j * 2 + q
                            pool.wait_ge(s["Cb_ready"], it + 1)
                            for c in range(C):
                                pool.wait_ge(s["h_ok"], it * C + (c + 1))
                                pool.wait_ge(s["y_add"], it)
                                pool.tensor_tensor(hc[:, q, c, :], h[:, q, c, :], Cb[:, q, :],
                                                   ALU.mult).then_inc(s["hc_ok"], 1)

            @block.scalar
            def _(act):
                act.wait_ge(s["loaded"], 9 * 16)
                nc.scalar.activation(Aneg[:, :, :], Aneg[:, :, :], ACT.Exp).then_inc(s["r_ok"], 1)
                with act.Fori(0, NB) as b:
                    for m in range(C):
                        act.wait_ge(s["xz"], b * 2 * C + (m + 1))
                        nc.scalar.copy(xe[:, m, TAPS - 1:], G[:, 2 * m:2 * m + 2, :]).then_inc(s["xe_ok"], 1)
                    for m in range(C):
                        act.wait_ge(s["xz"], b * 2 * C + (C + m + 1))
                        nc.scalar.activation(sz[:, m, :], G[:, 2 * C + 2 * m:2 * C + 2 * m + 2, :],
                                             ACT.Silu).then_inc(s["sz_ok"], 1)
                    for c in range(C):
                        act.wait_ge(s["conv_ok"], b * C + (c + 1))
                        nc.scalar.activation(xc[:, c, :], conv[:, c, :], ACT.Silu,
                                             bias=cb[:, c:c + 1]).then_inc(s["xc_ok"], 1)
                    act.wait_ge(s["dbl"], b + 1)
                    nc.scalar.copy(dR[:, :], G[0:R, 0:2, :]).then_inc(s["dR_ok"], 1)
                    for c in range(C):
                        act.wait_ge(s["dt_ok"], b * C + (c + 1))
                        nc.scalar.activation(soft[:, c, :], G[:, 4 + 2 * c:6 + 2 * c, :], ACT.Abs,
                                             bias=bdt[:, c:c + 1]).then_inc(s["abs_ok"], 1)
                    act.wait_ge(s["abs_ok"], b * C + C)
                    nc.scalar.activation(soft[:, :, :], soft[:, :, :], ACT.Exp, scale=-1.0).then_inc(s["exp_ok"], 1)
                    act.wait_ge(s["exp_ok"], b + 1)
                    nc.scalar.activation(soft[:, :, :], soft[:, :, :], ACT.Ln, bias=1.0).then_inc(s["log_ok"], 1)
                    act.wait_ge(s["u_ok"], b + 1)
                    with act.Fori(0, NS // 2) as j:
                        for q in range(2):
                            it = b * NS + j * 2 + q
                            n = j * 2 + q
                            act.wait_ge(s["C_ready"], it + 1)
                            act.wait_ge(s["y_add"], it)
                            nc.scalar.copy(Cb[:, q, :], G[:, 2:4, :]).then_inc(s["Cb_ready"], 1)
                            for c in range(C):
                                nc.scalar.activation(decay[:, q, c, :], delta[:, c, :], ACT.Exp,
                                                     scale=Aneg[:, c, ds(n, 1)]
                                                     ).then_inc(s["decay_ok"], 1)

            @block.vector
            def _(dve):
                step = Steps(dve, s["dve_step"])
                dve.wait_ge(s["r_ok"], 1)
                step(dve.tensor_scalar(Aneg[:, :, :], Aneg[:, :, :], -1.0, None, ALU.mult))
                for c in range(C):
                    step(dve.tensor_scalar(Ddiag[:, c, :], ident[:, :], Dv[:, c:c + 1], None, ALU.mult))
                    step(dve.memset(xe[:, c, 0:TAPS - 1], 0.0))
                base = step.n
                per_batch = C * (TAPS - 1) + 4 + C + 1
                with dve.Fori(0, NB) as b:
                    step = Steps(dve, s["dve_step"], b * per_batch + base)
                    for c in range(C):
                        dve.wait_ge(s["xe_ok"], b * C + (c + 1))
                        for k in range(TAPS):
                            if k == 0:
                                last = dve.tensor_scalar(conv[:, c, :], xe[:, c, 0:L], cw[:, c, 0:1], None, ALU.mult)
                            else:
                                last = dve.scalar_tensor_tensor(out=conv[:, c, :], in0=xe[:, c, k:k + L],
                                                                scalar=cw[:, c, k:k + 1], in1=conv[:, c, :],
                                                                op0=ALU.mult, op1=ALU.add)
                            if k < TAPS - 1:
                                step(last)
                        last.then_inc(s["conv_ok"], 1)
                    dve.wait_ge(s["dbl"], b + 1)
                    BCp = G[0:2 * NS, 2:4, :]
                    r2 = bc_rest[:, :].rearrange("p (k n) -> p k n", k=HALF)
                    hi2 = bc3[0:2 * NS, :].rearrange("p (k n) -> p k n", k=HALF)
                    step(dve.tensor_copy(bc3[0:2 * NS, :], BCp))
                    step(dve.tensor_tensor(r2, BCp, hi2, ALU.subtract))
                    step(dve.tensor_copy(bc_mid[:, :], bc_rest[:, :]))
                    step(dve.tensor_copy(bc3[2 * NS:4 * NS, :], bc_mid[:, :]))
                    dve.tensor_tensor(bc3[4 * NS:6 * NS, :], bc_rest[:, :], bc_mid[:, :],
                                      ALU.subtract).then_inc(s["bc_ok"], 1)
                    dve.wait_ge(s["bc_ok"], b + 1)
                    for c in range(C):
                        dve.wait_ge(s["abs_ok"], b * C + (c + 1))
                        d2 = delta[:, c, :].rearrange("p (k n) -> p k n", k=HALF)
                        step(dve.tensor_scalar(d2, G[:, 4 + 2 * c:6 + 2 * c, :], bdt[:, c:c + 1], 0.0,
                                               ALU.add, ALU.max))
                    dve.wait_ge(s["log_ok"], b + 1)
                    step(dve.tensor_tensor(delta[:, :, :], delta[:, :, :], soft[:, :, :], ALU.add))
                    dve.wait_ge(s["xc_ok"], (b + 1) * C)
                    dve.tensor_tensor(u[:, :, :], delta[:, :, :], xc[:, :, :], ALU.mult).then_inc(s["u_ok"], 1)
                    with dve.Fori(0, NS // 2) as j:
                        for q in range(2):
                            it = b * NS + j * 2 + q
                            dve.wait_ge(s["u_ok"], b + 1)
                            dve.wait_ge(s["B_ready"], it + 1)
                            dve.wait_ge(s["y_add"], it)
                            for c in range(C):
                                last = dve.tensor_tensor(drive[:, q, c, :].rearrange("p (k n) -> p k n", k=HALF),
                                                         u[:, c, :].rearrange("p (k n) -> p k n", k=HALF),
                                                         G[:, 0:2, :], ALU.mult)
                                last.then_inc(s["drive_ok"], 1)
                            for c in range(C):
                                dve.wait_ge(s["drive_ok"], it * C + (c + 1))
                                dve.wait_ge(s["decay_ok"], it * C + (c + 1))
                                dve.tensor_tensor_scan(h[:, q, c, :], decay[:, q, c, :], drive[:, q, c, :], 0.0,
                                                       ALU.mult, ALU.add).then_inc(s["h_ok"], 1)
                    dve.wait_ge(s["sz_ok"], (b + 1) * C)
                    dve.wait_ge(s["y_add"], (b + 1) * NS + 1)
                    for c in range(C):
                        last = dve.tensor_tensor(sz[:, c, :].rearrange("p (k n) -> p k n", k=HALF),
                                                 sz[:, c, :].rearrange("p (k n) -> p k n", k=HALF),
                                                 G[:, 4 + 2 * c:6 + 2 * c, :], ALU.mult)
                        last.then_inc(s["gated"], 1)
                    for g in range(2):
                        dve.wait_ge(s["proj"], b * 2 + (g + 1))
                        xs = X[:, ds(b * 8 + 4 * g, 4), :]
                        dve.tensor_tensor(xs, xs, G[:, g, :].rearrange("p (t d) -> p t d", d=DM),
                                          ALU.add).then_inc(s["added"], 1)
                dve.wait_ge(s["added"], 2 * NB)

            @block.tensor
            def _(pe):
                pe.wait_ge(s["consts"], 4)
                pe.wait_ge(s["loaded"], 9 * 16)
                pe.wait_ge(s["dve_step"], 1 + 2 * C)
                with pe.Fori(0, NB) as b:
                    pe.wait_ge(s["added"], b * 2)
                    for m in range(2 * C):
                        for k in range(HALF):
                            last = pe.matmul(G[:, 2 * m + k, :], win[:, m * P:(m + 1) * P],
                                             XT[:, ds(b * L + 512 * k, 512)], start=True, stop=True)
                        last.then_inc(s["xz"], 1)
                    pe.wait_ge(s["xc_ok"], (b + 1) * C)
                    for k in range(HALF):
                        for g, (lo, hi) in enumerate(((0, R), (R, R + 2 * NS))):
                            for c in range(C):
                                last = pe.matmul(G[0:hi - lo, 2 * g + k, :], wx[:, c, lo:hi],
                                                 xc[:, c, 512 * k:512 * (k + 1)], start=(c == 0), stop=(c == C - 1))
                    last.then_inc(s["dbl"], 1)
                    pe.wait_ge(s["dR_ok"], b + 1)
                    pe.wait_ge(s["sz_ok"], (b + 1) * C)
                    for c in range(C):
                        for k in range(HALF):
                            last = pe.matmul(G[:, 4 + 2 * c + k, :], wdt[:, c * P:(c + 1) * P],
                                             dR[:, 512 * k:512 * (k + 1)], start=True, stop=True)
                        last.then_inc(s["dt_ok"], 1)
                    pe.wait_ge(s["u_ok"], b + 1)
                    pe.wait_ge(s["bc_ok"], b + 1)
                    for c in range(C):
                        for k in range(HALF):
                            last = pe.matmul(G[:, 4 + 2 * c + k, :], Ddiag[:, c, :],
                                             xc[:, c, 512 * k:512 * (k + 1)], start=True, stop=False,
                                             skip_group_check=True)
                    def spread(n, it):
                        pe.wait_ge(s["drive_ok"], it * C)
                        for k in range(HALF):
                            last = pe.matmul(G[:, k, :], sel[:, ds(n * P, P)], bc3[:, 512 * k:512 * (k + 1)],
                                             start=True, stop=True)
                        last.then_inc(s["B_ready"], 1)
                        pe.wait_ge(s["Cb_ready"], it)
                        for k in range(HALF):
                            last = pe.matmul(G[:, 2 + k, :], sel[:, ds(n * P + NS * P, P)],
                                             bc3[:, 512 * k:512 * (k + 1)], start=True, stop=True)
                        last.then_inc(s["C_ready"], 1)

                    def sum_state(q, it):
                        for c in range(C):
                            pe.wait_ge(s["hc_ok"], it * C + (c + 1))
                            for k in range(HALF):
                                last = pe.matmul(G[:, 4 + 2 * c + k, :], ident[:, :],
                                                 hc[:, q, c, 512 * k:512 * (k + 1)], start=False, stop=False,
                                                 skip_group_check=True)
                        last.then_inc(s["y_add"], 1)

                    spread(0, b * NS)
                    with pe.Fori(0, NS // 2 - 1) as j:
                        for q in range(2):
                            spread(j * 2 + (q + 1), b * NS + j * 2 + (q + 1))
                            sum_state(q, b * NS + j * 2 + q)
                    spread(NS - 1, b * NS + (NS - 1))
                    sum_state(0, b * NS + (NS - 2))
                    sum_state(1, b * NS + (NS - 1))
                    for g in range(2):
                        for t in range(4):
                            for c in range(C):
                                if g == 0 and t == 0:
                                    pe.wait_ge(s["gated"], (b + 1) * C)
                                tok = (4 * g + t) * P
                                last = pe.matmul(G[:, g, t * DM:(t + 1) * DM], sz[:, c, tok:tok + P], wout[:, c, :],
                                                 start=(c == 0), stop=(c == C - 1))
                        last.then_inc(s["proj"], 1)


def route(nc, name, score, softmax_gates, slot, gate, tile_expert, lead_tiles, lead_expert, zero_dram):
    T, E = score.shape[1], score.shape[2]
    NT = tile_expert.shape[1] - lead_tiles
    with Room(nc, name) as room:
        sb, sem = room.sb, room.sem
        rev_i, rev = sb("rev_i", [P, E], I32), sb("rev", [P, E])
        k_i, k_f = sb("k_i", [P, T], I32), sb("k_f", [P, T])
        t_i, t_f = sb("t_i", [1, NT], I32), sb("t_f", [1, NT])
        before, ones = sb("before", [P, P]), sb("ones", [P, P])
        keep = sb("keep", [P, E, T])
        oh = [sb("oh1", [P, T, E]), sb("oh2", [P, T, E])]
        w, left = sb("w", [P, T, E]), sb("left", [P, T, E])
        m, mw, ex = sb("m", [P, 2, T]), sb("mw", [P, T]), sb("ex", [P, T])
        both = sb("both", [P, T, E])
        tot, incl, off, over = sb("tot", [P, E, T]), sb("incl", [P, E, T]), sb("off", [P, E, T]), sb("over", [P, E, T])
        n, end, base = sb("n", [P, E]), sb("end", [P, E]), sb("base", [P, E])
        pos, slot_f = sb("pos", [P, T, E]), sb("slot_f", [P, 2, T])
        te, te_s = sb("te", [1, NT, E]), sb("te_s", [1, NT])
        zero = sb("zero", [P, 1024])
        rank = room.ps("rank", [P, T, E], F32)
        total = room.ps("total", [P, T, E], F32)
        const, dve_step, top2, exped, counted, zeroed, cleared = (
            sem(s) for s in ("const", "dve_step", "top2", "exped", "counted", "zeroed", "cleared"))

        def over_e(v):
            return v.rearrange("p (t o) -> p t o", o=1).broadcast_to([P, T, E])

        def over_t(v):
            return v.rearrange("p (e o) -> p e o", o=1).broadcast_to([P, E, T])

        with nc.Block() as block:
            @block.gpsimd
            def _(pool):
                pool.memset(zero[:, :], 0.0).then_inc(zeroed, 1)
                pool.iota(rev_i[:, :], pattern=[[-1, E]], base=E, channel_multiplier=0).then_inc(const, 1)
                pool.iota(k_i[:, :], pattern=[[P, T]], base=0, channel_multiplier=0).then_inc(const, 1)
                pool.iota(t_i[:, :], pattern=[[1, NT]], base=0, channel_multiplier=0).then_inc(const, 1)
                pool.memset(ones[:, :], 1.0).then_inc(const, 1)
                pool.memset(keep[:, :, :], 1.0).then_inc(const, 1)
                pool.wait_ge(const, 5)
                pool.memset(keep[:, :, 0:1], 0.0).then_inc(const, 1)
                pool.affine_select(out=before[:, :], in_=ones[:, :], compare_op=ALU.is_gt, fill=0.0,
                                   base=0, pattern=[[1, P]], channel_multiplier=-1).then_inc(const, 1)
                if lead_tiles:
                    pool.memset(tile_expert[:, 0:lead_tiles], lead_expert).then_inc(const, 1)
                    pool.wait_ge(const, 8)
                pool.wait_ge(const, 7)

            @block.sync
            def _(sp):
                rows = zero_dram.shape[0]
                sp.wait_ge(zeroed, 1)
                step = P * 8
                for r in range(0, rows, step):
                    sp.dma_start(zero_dram[r:r + step, :].rearrange("(p a) d -> p (a d)", p=P),
                                 zero[:, :]).then_inc(cleared, 16)
                sp.wait_ge(cleared, 16 * (rows // step))

            @block.vector
            def _(dve):
                step = Steps(dve, dve_step)
                dve.wait_ge(const, 7)
                step(dve.tensor_copy(rev[:, :], rev_i[:, :]))
                step(dve.tensor_copy(k_f[:, :], k_i[:, :]))
                step(dve.tensor_copy(t_f[:, :], t_i[:, :]))
                rev_w = rev[:, :].rearrange("p (o e) -> p o e", o=1).broadcast_to([P, T, E])
                for k in range(2):
                    src = score if k == 0 else left
                    step(dve.tensor_reduce(m[:, k, :], src[:, :, :], AX, ALU.max))
                    step(dve.tensor_tensor(w[:, :, :], src[:, :, :], over_e(m[:, k, :]), ALU.is_equal))
                    step(dve.tensor_tensor(w[:, :, :], w[:, :, :], rev_w, ALU.mult))
                    step(dve.tensor_reduce(mw[:, :], w[:, :, :], AX, ALU.max))
                    step(dve.tensor_tensor(oh[k][:, :, :], w[:, :, :], over_e(mw[:, :]), ALU.is_equal))
                    if k == 0:
                        step(dve.scalar_tensor_tensor(out=left[:, :, :], in0=oh[0][:, :, :], scalar=-3.0e38,
                                                      in1=score[:, :, :], op0=ALU.mult, op1=ALU.add))
                if softmax_gates:
                    step(dve.tensor_tensor(gate[:, 0, :], m[:, 1, :], m[:, 0, :], ALU.subtract))
                dve.tensor_tensor(both[:, :, :], oh[0][:, :, :], oh[1][:, :, :], ALU.add).then_inc(top2, 1)
                if softmax_gates:
                    dve.wait_ge(exped, 1)
                    step(dve.tensor_scalar(ex[:, :], gate[:, 1, :], 1.0, None, ALU.add))
                    step(dve.reciprocal(gate[:, 0, :], ex[:, :]))
                    step(dve.tensor_tensor(gate[:, 1, :], gate[:, 1, :], gate[:, 0, :], ALU.mult))
                else:
                    step(dve.tensor_tensor(ex[:, :], m[:, 0, :], m[:, 1, :], ALU.add))
                    step(dve.reciprocal(ex[:, :], ex[:, :]))
                    for k in range(2):
                        step(dve.tensor_tensor(gate[:, k, :], m[:, k, :], ex[:, :], ALU.mult))
                dve.wait_ge(counted, 2)
                step(dve.tensor_copy(tot[:, :, :], total[:, :, :].rearrange("p t e -> p e t")))
                step(dve.tensor_tensor_scan(incl[:, :, :].rearrange("p e t -> p (e t)"),
                                            keep[:, :, :].rearrange("p e t -> p (e t)"),
                                            tot[:, :, :].rearrange("p e t -> p (e t)"), 0.0, ALU.mult, ALU.add))
                count = incl[:, :, T - 1:T].broadcast_to([P, E, T])
                kk = k_f[:, :].rearrange("p (o t) -> p o t", o=1).broadcast_to([P, E, T])
                step(dve.tensor_tensor(over[:, :, :], count, kk, ALU.is_gt))
                step(dve.tensor_reduce(n[:, :], over[:, :, :], AX, ALU.add))
                step(dve.tensor_tensor_scan(end[:, :], ones[:, 0:E], n[:, :], 0.0, ALU.mult, ALU.add))
                step(dve.tensor_tensor(base[:, :], end[:, :], n[:, :], ALU.subtract))
                step(dve.tensor_scalar(base[:, :], base[:, :], float(P), float(lead_tiles * P), ALU.mult, ALU.add))
                step(dve.tensor_tensor(off[:, :, :], incl[:, :, :], tot[:, :, :], ALU.subtract))
                step(dve.tensor_tensor(off[:, :, :], off[:, :, :], over_t(base[:, :]), ALU.add))
                step(dve.tensor_tensor(pos[:, :, :], rank[:, :, :], off[:, :, :].rearrange("p e t -> p t e"), ALU.add))
                for k in range(2):
                    step(dve.tensor_tensor(w[:, :, :], oh[k][:, :, :], pos[:, :, :], ALU.mult))
                    step(dve.tensor_reduce(slot_f[:, k, :], w[:, :, :], AX, ALU.add))
                step(dve.tensor_copy(slot[:, :, :], slot_f[:, :, :]))
                tt = t_f[:, :].rearrange("p (t o) -> p t o", o=1).broadcast_to([1, NT, E])
                ee = end[0:1, :].rearrange("p (o e) -> p o e", o=1).broadcast_to([1, NT, E])
                step(dve.tensor_tensor(te[:, :, :], tt, ee, ALU.is_ge))
                step(dve.tensor_reduce(te_s[:, :], te[:, :, :], AX, ALU.add))
                step(dve.tensor_scalar(tile_expert[:, lead_tiles:], te_s[:, :], float(E - 1), None, ALU.min))

            @block.scalar
            def _(act):
                if softmax_gates:
                    act.wait_ge(top2, 1)
                    nc.scalar.activation(gate[:, 1, :], gate[:, 0, :], ACT.Exp).then_inc(exped, 1)

            @block.tensor
            def _(pe):
                pe.wait_ge(top2, 1)
                pe.matmul(rank[:, :, :], before[:, :], both[:, :, :], start=True, stop=True).then_inc(counted, 1)
                pe.matmul(total[:, :, :], ones[:, :], both[:, :, :], start=True, stop=True).then_inc(counted, 1)


def dispatch(nc, name, rows, slot, dram, lead):
    T = rows.shape[1]
    with Room(nc, name) as room:
        sent, copied = room.sem("sent"), room.sem("copied")
        with nc.Block() as block:
            @block.gpsimd
            def _(pool):
                for t in range(T):
                    for k in range(2):
                        pool.indirect_dma_start(dram, bass.IndirectOffsetOnAxis(ap=slot[:, k, t:t + 1], axis=0),
                                                rows[:, t, :], None).then_inc(sent, 16)
                pool.wait_ge(sent, 16 * 2 * T)

            if lead:
                @block.sync
                def _(sp):
                    sp.dma_start(dram[0:T * P, :].rearrange("(t p) d -> p t d", p=P), rows[:, :, :]).then_inc(copied, 16)
                    sp.wait_ge(copied, 16)


def combine(nc, name, X, slot, gate, dram, lead):
    T, D = X.shape[1], X.shape[2]
    RING, GROUP = 4, 4
    with Room(nc, name) as room:
        got = room.sb("got", [P, RING, 2, D])
        head = room.sb("head", [P, 2, GROUP, D])
        arrived = [room.sem(f"arrived{r}") for r in range(RING)]
        first, second, head_in, head_done = (room.sem(s) for s in ("first", "second", "head_in", "head_done"))
        with nc.Block() as block:
            @block.gpsimd
            def _(pool):
                for t in range(T):
                    if t >= RING:
                        pool.wait_ge(second, t - RING + 1)
                    for k in range(2):
                        pool.indirect_dma_start(got[:, t % RING, k, :], None, dram,
                                                bass.IndirectOffsetOnAxis(ap=slot[:, k, t:t + 1], axis=0)
                                                ).then_inc(arrived[t % RING], 16)

            if lead:
                @block.sync
                def _(sp):
                    for g in range(T // GROUP):
                        if g >= 2:
                            sp.wait_ge(head_done, g - 1)
                        if g >= 1:
                            sp.wait_ge(head_in, 16 * g)
                        sp.dma_start(head[:, g % 2, :, :], dram[g * GROUP * P:(g + 1) * GROUP * P, :]
                                     .rearrange("(t p) d -> p t d", p=P)).then_inc(head_in, 16)

            @block.vector
            def _(dve):
                for t in range(T):
                    if lead and t % GROUP == 0:
                        g = t // GROUP
                        dve.wait_ge(head_in, 16 * (g + 1))
                        xs = X[:, t:t + GROUP, :]
                        dve.tensor_tensor(xs, xs, head[:, g % 2, :, :], ALU.add).then_inc(head_done, 1)
                        dve.wait_ge(head_done, g + 1)
                    dve.wait_ge(arrived[t % RING], 32 * (t // RING + 1))
                    for k, done in enumerate((first, second)):
                        dve.scalar_tensor_tensor(out=X[:, t, :], in0=got[:, t % RING, k, :],
                                                 scalar=gate[:, k, t:t + 1], in1=X[:, t, :],
                                                 op0=ALU.mult, op1=ALU.add).then_inc(done, 1)
                        dve.wait_ge(done, t + 1)


def router_scores(nc, name, HT, weight, score, bias):
    T, E = score.shape[1], score.shape[2]
    with Room(nc, name) as room:
        rw = room.sb("rw", [P, E])
        bb = room.sb("bb", [P, E])
        lg = room.ps("lg", [P, T, E])
        loaded, made, scaled, done = (room.sem(s) for s in ("loaded", "made", "scaled", "done"))
        with nc.Block() as block:
            @block.sync
            def _(sp):
                sp.dma_start(rw[:, :], weight).then_inc(loaded, 16)
                if bias is not None:
                    sp.dma_start(bb[:, :], bias.rearrange("(o e) -> o e", o=1).broadcast_to([P, E])).then_inc(loaded, 16)

            @block.tensor
            def _(pe):
                pe.wait_ge(loaded, 16 if bias is None else 32)
                for t in range(T):
                    last = pe.matmul(lg[:, t, :], HT[:, t * P:(t + 1) * P], rw[:, :], start=True, stop=True)
                last.then_inc(made, 1)

            @block.vector
            def _(dve):
                dve.wait_ge(made, 1)
                if bias is None:
                    dve.tensor_copy(score[:, :, :], lg[:, :, :]).then_inc(done, 1)
                else:
                    bw = bb[:, :].rearrange("p (o e) -> p o e", o=1).broadcast_to([P, T, E])
                    dve.wait_ge(loaded, 32)
                    dve.tensor_tensor(score[:, :, :], lg[:, :, :], bw, ALU.mult).then_inc(scaled, 1)

                    dve.wait_ge(scaled, 1)
                    dve.tensor_scalar(score[:, :, :], score[:, :, :], -1.0, 88.0, ALU.mult, ALU.min).then_inc(scaled, 1)
                    dve.wait_ge(done, 1)
                    dve.tensor_scalar(score[:, :, :], score[:, :, :], 1.0, None, ALU.add).then_inc(done, 1)
                    dve.wait_ge(done, 2)
                    dve.reciprocal(score[:, :, :], score[:, :, :]).then_inc(done, 1)

            if bias is not None:
                @block.scalar
                def _(act):
                    act.wait_ge(scaled, 2)
                    nc.scalar.activation(score[:, :, :], score[:, :, :], ACT.Exp).then_inc(done, 1)


def experts_ln(nc, Zs, Os, tile_expert, ident, eg, eb, W1, b1, W2, b2, Wo, bo):
    E, D, H = W1.shape
    NT, HC = tile_expert.shape[1], H // P
    CLIP2, CLIP = 20.0, 10000.0
    with Room(nc, "e0") as room:
        sb, sem = room.sb, room.sem
        w1, w2, wo = sb("w1", [P, E, H]), sb("w2", [P, E, H]), sb("wo", [P, E, HC * D])
        bias1, bias2, biaso = sb("bias1", [P, E, H]), sb("bias2", [P, E, H]), sb("biaso", [P, E, D])
        egT, ebT, ebW = sb("egT", [P, E]), sb("ebT", [P, E]), sb("ebW", [P, E, P])
        xs, xT = sb("xs", [P, 2, D]), sb("xT", [P, 2, P])
        t1, t2, sl = sb("t1", [P, 2, H]), sb("t2", [P, 2, H]), sb("sl", [P, 2, H])
        hid, hT = sb("hid", [P, 2, H]), sb("hT", [P, 2, HC * P])
        o = sb("o", [P, 2, D])
        warm = sb("warm", [P, 1])
        A, B, HP, XO = (room.ps(n, [P, 2, 512]) for n in ("A", "B", "HP", "XO"))
        names = ("loaded", "wide_ok", "bias_mm", "bias_ok", "scaled", "x_in0", "x_in1", "x_turned", "xT_ok", "A_ok", "B_ok",
                 "t2_ok", "clip_ok", "silu_ok", "t1_ok", "h_ok", "h_turned", "hT_ok", "O_ok", "o_add", "o_ok",
                 "stored0", "stored1", "warmed")
        s = {n: sem(n) for n in names}
        x_in = [s["x_in0"], s["x_in1"]]
        stored = [s["stored0"], s["stored1"]]
        with nc.Block() as block:
            @block.sync
            def _(sp):
                for dst, src in ((w1[:, :, :], W1.rearrange("e p h -> p e h")),
                                 (w2[:, :, :], W2.rearrange("e p h -> p e h")),
                                 (egT[:, :], eg.rearrange("e p -> p e")), (ebT[:, :], eb.rearrange("e p -> p e")),
                                 (biaso[:, :, :], bo.rearrange("(o e) d -> o e d", o=1).broadcast_to([P, E, D])),
                                 (bias1[:, :, :], b1.rearrange("(o e) d -> o e d", o=1).broadcast_to([P, E, H])),
                                 (bias2[:, :, :], b2.rearrange("(o e) d -> o e d", o=1).broadcast_to([P, E, H]))):
                    with nc.allow_non_contiguous_dma(reason="two small matrices are transposed"):
                        sp.dma_start(dst, src).then_inc(s["loaded"], 16)
                for e in range(E):
                    sp.dma_start(wo[:, e, :].rearrange("p (c d) -> p c d", c=HC),
                                 Wo[e].rearrange("(c p) d -> p c d", p=P)).then_inc(s["loaded"], 16)
                sp.wait_ge(s["loaded"], 16 * (7 + E))

            @block.tensor
            def _(pe):
                pe.wait_ge(s["loaded"], 16 * (7 + E))
                pe.wait_ge(s["wide_ok"], 1)
                for e in range(E):
                    if e >= 2:
                        pe.wait_ge(s["bias_ok"], 2 * (e - 1))
                    for ps, w in ((A, w1), (B, w2)):
                        pe.matmul(ps[:, e % 2, :], ebW[:, e, :], w[:, e, :], start=True,
                                  stop=True).then_inc(s["bias_mm"], 1)

            @block.vector
            def _(dve):
                dve.wait_ge(s["loaded"], 16 * (7 + E))
                dve.tensor_copy(ebW[:, :, :], ebT[:, :].rearrange("p (e o) -> p e o", o=1)
                                .broadcast_to([P, E, P])).then_inc(s["wide_ok"], 1)
                for e in range(E):
                    for k, (ps, b) in enumerate(((A, bias1), (B, bias2))):
                        dve.wait_ge(s["bias_mm"], 2 * e + k + 1)
                        dve.tensor_tensor(b[:, e, :], ps[:, e % 2, :], b[:, e, :], ALU.add).then_inc(s["bias_ok"], 1)
                    for w in (w1, w2):
                        dve.tensor_scalar(w[:, e, :], w[:, e, :], egT[:, e:e + 1], None,
                                          ALU.mult).then_inc(s["scaled"], 1)
                dve.wait_ge(s["scaled"], 2 * E)

        with nc.Block() as block:
            @block.sync
            def _(sp):
                with sp.Fori(0, NT // 2) as j:
                    for q in range(2):
                        T = j * 2 + q
                        sp.wait_ge(s["o_ok"], T + 1)
                        sp.dma_start(Os[ds(T * P, P), :], o[:, q, :]).then_inc(stored[q], 16)
                for q in range(2):
                    sp.wait_ge(stored[q], 16 * (NT // 2))

            @block.tensor
            def _(pe):
                def turn_x(T, q, j1, early=False):
                    pe.wait_ge(x_in[q], j1 * 16)
                    if not early:
                        pe.wait_ge(s["o_add"], T - 3)
                    pe.transpose(XO[:, q, 0:P], xs[:, q, :], ident[:, :]).then_inc(s["x_turned"], 1)

                def up(T, q, early):
                    e = pe.value_load(tile_expert[0:1, ds(T, 1)], min_val=0, max_val=E - 1)
                    pe.wait_ge(s["xT_ok"], T + 1)
                    if not early:
                        pe.wait_ge(s["t1_ok"], T - 1)
                    pe.matmul(B[:, q, 0:H], xT[:, q, :], w2[:, ds(e, 1), :], start=True, stop=True).then_inc(s["B_ok"], 1)
                    pe.matmul(A[:, q, 0:H], xT[:, q, :], w1[:, ds(e, 1), :], start=True, stop=True).then_inc(s["A_ok"], 1)

                def turn_h(T, q):
                    pe.wait_ge(s["h_ok"], T + 1)
                    for c in range(HC):
                        last = pe.transpose(HP[:, q, c * P:(c + 1) * P], hid[:, q, c * P:(c + 1) * P], ident[:, :])
                    last.then_inc(s["h_turned"], 1)

                def down(T, q):
                    e = pe.value_load(tile_expert[0:1, ds(T, 1)], min_val=0, max_val=E - 1)
                    pe.wait_ge(s["hT_ok"], T + 1)
                    for c in range(HC):
                        last = pe.matmul(XO[:, q, 256:256 + D], hT[:, q, c * P:(c + 1) * P],
                                         wo[:, ds(e, 1), c * D:(c + 1) * D], start=(c == 0), stop=(c == HC - 1))
                    last.then_inc(s["O_ok"], 1)

                turn_x(0, 0, 1, True)
                up(0, 0, True)
                turn_x(1, 1, 1, True)
                up(1, 1, True)
                turn_x(2, 0, 2, True)
                turn_h(0, 0)
                with pe.Fori(0, NT // 2 - 2) as j:
                    for q in range(2):
                        T = j * 2 + (q + 2)
                        up(T, q, False)
                        turn_x(T + 1, 1 - q, j + (2 + q))
                        down(T - 2, q)
                        turn_h(T - 1, 1 - q)
                for T in (NT - 2, NT - 1):
                    q = T % 2
                    up(T, q, False)
                    if T + 1 < NT:
                        turn_x(T + 1, 1 - q, NT // 2)
                    down(T - 2, q)
                    turn_h(T - 1, 1 - q)
                down(NT - 2, 0)
                turn_h(NT - 1, 1)
                down(NT - 1, 1)

            @block.scalar
            def _(act):
                def load(T, q):
                    act.dma_start(xs[:, q, :], Zs[ds(T * P, P), :]).then_inc(x_in[q], 16)

                def turn(T, q, more=True):
                    act.wait_ge(s["x_turned"], T + 1)
                    if more:
                        load(T + 2, q)
                    nc.scalar.activation(xT[:, q, :], XO[:, q, 0:P], ACT.Copy).then_inc(s["xT_ok"], 1)

                def silu(T, q):
                    act.wait_ge(s["clip_ok"], T + 1)
                    nc.scalar.activation(sl[:, q, :], t2[:, q, :], ACT.Silu).then_inc(s["silu_ok"], 1)

                load(0, 0)
                load(1, 1)
                act.wait_ge(x_in[0], 16)
                nc.scalar.activation(warm[:, :], ident[:, 0:1], ACT.Silu).then_inc(s["warmed"], 1)
                turn(0, 0)
                with act.Fori(0, NT // 2 - 2) as j:
                    for q in range(2):
                        turn(j * 2 + (q + 1), 1 - q)
                        silu(j * 2 + q, q)
                turn(NT - 3, 1)
                silu(NT - 4, 0)
                turn(NT - 2, 0, False)
                silu(NT - 3, 1)
                turn(NT - 1, 1, False)
                silu(NT - 2, 0)
                silu(NT - 1, 1)

            @block.gpsimd
            def _(pool):
                with pool.Fori(0, NT // 2) as j:
                    for q in range(2):
                        T = j * 2 + q
                        pool.wait_ge(s["silu_ok"], T + 1)
                        pool.wait_ge(s["t1_ok"], T + 1)
                        pool.tensor_tensor(hid[:, q, :], t1[:, q, :], sl[:, q, :], ALU.mult).then_inc(s["h_ok"], 1)

            @block.vector
            def _(dve):
                def act_in(T, q):
                    e = dve.value_load(tile_expert[0:1, ds(T, 1)], min_val=0, max_val=E - 1)
                    dve.wait_ge(s["B_ok"], T + 1)
                    dve.tensor_tensor(t2[:, q, :], B[:, q, 0:H], bias2[:, ds(e, 1), :], ALU.add).then_inc(s["t2_ok"], 1)
                    dve.wait_ge(s["t2_ok"], T + 1)
                    dve.tensor_scalar(t2[:, q, :], t2[:, q, :], CLIP2, -CLIP2, ALU.min, ALU.max).then_inc(s["clip_ok"], 1)
                    dve.wait_ge(s["A_ok"], T + 1)
                    dve.tensor_tensor(t1[:, q, :], A[:, q, 0:H], bias1[:, ds(e, 1), :], ALU.add).then_inc(s["t1_ok"], 1)

                def hidden(T, q):
                    dve.wait_ge(s["h_turned"], T + 1)
                    dve.tensor_scalar(hT[:, q, :], HP[:, q, 0:HC * P], CLIP, -CLIP, ALU.min, ALU.max
                                      ).then_inc(s["hT_ok"], 1)

                def out(T, q, j0):
                    e = dve.value_load(tile_expert[0:1, ds(T, 1)], min_val=0, max_val=E - 1)
                    dve.wait_ge(s["O_ok"], T + 1)
                    dve.wait_ge(stored[q], j0 * 16)
                    dve.tensor_tensor(o[:, q, :], XO[:, q, 256:256 + D], biaso[:, ds(e, 1), :], ALU.add
                                      ).then_inc(s["o_add"], 1)
                    dve.wait_ge(s["o_add"], T + 1)
                    dve.tensor_scalar(o[:, q, :], o[:, q, :], CLIP, -CLIP, ALU.min, ALU.max).then_inc(s["o_ok"], 1)

                act_in(0, 0)
                act_in(1, 1)
                hidden(0, 0)
                with dve.Fori(0, NT // 2 - 1) as j:
                    for q in range(2):
                        T = j * 2 + (q + 2)
                        act_in(T, q)
                        out(T - 2, q, j)
                        hidden(T - 1, 1 - q)
                out(NT - 2, 0, NT // 2 - 1)
                hidden(NT - 1, 1)
                out(NT - 1, 1, NT // 2 - 1)


def ffn0(nc, X, XN, XT, ident, ln_g, ln_b, router_w, eg, eb, W1, b1, W2, b2, Wo, bo):
    T, D, E = X.shape[1], X.shape[2], router_w.shape[1]
    NT = (2 * T * P + E * (P - 1)) // P
    NT += NT % 2
    rows = (NT + 7) // 8 * 8 * P
    Zs = nc.dram_tensor("ffn0_rows", (rows, D), F32, kind="Internal").ap()
    Os = nc.dram_tensor("ffn0_outs", (NT * P, D), F32, kind="Internal").ap()
    with Room(nc, "f0") as room:
        gb = room.sb("gb", [P, 2, D])
        loaded = room.sem("gb_in")
        slot, gate = room.sb("slot", [P, 2, T], U32), room.sb("gate", [P, 2, T])
        score = room.sb("score", [P, T, E])
        tile_expert = room.sb("tile_expert", [1, NT], I32)
        with nc.Block() as block:
            @block.sync
            def _(sp):
                for k, v in enumerate((ln_g, ln_b)):
                    sp.dma_start(gb[:, k, :], v.rearrange("(o d) -> o d", o=1).broadcast_to([P, D])).then_inc(loaded, 16)
                sp.wait_ge(loaded, 32)
        layernorm(nc, "ln1", X, XN, XT, ident, var_scale=1.0 + EPS, var_bias=EPS * EPS,
                  gb=(gb[:, 0, :], gb[:, 1, :]))
        router_scores(nc, "rs0", XT, router_w, score, None)
        with Room(nc, "z0") as inner:
            Z = inner.sb("Z", [P, T, D])
            layernorm(nc, "ln2", XN, Z, None, ident)
            route(nc, "rt0", score, True, slot, gate, tile_expert, 0, 0, Zs)
            dispatch(nc, "ds0", Z, slot, Zs, False)
        experts_ln(nc, Zs, Os, tile_expert, ident, eg, eb, W1, b1, W2, b2, Wo, bo)
        combine(nc, "cb0", X, slot, gate, Os, False)


def experts_swiglu(nc, Zs, Os, tile_expert, ident, shared, routed):
    E = routed[0].shape[0] + 1
    D, H = shared[0].shape
    NT = tile_expert.shape[1]
    cuts = [(lo, min(lo + P, H)) for lo in range(0, H, P)]
    HC = len(cuts)
    with Room(nc, "e1") as room:
        sb, sem = room.sb, room.sem
        wg, wu, wd = sb("wg", [P, E, H]), sb("wu", [P, E, H]), sb("wd", [P, E, HC * D])
        xs, xT = sb("xs", [P, 2, D]), sb("xT", [P, 2, P])
        sl, hid, hT = sb("sl", [P, 2, H]), sb("hid", [P, 2, H]), sb("hT", [P, 2, HC * P])
        o = sb("o", [P, 2, D])
        warm = sb("warm", [P, 1])
        A, B, HP, XO = (room.ps(n, [P, 2, 512]) for n in ("A", "B", "HP", "XO"))
        names = ("loaded", "x_in0", "x_in1", "x_turned", "xT_ok", "A_ok", "B_ok", "silu_ok", "h_ok", "h_turned",
                 "hT_ok", "O_ok", "o_ok", "stored0", "stored1", "warmed")
        s = {n: sem(n) for n in names}
        x_in, stored = [s["x_in0"], s["x_in1"]], [s["stored0"], s["stored1"]]
        with nc.Block() as block:
            @block.sync
            def _(sp):
                n = 0
                for dst, sh, ro in ((wg, shared[0], routed[0]), (wu, shared[1], routed[1])):
                    sp.dma_start(dst[:, E - 1, :], sh).then_inc(s["loaded"], 16)
                    sp.dma_start(dst[:, 0:E - 1, :], ro.rearrange("e p h -> p e h")).then_inc(s["loaded"], 16)
                    n += 2
                for c, (lo, hi) in enumerate(cuts):
                    sp.dma_start(wd[0:hi - lo, E - 1, c * D:(c + 1) * D], shared[2][lo:hi, :]).then_inc(s["loaded"], 16)
                    sp.dma_start(wd[0:hi - lo, 0:E - 1, c * D:(c + 1) * D],
                                 routed[2][:, lo:hi, :].rearrange("e p d -> p e d")).then_inc(s["loaded"], 16)
                    n += 2
                sp.wait_ge(s["loaded"], 16 * n)
                with sp.Fori(0, NT // 2) as j:
                    for q in range(2):
                        T = j * 2 + q
                        sp.wait_ge(s["o_ok"], T + 1)
                        sp.dma_start(Os[ds(T * P, P), :], o[:, q, :]).then_inc(stored[q], 16)
                for q in range(2):
                    sp.wait_ge(stored[q], 16 * (NT // 2))

            @block.tensor
            def _(pe):
                pe.wait_ge(s["loaded"], 16 * (4 + 2 * HC))

                def turn_x(T, q, j1):
                    pe.wait_ge(x_in[q], j1 * 16)
                    pe.transpose(XO[:, q, 0:P], xs[:, q, :], ident[:, :]).then_inc(s["x_turned"], 1)

                def up(T, q, early):
                    e = pe.value_load(tile_expert[0:1, ds(T, 1)], min_val=0, max_val=E - 1)
                    pe.wait_ge(s["xT_ok"], T + 1)
                    if not early:
                        pe.wait_ge(s["h_ok"], T - 1)
                    pe.matmul(A[:, q, 0:H], xT[:, q, :], wg[:, ds(e, 1), :], start=True, stop=True).then_inc(s["A_ok"], 1)
                    pe.matmul(B[:, q, 0:H], xT[:, q, :], wu[:, ds(e, 1), :], start=True, stop=True).then_inc(s["B_ok"], 1)

                def turn_h(T, q):
                    pe.wait_ge(s["h_ok"], T + 1)
                    for c, (lo, hi) in enumerate(cuts):
                        last = pe.transpose(HP[0:hi - lo, q, c * P:(c + 1) * P], hid[:, q, lo:hi], ident[:, :])
                    last.then_inc(s["h_turned"], 1)

                def down(T, q):
                    e = pe.value_load(tile_expert[0:1, ds(T, 1)], min_val=0, max_val=E - 1)
                    pe.wait_ge(s["hT_ok"], T + 1)
                    for c, (lo, hi) in enumerate(cuts):
                        last = pe.matmul(XO[:, q, 256:256 + D], hT[0:hi - lo, q, c * P:(c + 1) * P],
                                         wd[0:hi - lo, ds(e, 1), c * D:(c + 1) * D], start=(c == 0),
                                         stop=(c == HC - 1))
                    last.then_inc(s["O_ok"], 1)

                turn_x(0, 0, 1)
                up(0, 0, True)
                turn_x(1, 1, 1)
                up(1, 1, True)
                turn_x(2, 0, 2)
                turn_h(0, 0)
                with pe.Fori(0, NT // 2 - 2) as j:
                    for q in range(2):
                        T = j * 2 + (q + 2)
                        up(T, q, False)
                        pe.wait_ge(s["o_ok"], j * 2 + q)
                        turn_x(T + 1, 1 - q, j + (2 + q))
                        down(T - 2, q)
                        turn_h(T - 1, 1 - q)
                for T in (NT - 2, NT - 1):
                    q = T % 2
                    up(T, q, False)
                    if T + 1 < NT:
                        pe.wait_ge(s["o_ok"], T - 2)
                        turn_x(T + 1, 1 - q, NT // 2)
                    down(T - 2, q)
                    turn_h(T - 1, 1 - q)
                down(NT - 2, 0)
                turn_h(NT - 1, 1)
                down(NT - 1, 1)

            @block.scalar
            def _(act):
                def load(T, q):
                    act.dma_start(xs[:, q, :], Zs[ds(T * P, P), :]).then_inc(x_in[q], 16)

                def turn(T, q, more=True):
                    act.wait_ge(s["x_turned"], T + 1)
                    if more:
                        load(T + 2, q)
                    nc.scalar.activation(xT[:, q, :], XO[:, q, 0:P], ACT.Copy).then_inc(s["xT_ok"], 1)

                def silu(T, q):
                    act.wait_ge(s["A_ok"], T + 1)
                    nc.scalar.activation(sl[:, q, :], A[:, q, 0:H], ACT.Silu).then_inc(s["silu_ok"], 1)

                load(0, 0)
                load(1, 1)
                act.wait_ge(x_in[0], 16)
                nc.scalar.activation(warm[:, :], ident[:, 0:1], ACT.Silu).then_inc(s["warmed"], 1)
                turn(0, 0)
                with act.Fori(0, NT // 2 - 2) as j:
                    for q in range(2):
                        turn(j * 2 + (q + 1), 1 - q)
                        silu(j * 2 + q, q)
                turn(NT - 3, 1)
                silu(NT - 4, 0)
                turn(NT - 2, 0, False)
                silu(NT - 3, 1)
                turn(NT - 1, 1, False)
                silu(NT - 2, 0)
                silu(NT - 1, 1)

            @block.vector
            def _(dve):
                def gate_up(T, q):
                    dve.wait_ge(s["silu_ok"], T + 1)
                    dve.wait_ge(s["B_ok"], T + 1)
                    dve.tensor_tensor(hid[:, q, :], B[:, q, 0:H], sl[:, q, :], ALU.mult).then_inc(s["h_ok"], 1)

                def hidden(T, q):
                    dve.wait_ge(s["h_turned"], T + 1)
                    full = (H // P) * P
                    dve.tensor_copy(hT[:, q, 0:full], HP[:, q, 0:full])
                    last = H - full
                    dve.tensor_copy(hT[0:last, q, full:full + P], HP[0:last, q, full:full + P]).then_inc(s["hT_ok"], 1)

                def out(T, q, j0):
                    dve.wait_ge(s["O_ok"], T + 1)
                    dve.wait_ge(stored[q], j0 * 16)
                    dve.tensor_copy(o[:, q, :], XO[:, q, 256:256 + D]).then_inc(s["o_ok"], 1)

                gate_up(0, 0)
                gate_up(1, 1)
                hidden(0, 0)
                with dve.Fori(0, NT // 2 - 1) as j:
                    for q in range(2):
                        T = j * 2 + (q + 2)
                        gate_up(T, q)
                        out(T - 2, q, j)
                        hidden(T - 1, 1 - q)
                out(NT - 2, 0, NT // 2 - 1)
                hidden(NT - 1, 1)
                out(NT - 1, 1, NT // 2 - 1)


def ffn1(nc, X, XN, XT, ident, shared, routed, Wr, routing_bias):
    T, D, E = X.shape[1], X.shape[2], Wr.shape[1]
    NT = T + (2 * T * P + E * (P - 1)) // P
    NT += NT % 2
    rows = (NT + 7) // 8 * 8 * P
    Zs = nc.dram_tensor("ffn1_rows", (rows, D), F32, kind="Internal").ap()
    Os = nc.dram_tensor("ffn1_outs", (NT * P, D), F32, kind="Internal").ap()
    with Room(nc, "f1") as room:
        slot, gate = room.sb("slot", [P, 2, T], U32), room.sb("gate", [P, 2, T])
        score = room.sb("score", [P, T, E])
        tile_expert = room.sb("tile_expert", [1, NT], I32)
        layernorm(nc, "ln4", X, XN, XT, ident)
        router_scores(nc, "rs1", XT, Wr, score, routing_bias)
        route(nc, "rt1", score, False, slot, gate, tile_expert, T, E, Zs)
        dispatch(nc, "ds1", XN, slot, Zs, True)
        experts_swiglu(nc, Zs, Os, tile_expert, ident, shared, routed)
        combine(nc, "cb1", X, slot, gate, Os, True)


HEADS, HD, GROUP = 16, 8, 4
LEFT, RIGHT = 64, 8
BAND = LEFT + P + RIGHT
PITCH = BAND + P
ROW = GROUP * PITCH + 8
QPARTS, KPARTS = (0, 0, 1, 0, 1, 2), (0, 1, 0, 2, 1, 0)
STACK = HD * len(QPARTS)


def attention_inputs(nc, XT, ident, Wq, bq, Wk, bk, Wv, bv, dist_emb, V, ES, parts, skew, skew_bufs):
    NTOK = XT.shape[1]
    SC = 1.0 / float(HD) ** 0.5
    with Room(nc, "ai") as room:
        sb, sem = room.sb, room.sem
        wraw, wT = sb("wraw", [P, 3, P]), sb("wT", [P, 3, P])
        bias, E0, E72 = sb("bias", [P, 3]), sb("E0", [P, 1]), sb("E72", [P, 1])
        bvb = sb("bvb", [P, P])
        val, part = sb("val", [P, NTOK]), [sb(f"part{k}", [P, NTOK], BF16) for k in range(3)]
        et, de = sb("et", [HD, LEFT + RIGHT + 1]), sb("de", [HD, BAND])
        der, ep = sb("der", [HD, BAND]), sb("ep", [HD, 3, BAND], BF16)
        zero = sb("zero", [P, ROW])
        G = room.ps("G", [P, 8, 512])
        loaded, turned, wT_ok, step_s, bias_ok, proj, evac, hi_ok, parts_ok, sent, e_sent, vproj, v_ok, zs, zw = (
            sem(n) for n in ("loaded", "turned", "wT_ok", "dve_step", "bias_ok", "proj", "evac", "hi_ok", "parts_ok",
                             "sent", "e_sent", "vproj", "v_ok", "zs", "zw"))
        NCH = NTOK // 512
        biases = [bias[:, 0:1], E0[:, :], E72[:, :]]
        with nc.Block() as block:
            @block.sync
            def _(sp):
                with nc.allow_non_contiguous_dma(reason="small vectors and the embedding's transpose"):
                    for k, w in enumerate((Wq, Wk, Wv)):
                        sp.dma_start(wraw[:, k, :], w).then_inc(loaded, 16)
                    for k, v in enumerate((bq, bk)):
                        sp.dma_start(bias[:, k:k + 1], v.rearrange("(p o) -> p o", o=1)).then_inc(loaded, 16)
                    for dst, row in ((E0, 0), (E72, LEFT + RIGHT)):
                        for h in range(HEADS):
                            sp.dma_start(dst[HD * h:HD * (h + 1), :],
                                         dist_emb[row:row + 1, :].rearrange("o d -> d o")).then_inc(loaded, 16)
                    sp.dma_start(et[:, :], dist_emb.rearrange("p d -> d p")).then_inc(loaded, 16)
                    sp.dma_start(bvb[:, :], bv.rearrange("(o d) -> o d", o=1).broadcast_to([P, P])).then_inc(loaded, 16)
                sp.wait_ge(zs, 1)
                for k in range(skew_bufs):
                    sp.dma_start(skew[k * P * ROW:(k + 1) * P * ROW].rearrange("(p w) -> p w", p=P),
                                 zero[:, :]).then_inc(zw, 16)
                for a in range(3):
                    sp.wait_ge(parts_ok, a + 1)
                    for k in range(3):
                        sp.dma_start(parts[a][k, :, 0:NTOK], part[k][:, :]).then_inc(sent, 16)
                        sp.dma_start(parts[a][k, :, NTOK:], part[k][:, 0:1024]).then_inc(sent, 16)
                    sp.wait_ge(sent, 96 * (a + 1))
                sp.wait_ge(zw, 16 * skew_bufs)
                sp.wait_ge(e_sent, 16 * 6)

            @block.gpsimd
            def _(pool):
                pool.memset(zero[:, :], 0.0).then_inc(zs, 1)
                pool.wait_ge(bias_ok, 1)
                for i, p in enumerate(KPARTS):
                    pool.dma_start(ES[i * HD:(i + 1) * HD, :], ep[:, p, :]).then_inc(e_sent, 16)
                pool.wait_ge(e_sent, 96)

            @block.tensor
            def _(pe):
                pe.wait_ge(loaded, 16 * (3 + 2 + 2 * HEADS + 2))
                for k in range(3):
                    last = pe.transpose(G[:, 0, k * P:(k + 1) * P], wraw[:, k, :], ident[:, :])
                last.then_inc(turned, 1)
                pe.wait_ge(wT_ok, 1)
                for a, w in enumerate((0, 1, 1)):
                    if a:
                        pe.wait_ge(evac, a)
                    for c in range(NCH):
                        last = pe.matmul(G[:, c, :], wT[:, w, :], XT[:, 512 * c:512 * (c + 1)], start=True, stop=True)
                    last.then_inc(proj, 1)
                pe.wait_ge(evac, 3)
                for c in range(NCH):
                    for t in range(4):
                        last = pe.matmul(G[:, c, t * P:(t + 1) * P], XT[:, (4 * c + t) * P:(4 * c + t + 1) * P],
                                         wT[:, 2, :], start=True, stop=True)
                last.then_inc(vproj, 1)

            @block.scalar
            def _(act):
                act.wait_ge(bias_ok, 1)
                v2 = val[:, :].rearrange("p (c n) -> p c n", n=512)
                p2 = part[0][:, :].rearrange("p (c n) -> p c n", n=512)
                half = NCH // 2
                for a in range(3):
                    act.wait_ge(proj, a + 1)
                    if a:
                        act.wait_ge(parts_ok, a)
                    for c in (0, half):
                        last = nc.scalar.activation(v2[:, c:c + half, :], G[:, c:c + half, :], ACT.Identity,
                                                    bias=biases[a], scale=SC if a == 0 else 1.0)
                    last.then_inc(evac, 1)
                    act.wait_ge(evac, a + 1)
                    if a:
                        act.wait_ge(sent, 96 * a)
                    nc.scalar.activation(part[0][:, :], val[:, :], ACT.Copy).then_inc(hi_ok, 1)

            @block.vector
            def _(dve):
                step = Steps(dve, step_s)
                dve.wait_ge(loaded, 16 * (3 + 2 + 2 * HEADS + 2))
                dve.wait_ge(turned, 1)
                dve.tensor_copy(wT[:, :, :], G[:, 0, 0:3 * P].rearrange("p (k m) -> p k m", k=3)).then_inc(wT_ok, 1)
                step(dve.tensor_scalar(bias[:, 0:1], bias[:, 0:1], SC, None, ALU.mult))
                step(dve.tensor_tensor(E0[:, :], E0[:, :], bias[:, 1:2], ALU.add))
                step(dve.tensor_tensor(E72[:, :], E72[:, :], bias[:, 1:2], ALU.add))
                NP = LEFT + RIGHT + 1
                step(dve.tensor_scalar(de[:, 0:NP], et[:, :], et[:, 0:1], None, ALU.subtract))
                step(dve.tensor_copy(de[:, NP:], de[:, NP - 1:NP].broadcast_to([HD, BAND - NP])))
                step(dve.tensor_copy(ep[:, 0, :], de[:, :]))
                step(dve.tensor_tensor(der[:, :], de[:, :], ep[:, 0, :], ALU.subtract))
                step(dve.tensor_copy(ep[:, 1, :], der[:, :]))
                dve.tensor_tensor(ep[:, 2, :], der[:, :], ep[:, 1, :], ALU.subtract).then_inc(bias_ok, 1)
                for a in range(3):
                    dve.wait_ge(hi_ok, a + 1)
                    step(dve.tensor_tensor(val[:, :], val[:, :], part[0][:, :], ALU.subtract))
                    step(dve.tensor_copy(part[1][:, :], val[:, :]))
                    dve.tensor_tensor(part[2][:, :], val[:, :], part[1][:, :], ALU.subtract).then_inc(parts_ok, 1)
                dve.wait_ge(vproj, 1)
                bw = bvb[:, :].rearrange("p (o d) -> p o d", o=1).broadcast_to([P, 4, P])
                for c in range(NCH):
                    dve.tensor_tensor(V[:, 4 * c:4 * c + 4, :], G[:, c, :].rearrange("p (t d) -> p t d", t=4), bw,
                                      ALU.add).then_inc(v_ok, 1)


def attention(nc, ident, V, ES, parts, skew, O):
    LT = 8
    NL, NU = 2 * LT, 2 * LT * GROUP
    IN = 16 * 3 * len(QPARTS)
    PAIRS = V.shape[1] // LT * (HEADS // GROUP) // 2
    with Room(nc, "at") as room:
        sb, sem = room.sb, room.sem
        st = [[sb(f"stack{s}{a}", [STACK, GROUP, 1024], BF16) for a in range(3)] for s in range(2)]
        Vg = sb("Vg", [P, 2, LT, GROUP, 32])
        qe, band = sb("qe", [P, 2, GROUP, BAND]), sb("band", [P, 4, GROUP, BAND])
        nmax, prob = sb("nmax", [P, 4]), sb("prob", [P, 4, 1024])
        pT = sb("pT", [P, 8, LT, P])
        acc_sb, rden = sb("acc_sb", [P, 2, P]), sb("rden", [P, GROUP])
        S = room.ps("S", [P, 2, 1024])
        TP = room.ps("TP", [P, 2, 4, P])
        QE = room.ps("QE", [P, 512])
        AC = room.ps("AC", [P, 512])
        TURNED = 2 * BAND
        turned = sb("turned", [P, 2, GROUP, HD + 1])
        picks = ident[:, :].rearrange("p (h c) -> p h c", h=GROUP)[:, :, 0:HD + 1]
        names = ("v_const", "v_ok", "set0_in", "set1_in", "S_ok", "max_ok", "exp_ok", "ta_ok", "tb_ok", "ea_ok", "eb_ok",
                 "qe_mm", "qe_ok", "skew_out", "band_in0", "band_in1", "av_ok", "acc_ok", "at_ok", "tu_ok", "rd_ok", "out_ok")
        s = {n: sem(n) for n in names}
        set_in = [s["set0_in"], s["set1_in"]]
        band_in = [s["band_in0"], s["band_in1"]]

        with nc.Block() as block:
            @block.gpsimd
            def _(pool):
                def load(k, batch, group):
                    for a, order in enumerate((QPARTS, KPARTS, KPARTS)):
                        for i, which in enumerate(order):
                            src = parts[a][which, ds(group * (GROUP * HD), GROUP * HD), ds(batch * 1024, 1024)]
                            pool.dma_start(st[k][a][i * HD:(i + 1) * HD, :, :],
                                           src.rearrange("(h d) t -> d h t", d=HD)).then_inc(set_in[k], 16)

                pool.memset(Vg[:, :, :, :, :], 0.0).then_inc(s["v_const"], 1)
                pool.wait_ge(s["v_const"], 1)
                pool.memset(Vg[:, :, :, :, HD:HD + 1], 1.0).then_inc(s["v_const"], 1)
                pool.wait_ge(s["v_const"], 2)
                load(0, 0, 0)
                with pool.Fori(0, PAIRS) as j:
                    pool.wait_ge(s["av_ok"], j * NL)
                    for k in range(2):
                        b8 = j // 2 * LT
                        hg = (j % 2) * 2 + k
                        pool.tensor_copy(Vg[:, k, :, :, 0:HD],
                                         V[:, ds(b8, LT), ds(hg * GROUP * HD, GROUP * HD)]
                                         .rearrange("p t (h d) -> p t h d", d=HD)).then_inc(s["v_ok"], 1)
                    load(1, j // 2, (j % 2) * 2 + 1)
                    pool.wait_ge(s["S_ok"], j * NU + NU // 2 + 1)
                    load(0, (j + 1) // 2, ((j + 1) % 2) * 2)
                pool.wait_ge(set_in[0], IN * (PAIRS + 1))
                pool.wait_ge(set_in[1], IN * PAIRS)

            @block.sync
            def _(sp):
                def skew_tile(lam, base):
                    sp.wait_ge(s["qe_ok"], (base + lam + 1) * 2)
                    buf = skew[(lam % 4) * P * ROW:(lam % 4 + 1) * P * ROW]
                    rows = buf.rearrange("(p w) -> p w", p=P)[:, 0:GROUP * PITCH].rearrange("p (h w) -> p h w", h=GROUP)
                    sp.dma_start(rows[:, :, 0:BAND], qe[:, lam % 2, :, :]).then_inc(s["skew_out"], 16)
                    sp.wait_ge(s["skew_out"], (base + lam + 1) * 16)
                    skewed = buf[0:P * (ROW - 1)].rearrange("(p w) -> p w", p=P)[:, 0:GROUP * PITCH]
                    sp.dma_start(band[:, lam % 4, :, :], skewed.rearrange("p (h w) -> p h w", h=GROUP)[:, :, 0:BAND]
                                 ).then_inc(band_in[lam % 2], 16)

                skew_tile(0, 0)
                skew_tile(1, 0)
                with sp.Fori(0, PAIRS) as j:
                    for lam in range(2, NL + 2):
                        skew_tile(lam, j * NL)
                for q in range(2):
                    sp.wait_ge(band_in[q], (PAIRS * NL // 2 + 1) * 16)

            @block.tensor
            def _(pe):
                def q_dot_e(lam, half):
                    k, L = (lam // LT) % 2, lam % LT
                    for h in range(2):
                        last = pe.matmul(QE[:, h * BAND:(h + 1) * BAND], st[k][0][:, 2 * half + h, L * P:(L + 1) * P],
                                         ES[:, :], start=True, stop=True)
                    last.then_inc(s["qe_mm"], 1)

                def scores(m, half_l):
                    lam, h = m // GROUP, m % GROUP
                    k, L = (lam // LT) % 2, lam % LT
                    q = st[k][0][:, h, L * P:(L + 1) * P]
                    if h == 0:
                        pe.wait_ge(band_in[lam % 2], half_l * 16 + (lam // 2 + 1) * 16)
                    cut = min(L * P + P + RIGHT, 1024)
                    lo = L * P - LEFT
                    for bank in (0, 512):
                        first = True
                        for a, (x, y) in ((1, (0, cut)), (2, (cut, 1024))):
                            x, y = max(x, bank), min(y, bank + 512)
                            if x < y:
                                last = pe.matmul(S[:, m % 2, x:y], q, st[k][a][:, h, x:y], start=first, stop=False,
                                                 skip_group_check=True)
                                first = False
                        x, y = max(lo, bank), min(lo + BAND, bank + 512)
                        if x < y:
                            last = pe.matmul(S[:, m % 2, x:y], ident[:, :], band[:, lam % 4, h, x - lo:y - lo],
                                             start=False, stop=False, skip_group_check=True)
                    last.then_inc(s["S_ok"], 1)

                def turn(m, base_u):
                    for half, (ok, out) in enumerate((("ea_ok", "ta_ok"), ("eb_ok", "tb_ok"))):
                        pe.wait_ge(s[ok], base_u + m)
                        for r in range(4):
                            c = (4 * half + r) * P
                            last = pe.transpose(TP[:, half, r, :], prob[:, m % 4, c:c + P], ident[:, :])
                        last.then_inc(s[out], 1)

                def weigh(lam, j, part):
                    if part == 0:
                        if lam % LT == 0:
                            pe.wait_ge(s["v_ok"], j * 2 + (lam // LT + 1))
                        pe.wait_ge(s["ea_ok"], j * NU + (lam + 1) * GROUP)
                        pe.wait_ge(s["eb_ok"], j * NU + (lam + 1) * GROUP)
                        if lam:
                            pe.wait_ge(s["acc_ok"], j * NL + lam)
                    for r in range(3 * part, min(3 * part + 3, LT)):
                        for h in range(GROUP):
                            last = pe.matmul(AC[32 * h:32 * (h + 1), 0:P], Vg[:, lam // LT, r, h, :],
                                             pT[:, (lam * GROUP + h) % 8, r, :], start=(r == 0), stop=(r == LT - 1),
                                             skip_group_check=True)
                    if part == 2:
                        last.then_inc(s["av_ok"], 1)

                def turn_out(lam, j):
                    pe.wait_ge(s["acc_ok"], j * NL + (lam + 1))
                    pe.matmul(QE[:, TURNED:TURNED + GROUP * (HD + 1)], acc_sb[:, lam % 2, :], picks, start=True,
                              stop=True, skip_group_check=True).then_inc(s["at_ok"], 1)

                pe.wait_ge(set_in[0], IN)
                for lam in range(2):
                    for half in range(2):
                        if lam + half:
                            pe.wait_ge(s["qe_ok"], lam * 2 + half)
                        q_dot_e(lam, half)
                scores(0, 0)
                scores(1, 0)
                with pe.Fori(0, PAIRS) as j:
                    for m in range(NU):
                        lam, h = m // GROUP, m % GROUP
                        if h in (0, 2):
                            pe.wait_ge(s["qe_ok"], j * (2 * NL) + ((lam + 2) * 2 + h // 2))
                            if h == 0 and (lam == 0 or lam > 2):
                                pe.wait_ge(s["tu_ok"], j * NL + (max(lam - 2, 0) + 1))
                            if h == 2 and lam >= 2:
                                turn_out(lam - 2, j)
                            if lam + 2 == LT and h == 0:
                                pe.wait_ge(set_in[1], j * IN + IN)
                            if lam + 2 == NL and h == 0:
                                pe.wait_ge(set_in[0], j * IN + 2 * IN)
                            q_dot_e(lam + 2, h // 2)
                        pe.wait_ge(s["exp_ok"], j * NU + (m + 1))
                        scores(m + 2, j * (NL // 2))
                        turn(m, j * NU)
                        if lam >= 1 and h:
                            weigh(lam - 1, j, h - 1)
                    for part in range(3):
                        weigh(NL - 1, j, part)
                    pe.wait_ge(s["qe_ok"], j * (2 * NL) + (NL + 2) * 2)
                    turn_out(NL - 2, j)
                    pe.wait_ge(s["tu_ok"], j * NL + NL)
                    turn_out(NL - 1, j)

            @block.scalar
            def _(act):
                def qe_copy(lam, half, base, wait):
                    act.wait_ge(s["qe_mm"], base * 2 + (lam * 2 + half + 1))
                    if wait:
                        act.wait_ge(s["skew_out"], (base + lam - 1) * 16)
                    nc.scalar.activation(qe[:, lam % 2, 2 * half:2 * half + 2, :],
                                         QE[:, 0:2 * BAND].rearrange("p (h u) -> p h u", h=2),
                                         ACT.Copy).then_inc(s["qe_ok"], 1)

                def copy_turned(m, base_u):
                    act.wait_ge(s["ta_ok"], base_u + (m + 1))
                    nc.scalar.activation(pT[:, m % 8, 0:4, :], TP[:, 0, :, :], ACT.Copy).then_inc(s["ea_ok"], 1)

                def copy_acc(lam, j):
                    act.wait_ge(s["av_ok"], j * NL + (lam + 1))
                    nc.scalar.activation(acc_sb[:, lam % 2, :], AC[:, 0:P], ACT.Copy).then_inc(s["acc_ok"], 1)

                def copy_output(lam, j):
                    act.wait_ge(s["at_ok"], j * NL + (lam + 1))
                    act.wait_ge(s["out_ok"], j * NL + (lam + 1))
                    nc.scalar.activation(turned[:, lam % 2, :, :], QE[:, TURNED:TURNED + GROUP * (HD + 1)]
                                         .rearrange("p (h c) -> p h c", h=GROUP), ACT.Copy).then_inc(s["tu_ok"], 1)

                for lam in range(2):
                    for half in range(2):
                        qe_copy(lam, half, 0, False)
                with act.Fori(0, PAIRS) as j:
                    for m in range(NU):
                        lam, h = m // GROUP, m % GROUP
                        act.wait_ge(s["max_ok"], j * NU + (m + 1))
                        nc.scalar.activation(prob[:, m % 4, :], S[:, m % 2, :], ACT.Exp,
                                             bias=nmax[:, m % 4:m % 4 + 1]).then_inc(s["exp_ok"], 1)
                        if m:
                            copy_turned(m - 1, j * NU)
                        if h in (1, 3):
                            qe_copy(lam + 2, h // 2, j * NL, True)
                        if lam >= 2 and h == 3:
                            copy_output(lam - 2, j)
                        if lam >= 2 and h == 0:
                            copy_acc(lam - 2, j)
                    copy_turned(NU - 1, j * NU)
                    copy_acc(NL - 2, j)
                    copy_output(NL - 2, j)
                    copy_acc(NL - 1, j)
                    copy_output(NL - 1, j)

            @block.vector
            def _(dve):
                def copy_turned(m, base_u):
                    dve.wait_ge(s["tb_ok"], base_u + (m + 1))
                    dve.tensor_copy(pT[:, m % 8, 4:8, :], TP[:, 1, :, :]).then_inc(s["eb_ok"], 1)

                def out(lam, j):
                    k, L = lam // LT, lam % LT
                    dve.wait_ge(s["tu_ok"], j * NL + (lam + 2))
                    v = turned[:, lam % 2, :, :]
                    dve.wait_ge(s["out_ok"], j * NL + (lam + 1))
                    dve.reciprocal(rden[:, :], v[:, :, HD]).then_inc(s["rd_ok"], 1)
                    dve.wait_ge(s["rd_ok"], j * NL + (lam + 1))
                    dst = O[:, ds(j // 2 * LT + L, 1), ds(((j % 2) * 2 + k) * GROUP * HD, GROUP * HD)]
                    dve.tensor_tensor(dst.rearrange("p o (h d) -> p (o h) d", d=HD), v[:, :, 0:HD],
                                      rden[:, :].rearrange("p (h o) -> p h o", o=1).broadcast_to([P, GROUP, HD]),
                                      ALU.mult).then_inc(s["out_ok"], 1)

                def negated_max(m, base_u):
                    dve.wait_ge(s["S_ok"], base_u + (m + 1))
                    dve.tensor_reduce(nmax[:, m % 4:m % 4 + 1], S[:, m % 2, :], AX, ALU.max,
                                      negate=True).then_inc(s["max_ok"], 1)

                dve.memset(rden[:, :], 0.0).then_inc(s["out_ok"], 1)
                dve.memset(turned[:, :, :, :], 0.0).then_inc(s["tu_ok"], 1)
                negated_max(0, 0)
                with dve.Fori(0, PAIRS) as j:
                    for m in range(NU):
                        lam, h = m // GROUP, m % GROUP
                        negated_max(m + 1, j * NU)
                        if m:
                            copy_turned(m - 1, j * NU)
                        if lam >= 3 and h == 0:
                            out(lam - 3, j)
                    copy_turned(NU - 1, j * NU)
                    out(NL - 3, j)
                    out(NL - 2, j)
                    out(NL - 1, j)


def attention_output(nc, X, O, OT, ident, Wo, bo):
    T = X.shape[1]
    with Room(nc, "ao") as room:
        wraw, wT, bob = room.sb("wraw", [P, P]), room.sb("wT", [P, P]), room.sb("bob", [P, P])
        G = room.ps("G", [P, 8, 4, P])
        loaded, w_turned, w_ok, turned, copied, made, added, biased = (
            room.sem(n) for n in ("loaded", "w_turned", "w_ok", "turned", "copied", "made", "added", "biased"))
        NG = T // 4
        with nc.Block() as block:
            @block.sync
            def _(sp):
                sp.dma_start(wraw[:, :], Wo).then_inc(loaded, 16)
                sp.dma_start(bob[:, :], bo.rearrange("(o d) -> o d", o=1).broadcast_to([P, P])).then_inc(loaded, 16)

            @block.tensor
            def _(pe):
                pe.wait_ge(loaded, 32)
                pe.transpose(G[:, 0, 0, :], wraw[:, :], ident[:, :]).then_inc(w_turned, 1)
                pe.wait_ge(w_ok, 1)
                for g in range(NG):
                    if g >= 4:
                        pe.wait_ge(copied, g - 3)
                    for t in range(4):
                        last = pe.transpose(G[:, g % 4, t, :], O[:, 4 * g + t, :], ident[:, :])
                    last.then_inc(turned, 1)
                for g in range(NG):
                    pe.wait_ge(copied, g + 1)
                    if g >= 4:
                        pe.wait_ge(added, g - 3)
                    for t in range(4):
                        tok = (4 * g + t) * P
                        last = pe.matmul(G[:, 4 + g % 4, t, :], OT[:, tok:tok + P], wT[:, :], start=True, stop=True)
                    last.then_inc(made, 1)

            @block.scalar
            def _(act):
                for g in range(NG):
                    act.wait_ge(turned, g + 1)
                    nc.scalar.activation(OT[:, 512 * g:512 * (g + 1)], G[:, g % 4, :, :], ACT.Copy).then_inc(copied, 1)

            @block.vector
            def _(dve):
                dve.wait_ge(w_turned, 1)
                dve.tensor_copy(wT[:, :], G[:, 0, 0, :]).then_inc(w_ok, 1)
                dve.wait_ge(loaded, 32)
                bw = bob[:, :].rearrange("p (o d) -> p o d", o=1).broadcast_to([P, T, P])
                dve.tensor_tensor(X[:, :, :], X[:, :, :], bw, ALU.add).then_inc(biased, 1)
                dve.wait_ge(biased, 1)
                for g in range(NG):
                    dve.wait_ge(made, g + 1)
                    xs = X[:, 4 * g:4 * g + 4, :]
                    dve.tensor_tensor(xs, xs, G[:, 4 + g % 4, :, :], ALU.add).then_inc(added, 1)


def attn1(nc, X, XN, XT, ident, Wq, bq, Wk, bk, Wv, bv, Wo, bo, dist_emb):
    T = X.shape[1]
    parts = [nc.dram_tensor(f"parts_{n}", (3, P, T * P + 1024), BF16, kind="Internal").ap()
             for n in ("q", "k_left", "k_right")]
    skew = nc.dram_tensor("skew", (4 * P * ROW,), F32, kind="Internal").ap()
    layernorm(nc, "ln3", X, XN, XT, ident)
    with Room(nc, "a1") as room:
        V, ES = room.sb("V", [P, T, P]), room.sb("ES", [STACK, BAND], BF16)
        attention_inputs(nc, XT, ident, Wq, bq, Wk, bk, Wv, bv, dist_emb, V, ES, parts, skew, 4)
        attention(nc, ident, V, ES, parts, skew, XN)
    attention_output(nc, X, XN, XT, ident, Wo, bo)


def two_layers(nc, x, mamba_w, ffn0_w, attn_w, ffn1_w, out):
    tokens, D = x.shape[0] * x.shape[1], x.shape[2]
    with Room(nc, "all") as room:
        X, XN = room.sb("X", [P, tokens // P, D]), room.sb("XN", [P, tokens // P, D])
        XT = room.sb("XT", [P, tokens])
        ident = room.sb("ident", [P, P])
        load_constants(nc, x, X, ident)
        layernorm(nc, "ln0", X, XN, XT, ident)
        mamba(nc, X, XT, ident, *mamba_w)
        ffn0(nc, X, XN, XT, ident, *ffn0_w)
        attn1(nc, X, XN, XT, ident, *attn_w)
        shared_and_routed, Wr, routing_bias = ffn1_w[0:6], ffn1_w[6], ffn1_w[7]
        ffn1(nc, X, XN, XT, ident, shared_and_routed[0:3], shared_and_routed[3:6], Wr, routing_bias)
        stored = room.sem("stored")
        with nc.Block() as block:
            @block.sync
            def _(sp):
                sp.dma_start(out.rearrange("b (t p) d -> p (b t) d", p=P), X[:, :, :]).then_inc(stored, 16)
                sp.wait_ge(stored, 16)


_PARTS = [
    ["L0_attn_x"],
    ["L0_attn_" + n for n in ("W_in", "conv_w", "conv_b", "W_x", "W_dt", "b_dt", "A_log", "D", "W_out")],
    ["L0_ffn_" + n for n in ("ln_g", "ln_b", "router_w", "eg", "eb", "W1", "b1", "W2", "b2", "Wo", "bo")],
    ["L1_attn_" + n for n in ("Wq", "bq", "Wk", "bk", "Wv", "bv", "Wo", "bo", "dist_emb")],
    ["L1_ffn_" + n for n in ("shared_gate", "shared_up", "shared_down", "routed_gate", "routed_up", "routed_down", "Wr",
                             "routing_bias")],
]


def kernel(**inputs):
    import numpy as _np
    import concourse.bacc as _bacc
    from concourse import mybir as _mybir
    from concourse.bass_utils import run_bass_kernel_spmd as _run

    nc = _bacc.Bacc("TRN2", target_bir_lowering=False, num_devices=1)
    arrays, args = {}, []
    for part in _PARTS:
        args.append([])
        for name in part:
            a = _np.ascontiguousarray(inputs[name])
            arrays[f"in_{name}_dram"] = a
            args[-1].append(nc.dram_tensor(f"in_{name}_dram", a.shape, _mybir.dt.from_np(a.dtype),
                                           kind="ExternalInput").ap())
    out = nc.dram_tensor("out_0_dram", arrays["in_L0_attn_x_dram"].shape, _mybir.dt.float32,
                         kind="ExternalOutput").ap()
    two_layers(nc, args[0][0], *args[1:], out)
    r = _run(nc, [arrays], core_ids=[0])
    return r.results[0]["out_0_dram"]
```

```python
from contextlib import ExitStack

import concourse.bass as bass
from concourse import mybir

P = 128
F32 = mybir.dt.float32
BF16 = mybir.dt.bfloat16
U32 = mybir.dt.uint32
I32 = mybir.dt.int32
ALU = mybir.AluOpType
ACT = mybir.ActivationFunctionType
AX = mybir.AxisListType.X
ds = bass.ds
EPS = 1e-5


class Steps:

    def __init__(self, eng, sem, base=0):
        self.eng, self.sem, self.base, self.n = eng, sem, base, 0

    def __call__(self, ins):
        ins.then_inc(self.sem, 1)
        self.n += 1
        self.eng.wait_ge(self.sem, self.base + self.n)


class Room:

    def __init__(self, nc, prefix):
        self.nc, self.prefix, self.ctx, self.sems = nc, prefix, ExitStack(), []

    def sb(self, name, shape, dt=F32):
        return self.ctx.enter_context(self.nc.sbuf_tensor(f"{self.prefix}_{name}", shape, dt))

    def ps(self, name, shape, dt=F32):
        return self.ctx.enter_context(self.nc.psum_tensor(f"{self.prefix}_{name}", shape, dt))

    def sem(self, name):
        self.sems.append(self.nc.alloc_semaphore(name=f"{self.prefix}_{name}"))
        return self.sems[-1]

    def __enter__(self):
        return self

    def __exit__(self, *a):
        self.nc.clear_and_free_semaphores(self.sems)
        self.nc.all_engine_barrier()
        self.ctx.close()


def load_constants(nc, x, X, ident, zero=None):
    with Room(nc, "init") as room:
        loaded, built = room.sem("x_loaded"), room.sem("ident_built")
        with nc.Block() as block:
            @block.sync
            def _(sp):
                src = x.rearrange("b (t p) d -> p (b t) d", p=P)
                half = X.shape[1] // 2
                sp.dma_start(X[:, 0:half, :], src[:, 0:half, :]).then_inc(loaded, 16)
                sp.dma_start(X[:, half:, :], src[:, half:, :]).then_inc(loaded, 16)
                sp.wait_ge(loaded, 32)

            @block.gpsimd
            def _(pool):
                pool.memset(ident[:, :], 0.0).then_inc(built, 1)
                pool.wait_ge(built, 1)
                pool.affine_select(out=ident[:, :], in_=ident[:, :], compare_op=ALU.not_equal, fill=1.0,
                                   base=0, pattern=[[-1, P]], channel_multiplier=1).then_inc(built, 1)
                if zero is not None:
                    pool.memset(zero[:, :], 0.0).then_inc(built, 1)
                    pool.wait_ge(built, 3)
                pool.wait_ge(built, 2)


def layernorm(nc, name, src, out, outT, ident, var_scale=1.0, var_bias=EPS, gb=None, gb_in=None, loads=None,
              update=None, after=None, router=None):
    T, D = src.shape[1], src.shape[2]
    NC = 4
    CT = T // NC
    with Room(nc, name) as room:
        sq = room.sb("sq", [P, 2, CT, D])
        mean, var, rstd = room.sb("mean", [P, T]), room.sb("var", [P, T]), room.sb("rstd", [P, T])
        tp = room.ps("tp", [P, 4, 4, P])
        names = ("epsed", "summed", "averaged", "centred", "squared", "spread", "rooted", "inverted", "scaled",
                 "gained", "normed", "turned", "copied")
        s = {n: room.sem(n) for n in names}
        eps = room.sb("eps", [P, 1])

        def wide(m, c):
            return m[:, c * CT:(c + 1) * CT].rearrange("p (t o) -> p t o", o=1).broadcast_to([P, CT, D])

        def tiles(c):
            return slice(c * CT, (c + 1) * CT)

        with nc.Block() as block:
            if loads is not None:
                @block.sync
                def _(sp):
                    loads(sp)

            @block.vector
            def _(dve):
                def finish(c):
                    dve.wait_ge(s["rooted"], c + 1)
                    dve.reciprocal(rstd[:, tiles(c)], rstd[:, tiles(c)]).then_inc(s["inverted"], 1)
                    dve.wait_ge(s["inverted"], c + 1)
                    o = out[:, tiles(c), :]
                    last = dve.tensor_tensor(o, o, wide(rstd, c), ALU.mult)
                    if gb is not None:
                        gain, bias = (v[:, :].rearrange("p (o d) -> p o d", o=1).broadcast_to([P, CT, D]) for v in gb)
                        last.then_inc(s["scaled"], 1)
                        dve.wait_ge(*gb_in)
                        dve.wait_ge(s["scaled"], c + 1)
                        dve.tensor_tensor(o, o, gain, ALU.mult).then_inc(s["gained"], 1)
                        dve.wait_ge(s["gained"], c + 1)
                        last = dve.tensor_tensor(o, o, bias, ALU.add)
                    last.then_inc(s["normed"], 1)

                def variance(c):
                    dve.wait_ge(s["squared"], c + 1)
                    dve.tensor_reduce(var[:, tiles(c)], sq[:, c % 2, :, :], AX, ALU.add).then_inc(s["spread"], 1)

                dve.memset(eps[:, :], var_bias).then_inc(s["epsed"], 1)
                for c in range(NC):
                    if update is not None:
                        update.add(dve, range(c * CT, (c + 1) * CT))
                    dve.tensor_reduce(mean[:, tiles(c)], src[:, tiles(c), :], AX, ALU.add).then_inc(s["summed"], 1)
                    dve.wait_ge(s["summed"], c + 1)
                    dve.tensor_scalar(mean[:, tiles(c)], mean[:, tiles(c)], 1.0 / D, None,
                                      ALU.mult).then_inc(s["averaged"], 1)
                    if update is not None or after is not None:
                        dve.wait_ge(s["averaged"], c + 1)
                        dve.tensor_tensor(out[:, tiles(c), :], src[:, tiles(c), :], wide(mean, c),
                                          ALU.subtract).then_inc(s["centred"], 1)
                    if c >= 1:
                        variance(c - 1)
                    if c >= 2:
                        finish(c - 2)
                variance(NC - 1)
                finish(NC - 2)
                finish(NC - 1)
                dve.wait_ge(s["normed"], NC)
                if after is not None:
                    after.fold(dve)

            @block.gpsimd
            def _(pool):
                if update is not None:
                    update.gather(pool)
                    return
                if after is not None:
                    after.scatter(pool, s["normed"], CT)
                    return
                for c in range(NC):
                    pool.wait_ge(s["averaged"], c + 1)
                    pool.tensor_tensor(out[:, tiles(c), :], src[:, tiles(c), :], wide(mean, c),
                                       ALU.subtract).then_inc(s["centred"], 1)

            @block.scalar
            def _(act):
                def root(c):
                    act.wait_ge(s["spread"], c + 1)
                    if c == 0:
                        act.wait_ge(s["epsed"], 1)
                    nc.scalar.activation(rstd[:, tiles(c)], var[:, tiles(c)], ACT.Sqrt, scale=var_scale / D,
                                         bias=eps[:, 0:1]).then_inc(s["rooted"], 1)

                for c in range(NC):
                    act.wait_ge(s["centred"], c + 1)
                    nc.scalar.activation(sq[:, c % 2, :, :], out[:, tiles(c), :], ACT.Square).then_inc(s["squared"], 1)
                    if c >= 1:
                        root(c - 1)
                root(NC - 1)
                if outT is not None:
                    for g in range(T // 4):
                        act.wait_ge(s["turned"], g + 1)
                        nc.scalar.activation(outT[:, 4 * P * g:4 * P * (g + 1)], tp[:, g % 4, :, :],
                                             ACT.Copy).then_inc(s["copied"], 1)

            if after is not None:
                @block.tensor
                def _(pe):
                    after.spread_bias(pe)

            if outT is not None:
                @block.tensor
                def _(pe):
                    for g in range(T // 4):
                        if g % (CT // 4) == 0:
                            pe.wait_ge(s["normed"], g // (CT // 4) + 1)
                        if g >= 4:
                            pe.wait_ge(s["copied"], g - 3)
                        for j in range(4):
                            last = pe.transpose(tp[:, g % 4, j, :], out[:, 4 * g + j, :], ident[:, :])
                        last.then_inc(s["turned"], 1)
                        if router is not None and g:
                            pe.wait_ge(s["copied"], g)
                            router.multiply(pe, outT, range(4 * g - 4, 4 * g))
                    if router is not None:
                        pe.wait_ge(s["copied"], T // 4)
                        router.multiply(pe, outT, range(T - 4, T))


class MambaWeights:

    def __init__(self, room, W_in, conv_w, W_x, W_dt, A_log, W_out):
        (DM, DI2), (R, DI), self.loads = W_in.shape, W_dt.shape, 9
        C = DI // P
        self.win, self.wx = room.sb("win", [P, DI2]), room.sb("wx", [P, C, W_x.shape[1]])
        self.wdt, self.wout = room.sb("wdt", [R, DI]), room.sb("wout", [P, C, DM])
        self.cw, self.cb, self.bdt = room.sb("cw", [P, C, conv_w.shape[2]]), room.sb("cb", [P, C]), room.sb("bdt", [P, C])
        self.A, self.D = room.sb("A", [P, C, A_log.shape[1]]), room.sb("D", [P, C])
        self.loaded = room.sem("weights_in")

    def load(self, nc, queue, W_in, conv_w, conv_b, W_x, W_dt, b_dt, A_log, D, W_out):
        for dst, src in ((self.win[:, :], W_in), (self.wx[:, :, :], W_x.rearrange("(c p) m -> p c m", p=P)),
                         (self.wdt[:, :], W_dt), (self.wout[:, :, :], W_out.rearrange("(c p) m -> p c m", p=P)),
                         (self.cw[:, :, :], conv_w.rearrange("(c p) o k -> p c (o k)", p=P)),
                         (self.cb[:, :], conv_b.rearrange("(c p) -> p c", p=P)),
                         (self.bdt[:, :], b_dt.rearrange("(c p) -> p c", p=P)),
                         (self.A[:, :, :], A_log.rearrange("(c p) n -> p c n", p=P)),
                         (self.D[:, :], D.rearrange("(c p) -> p c", p=P))):
            with nc.allow_non_contiguous_dma(reason="a few small vectors"):
                queue.dma_start(dst, src).then_inc(self.loaded, 16)


def mamba(nc, X, XT, ident, weights):
    win, wx, wdt, wout, cw, cb, bdt = (weights.win, weights.wx, weights.wdt, weights.wout, weights.cw, weights.cb,
                                       weights.bdt)
    Aneg, Dv = weights.A, weights.D
    NS, R, TAPS, DM = Aneg.shape[2], wdt.shape[0], cw.shape[2], wout.shape[2]
    C, L = wdt.shape[1] // P, 1024
    NB, HALF = XT.shape[1] // L, L // 512
    with Room(nc, "mb") as room:
        Ddiag = room.sb("Ddiag", [P, C, P])
        sel = room.sb("sel", [3 * 2 * NS, 2 * NS * P], BF16)
        xe, conv, xc, sz = (room.sb("xe", [P, C, L + TAPS - 1]), room.sb("conv", [P, C, L]),
                            room.sb("xc", [P, C, L]), room.sb("sz", [P, 2, C, L]))
        dR = room.sb("dR", [R, L])
        bc_rest, bc_mid, bc3 = (room.sb("bc_rest", [R + 2 * NS, L]), room.sb("bc_mid", [R + 2 * NS, L], BF16),
                                room.sb("bc3", [3 * 2 * NS, L], BF16))
        delta, u = room.sb("delta", [P, C, L]), room.sb("u", [P, C, L])
        soft = conv
        decay = room.sb("decay", [P, 2, C, L])
        drive = room.sb("drive", [P, 2, C, L])
        h, hc, Cb = room.sb("h", [P, 2, C, L]), room.sb("hc", [P, 2, C, L]), room.sb("Cb", [P, 2, L])
        credit, warm = room.sb("credit", [P, 1]), room.sb("warm", [P, 1])
        G = room.ps("G", [P, 8, 512])
        names = ("consts", "dve_step", "xz", "xe_ok", "sz_ok", "conv_ok", "xc_ok", "dbl", "dR_ok", "bc_ok",
                 "dt_ok", "abs_ok", "exp_ok", "log_ok", "u_ok", "B_ready", "C_ready", "Cb_ready", "decay_ok",
                 "drive_ok", "h_ok", "hc_ok", "y_add", "gated", "proj", "added", "r_ok",
                 "warmed", "dt_used")
        s = {n: room.sem(n) for n in names}

        AHEAD = C + 1

        def dt_bank(c):
            return 2 if c == 0 else 6

        with nc.Block() as block:
            @block.gpsimd
            def _(pool):
                pool.memset(sel[:, :], 0.0).then_inc(s["consts"], 1)
                for k in range(3):
                    pool.wait_ge(s["consts"], k + 1)
                    v = sel[:, :].rearrange("k (j m) -> k j m", m=P)
                    pool.affine_select(out=v, in_=v, compare_op=ALU.not_equal, fill=1.0, base=-2 * NS * k,
                                       pattern=[[-1, 2 * NS], [0, P]], channel_multiplier=1).then_inc(s["consts"], 1)
                pool.wait_ge(s["consts"], 4)
                pool.memset(credit[:, :], 0.0).then_inc(s["y_add"], 2)
                pool.wait_ge(s["y_add"], 2)
                pool.memset(credit[:, :], 0.0).then_inc(s["hc_ok"], AHEAD)
                for b in range(NB):
                    with pool.Fori(0, NS // 2) as j:
                        for q in range(2):
                            it = b * NS + j * 2 + q
                            pool.wait_ge(s["Cb_ready"], it + 1)
                            for c in range(C):
                                pool.wait_ge(s["h_ok"], it * C + (c + 1))
                                pool.wait_ge(s["y_add"], it + 1)
                                pool.tensor_tensor(hc[:, q, c, :], h[:, q, c, :], Cb[:, q, :],
                                                   ALU.mult).then_inc(s["hc_ok"], 1)

            @block.scalar
            def _(act):
                act.wait_ge(weights.loaded, 16 * weights.loads)
                nc.scalar.activation(Aneg[:, :, :], Aneg[:, :, :], ACT.Exp).then_inc(s["r_ok"], 1)
                for b in range(NB):
                    for m in range(C):
                        act.wait_ge(s["xz"], b * 2 * C + (m + 1))
                        nc.scalar.copy(xe[:, m, TAPS - 1:], G[:, 2 * m:2 * m + 2, :]).then_inc(s["xe_ok"], 1)
                    for m in range(C):
                        act.wait_ge(s["xz"], b * 2 * C + (C + m + 1))
                        nc.scalar.activation(sz[:, b % 2, m, :], G[:, 2 * m:2 * m + 2, :], ACT.Silu).then_inc(s["sz_ok"], 1)
                    for c in range(C):
                        act.wait_ge(s["conv_ok"], b * C + (c + 1))
                        nc.scalar.activation(xc[:, c, :], conv[:, c, :], ACT.Silu,
                                             bias=cb[:, c:c + 1]).then_inc(s["xc_ok"], 1)
                    act.wait_ge(s["dbl"], b + 1)
                    nc.scalar.copy(dR[:, :], G[0:R, 0:2, :]).then_inc(s["dR_ok"], 1)
                    for c in range(C):
                        act.wait_ge(s["dt_ok"], b * C + (c + 1))
                        nc.scalar.activation(soft[:, c, :], G[:, dt_bank(c):dt_bank(c) + 2, :], ACT.Abs,
                                             bias=bdt[:, c:c + 1]).then_inc(s["abs_ok"], 1)
                    act.wait_ge(s["abs_ok"], b * C + C)
                    nc.scalar.activation(soft[:, :, :], soft[:, :, :], ACT.Exp, scale=-1.0).then_inc(s["exp_ok"], 1)
                    act.wait_ge(s["exp_ok"], b + 1)
                    nc.scalar.activation(soft[:, :, :], soft[:, :, :], ACT.Ln, bias=1.0).then_inc(s["log_ok"], 1)
                    nc.scalar.activation(warm[:, :], Dv[:, 0:1], ACT.Exp).then_inc(s["warmed"], 1)
                    with act.Fori(0, NS // 2) as j:
                        for q in range(2):
                            it = b * NS + j * 2 + q
                            n = j * 2 + q
                            act.wait_ge(s["u_ok"], b + 1)
                            act.wait_ge(s["C_ready"], it + 1)
                            act.wait_ge(s["hc_ok"], it * C + (AHEAD - C))
                            nc.scalar.copy(Cb[:, q, :], G[:, 2:4, :]).then_inc(s["Cb_ready"], 1)
                            for c in range(C):
                                nc.scalar.activation(decay[:, q, c, :], delta[:, c, :], ACT.Exp,
                                                     scale=Aneg[:, c, ds(n, 1)]
                                                     ).then_inc(s["decay_ok"], 1)

            @block.vector
            def _(dve):
                step = Steps(dve, s["dve_step"])
                dve.wait_ge(s["r_ok"], 1)
                step(dve.tensor_scalar(Aneg[:, :, :], Aneg[:, :, :], -1.0, None, ALU.mult))
                for c in range(C):
                    step(dve.tensor_scalar(Ddiag[:, c, :], ident[:, :], Dv[:, c:c + 1], None, ALU.mult))
                    step(dve.memset(xe[:, c, 0:TAPS - 1], 0.0))

                def convolve(b):
                    for c in range(C):
                        dve.wait_ge(s["xe_ok"], b * C + (c + 1))
                        for k in range(TAPS):
                            if k == 0:
                                last = dve.tensor_scalar(conv[:, c, :], xe[:, c, 0:L], cw[:, c, 0:1], None, ALU.mult)
                            else:
                                last = dve.scalar_tensor_tensor(out=conv[:, c, :], in0=xe[:, c, k:k + L],
                                                                scalar=cw[:, c, k:k + 1], in1=conv[:, c, :],
                                                                op0=ALU.mult, op1=ALU.add)
                            if k < TAPS - 1:
                                step(last)
                        last.then_inc(s["conv_ok"], 1)

                def gate_y(b):
                    dve.wait_ge(s["sz_ok"], (b + 1) * C)
                    dve.wait_ge(s["y_add"], (b + 1) * NS + 2)
                    for c in range(C):
                        z2 = sz[:, b % 2, c, :].rearrange("p (k n) -> p k n", k=HALF)
                        dve.tensor_tensor(z2, z2, G[:, 4 + 2 * c:6 + 2 * c, :], ALU.mult).then_inc(s["gated"], 1)

                def add_to_stream(b):
                    for g in range(2):
                        dve.wait_ge(s["proj"], b * 2 + (g + 1))
                        xs = X[:, b * 8 + 4 * g:b * 8 + 4 * g + 4, :]
                        dve.tensor_tensor(xs, xs, G[:, 4 + g, :].rearrange("p (t d) -> p t d", d=DM),
                                          ALU.add).then_inc(s["added"], 1)

                convolve(0)
                for b in range(NB):
                    dve.wait_ge(s["dbl"], b + 1)
                    lo3, hi3 = R, R + 2 * NS
                    BCp = G[lo3:hi3, 0:2, :]
                    rest, mid = bc_rest[lo3:hi3, :], bc_mid[lo3:hi3, :]
                    hi2 = bc3[lo3:hi3, :].rearrange("p (k n) -> p k n", k=HALF)
                    step(dve.tensor_copy(hi2, BCp))
                    step(dve.tensor_tensor(rest.rearrange("p (k n) -> p k n", k=HALF), BCp, hi2, ALU.subtract))
                    step(dve.tensor_copy(mid, rest))
                    step(dve.tensor_copy(bc3[0:2 * NS, :], mid))
                    dve.tensor_tensor(bc3[2 * NS:4 * NS, :], rest, mid, ALU.subtract).then_inc(s["bc_ok"], 1)
                    dve.wait_ge(s["bc_ok"], b + 1)
                    for c in range(C):
                        dve.wait_ge(s["abs_ok"], b * C + (c + 1))
                        d2 = delta[:, c, :].rearrange("p (k n) -> p k n", k=HALF)
                        dve.tensor_scalar(d2, G[:, dt_bank(c):dt_bank(c) + 2, :], bdt[:, c:c + 1], 0.0,
                                          ALU.add, ALU.max).then_inc(s["dt_used"], 1)
                    dve.wait_ge(s["dt_used"], (b + 1) * C)
                    if b:
                        add_to_stream(b - 1)
                    dve.wait_ge(s["log_ok"], b + 1)
                    step(dve.tensor_tensor(delta[:, :, :], delta[:, :, :], soft[:, :, :], ALU.add))
                    dve.wait_ge(s["xc_ok"], (b + 1) * C)
                    dve.tensor_tensor(u[:, :, :], delta[:, :, :], xc[:, :, :], ALU.mult).then_inc(s["u_ok"], 1)
                    with dve.Fori(0, NS // 2) as j:
                        for q in range(2):
                            it = b * NS + j * 2 + q
                            dve.wait_ge(s["u_ok"], b + 1)
                            dve.wait_ge(s["B_ready"], it + 1)
                            dve.wait_ge(s["hc_ok"], it * C + (AHEAD - C))
                            for c in range(C):
                                last = dve.tensor_tensor(drive[:, q, c, :].rearrange("p (k n) -> p k n", k=HALF),
                                                         u[:, c, :].rearrange("p (k n) -> p k n", k=HALF),
                                                         G[:, 0:2, :], ALU.mult)
                                last.then_inc(s["drive_ok"], 1)
                            for c in range(C):
                                dve.wait_ge(s["drive_ok"], it * C + (c + 1))
                                dve.wait_ge(s["decay_ok"], it * C + (c + 1))
                                dve.tensor_tensor_scan(h[:, q, c, :], decay[:, q, c, :], drive[:, q, c, :], 0.0,
                                                       ALU.mult, ALU.add).then_inc(s["h_ok"], 1)
                    if b + 1 < NB:
                        convolve(b + 1)
                    gate_y(b)
                    if b + 1 == NB:
                        add_to_stream(b)
                dve.wait_ge(s["added"], 2 * NB)

            @block.tensor
            def _(pe):
                pe.wait_ge(weights.loaded, 16 * weights.loads)
                pe.wait_ge(s["dve_step"], 1 + 2 * C)

                def project_in(b, part):
                    for m in range(C):
                        for k in range(HALF):
                            last = pe.matmul(G[:, 2 * m + k, :], win[:, (part * C + m) * P:(part * C + m + 1) * P],
                                             XT[:, b * L + 512 * k:b * L + 512 * (k + 1)], start=True, stop=True)
                        last.then_inc(s["xz"], 1)

                def project_z(b):
                    pe.wait_ge(s["xe_ok"], (b + 1) * C)
                    project_in(b, 1)

                def delta_b_c(b):
                    pe.wait_ge(s["sz_ok"], (b + 1) * C)
                    for c in range(C):
                        pe.wait_ge(s["xc_ok"], b * C + (c + 1))
                        for k in range(HALF):
                            last = pe.matmul(G[0:R + 2 * NS, k, :], wx[:, c, :], xc[:, c, 512 * k:512 * (k + 1)],
                                             start=(c == 0), stop=(c == C - 1))
                    last.then_inc(s["dbl"], 1)

                def delta(b):
                    pe.wait_ge(s["dR_ok"], b + 1)
                    for c in range(C):
                        for k in range(HALF):
                            last = pe.matmul(G[:, dt_bank(c) + k, :], wdt[:, c * P:(c + 1) * P],
                                             dR[:, 512 * k:512 * (k + 1)], start=True, stop=True)
                        last.then_inc(s["dt_ok"], 1)

                def start_y(b):
                    pe.wait_ge(s["abs_ok"], (b + 1) * C)
                    pe.wait_ge(s["dt_used"], (b + 1) * C)
                    if b:
                        pe.wait_ge(s["added"], b * 2)
                    for c in range(C):
                        for k in range(HALF):
                            pe.matmul(G[:, 4 + 2 * c + k, :], Ddiag[:, c, :], xc[:, c, 512 * k:512 * (k + 1)],
                                      start=True, stop=False, skip_group_check=True)

                def spread(n, it):
                    pe.wait_ge(s["drive_ok"], it * C)
                    for k in range(HALF):
                        last = pe.matmul(G[:, k, :], sel[:, ds(n * P, P)], bc3[:, 512 * k:512 * (k + 1)],
                                         start=True, stop=True)
                    last.then_inc(s["B_ready"], 1)
                    pe.wait_ge(s["Cb_ready"], it)
                    for k in range(HALF):
                        last = pe.matmul(G[:, 2 + k, :], sel[:, ds(n * P + NS * P, P)],
                                         bc3[:, 512 * k:512 * (k + 1)], start=True, stop=True)
                    last.then_inc(s["C_ready"], 1)

                def sum_chunk(q, c, it):
                    pe.wait_ge(s["hc_ok"], it * C + (c + 1 + AHEAD))
                    for k in range(HALF):
                        last = pe.matmul(G[:, 4 + 2 * c + k, :], ident[:, :], hc[:, q, c, 512 * k:512 * (k + 1)],
                                         start=False, stop=False, skip_group_check=True)
                    if c == C - 1:
                        last.then_inc(s["y_add"], 1)

                def project_out(b):
                    pe.wait_ge(s["gated"], (b + 1) * C)
                    for g in range(2):
                        for t in range(4):
                            for c in range(C):
                                tok = (4 * g + t) * P
                                last = pe.matmul(G[:, 4 + g, t * DM:(t + 1) * DM], sz[:, b % 2, c, tok:tok + P],
                                                 wout[:, c, :], start=(c == 0), stop=(c == C - 1))
                        last.then_inc(s["proj"], 1)

                project_in(0, 0)
                project_z(0)
                delta_b_c(0)
                for b in range(NB):
                    first = b * NS
                    if b:
                        pe.wait_ge(s["gated"], b * C)
                    delta(b)
                    pe.wait_ge(s["bc_ok"], b + 1)
                    if b == 0:
                        pe.wait_ge(s["consts"], 4)
                    pe.wait_ge(s["abs_ok"], b * C + 1)
                    pe.wait_ge(s["dt_used"], b * C + 1)
                    spread(0, first)
                    if b:
                        project_out(b - 1)
                    start_y(b)
                    spread(1, first + 1)
                    with pe.Fori(0, NS // 2 - 1) as j:
                        for q in range(2):
                            n = j * 2 + q
                            for c in range(C - 1):
                                sum_chunk(q, c, n + first)
                            spread(n + 2, n + (first + 2))
                            sum_chunk(q, C - 1, n + first)
                    for c in range(C):
                        sum_chunk(0, c, first + NS - 2)
                    if b + 1 < NB:
                        pe.wait_ge(s["drive_ok"], (b + 1) * NS * C)
                        pe.wait_ge(s["Cb_ready"], (b + 1) * NS)
                        project_in(b + 1, 0)
                    for c in range(C):
                        sum_chunk(1, c, first + NS - 1)
                    if b + 1 < NB:
                        project_z(b + 1)
                        delta_b_c(b + 1)
                project_out(NB - 1)


class RowBuffer:

    def __init__(self, nc, room, name, T, D, E, lead):
        self.lead, self.NT = lead, lead + (2 * T * P + E * (P - 1)) // P
        self.NT += self.NT % 2
        self.rows = (self.NT + 7) // 8 * 8 * P
        self.dram = nc.dram_tensor(f"{name}_rows", (self.rows, D), F32, kind="Internal").ap()
        self.cleared, self.fills = room.sem(f"{name}_cleared"), (self.rows - lead * P) // (8 * P)

    def clear(self, queue, zero):
        for k in range(self.fills):
            at = (self.lead + 8 * k) * P
            queue.dma_start(self.dram[at:at + 8 * P, :].rearrange("(p a) d -> p (a d)", p=P),
                            zero[:, :]).then_inc(self.cleared, 16)

    def wait(self, eng):
        eng.wait_ge(self.cleared, 16 * self.fills)


def route(nc, name, score, softmax_gates, slot, gate, tile_expert, lead_tiles, lead_expert):
    T, E = score.shape[1], score.shape[2]
    NT = tile_expert.shape[1] - lead_tiles
    with Room(nc, name) as room:
        sb, sem = room.sb, room.sem
        rev_i, rev = sb("rev_i", [P, E], I32), sb("rev", [P, E])
        k_i, k_f = sb("k_i", [P, T], I32), sb("k_f", [P, T])
        t_i, t_f = sb("t_i", [1, NT], I32), sb("t_f", [1, NT])
        before, ones = sb("before", [P, P]), sb("ones", [P, P])
        keep = sb("keep", [P, E, T])
        oh = [sb("oh1", [P, T, E]), sb("oh2", [P, T, E])]
        w, left = sb("w", [P, T, E]), sb("left", [P, T, E])
        m, mw, ex = sb("m", [P, 2, T]), sb("mw", [P, T]), sb("ex", [P, T])
        both = sb("both", [P, T, E])
        tot, incl, off, over = sb("tot", [P, E, T]), sb("incl", [P, E, T]), sb("off", [P, E, T]), sb("over", [P, E, T])
        n, end, base = sb("n", [P, E]), sb("end", [P, E]), sb("base", [P, E])
        pos, slot_f = sb("pos", [P, T, E]), sb("slot_f", [P, 2, T])
        te, te_s = sb("te", [1, NT, E]), sb("te_s", [1, NT])
        rank = room.ps("rank", [P, T, E], F32)
        total = room.ps("total", [P, T, E], F32)
        const, dve_step, top2, exped, counted = (sem(s) for s in ("const", "dve_step", "top2", "exped", "counted"))

        def over_e(v):
            return v.rearrange("p (t o) -> p t o", o=1).broadcast_to([P, T, E])

        def over_t(v):
            return v.rearrange("p (e o) -> p e o", o=1).broadcast_to([P, E, T])

        with nc.Block() as block:
            @block.gpsimd
            def _(pool):
                pool.iota(rev_i[:, :], pattern=[[-1, E]], base=E, channel_multiplier=0).then_inc(const, 1)
                pool.iota(k_i[:, :], pattern=[[P, T]], base=0, channel_multiplier=0).then_inc(const, 1)
                pool.iota(t_i[:, :], pattern=[[1, NT]], base=0, channel_multiplier=0).then_inc(const, 1)
                pool.memset(ones[:, :], 1.0).then_inc(const, 1)
                pool.memset(keep[:, :, :], 1.0).then_inc(const, 1)
                pool.wait_ge(const, 5)
                pool.memset(keep[:, :, 0:1], 0.0).then_inc(const, 1)
                pool.affine_select(out=before[:, :], in_=ones[:, :], compare_op=ALU.is_gt, fill=0.0,
                                   base=0, pattern=[[1, P]], channel_multiplier=-1).then_inc(const, 1)
                if lead_tiles:
                    pool.memset(tile_expert[:, 0:lead_tiles], lead_expert).then_inc(const, 1)
                    pool.wait_ge(const, 8)
                pool.wait_ge(const, 7)

            @block.vector
            def _(dve):
                step = Steps(dve, dve_step)
                dve.wait_ge(const, 7)
                step(dve.tensor_copy(rev[:, :], rev_i[:, :]))
                step(dve.tensor_copy(k_f[:, :], k_i[:, :]))
                step(dve.tensor_copy(t_f[:, :], t_i[:, :]))
                rev_w = rev[:, :].rearrange("p (o e) -> p o e", o=1).broadcast_to([P, T, E])
                for k in range(2):
                    src = score if k == 0 else left
                    step(dve.tensor_reduce(m[:, k, :], src[:, :, :], AX, ALU.max))
                    step(dve.tensor_tensor(w[:, :, :], src[:, :, :], over_e(m[:, k, :]), ALU.is_equal))
                    step(dve.tensor_tensor(w[:, :, :], w[:, :, :], rev_w, ALU.mult))
                    step(dve.tensor_reduce(mw[:, :], w[:, :, :], AX, ALU.max))
                    step(dve.tensor_tensor(oh[k][:, :, :], w[:, :, :], over_e(mw[:, :]), ALU.is_equal))
                    if k == 0:
                        step(dve.scalar_tensor_tensor(out=left[:, :, :], in0=oh[0][:, :, :], scalar=-3.0e38,
                                                      in1=score[:, :, :], op0=ALU.mult, op1=ALU.add))
                if softmax_gates:
                    step(dve.tensor_tensor(gate[:, 0, :], m[:, 1, :], m[:, 0, :], ALU.subtract))
                dve.tensor_tensor(both[:, :, :], oh[0][:, :, :], oh[1][:, :, :], ALU.add).then_inc(top2, 1)
                if softmax_gates:
                    dve.wait_ge(exped, 1)
                    step(dve.tensor_scalar(ex[:, :], gate[:, 1, :], 1.0, None, ALU.add))
                    step(dve.reciprocal(gate[:, 0, :], ex[:, :]))
                    step(dve.tensor_tensor(gate[:, 1, :], gate[:, 1, :], gate[:, 0, :], ALU.mult))
                else:
                    step(dve.tensor_tensor(ex[:, :], m[:, 0, :], m[:, 1, :], ALU.add))
                    step(dve.reciprocal(ex[:, :], ex[:, :]))
                    for k in range(2):
                        step(dve.tensor_tensor(gate[:, k, :], m[:, k, :], ex[:, :], ALU.mult))
                dve.wait_ge(counted, 2)
                step(dve.tensor_copy(tot[:, :, :], total[:, :, :].rearrange("p t e -> p e t")))
                step(dve.tensor_tensor_scan(incl[:, :, :].rearrange("p e t -> p (e t)"),
                                            keep[:, :, :].rearrange("p e t -> p (e t)"),
                                            tot[:, :, :].rearrange("p e t -> p (e t)"), 0.0, ALU.mult, ALU.add))
                count = incl[:, :, T - 1:T].broadcast_to([P, E, T])
                kk = k_f[:, :].rearrange("p (o t) -> p o t", o=1).broadcast_to([P, E, T])
                step(dve.tensor_tensor(over[:, :, :], count, kk, ALU.is_gt))
                step(dve.tensor_reduce(n[:, :], over[:, :, :], AX, ALU.add))
                step(dve.tensor_tensor_scan(end[:, :], ones[:, 0:E], n[:, :], 0.0, ALU.mult, ALU.add))
                step(dve.tensor_tensor(base[:, :], end[:, :], n[:, :], ALU.subtract))
                step(dve.tensor_scalar(base[:, :], base[:, :], float(P), float(lead_tiles * P), ALU.mult, ALU.add))
                step(dve.tensor_tensor(off[:, :, :], incl[:, :, :], tot[:, :, :], ALU.subtract))
                step(dve.tensor_tensor(off[:, :, :], off[:, :, :], over_t(base[:, :]), ALU.add))
                step(dve.tensor_tensor(pos[:, :, :], rank[:, :, :], off[:, :, :].rearrange("p e t -> p t e"), ALU.add))
                for k in range(2):
                    step(dve.tensor_tensor(w[:, :, :], oh[k][:, :, :], pos[:, :, :], ALU.mult))
                    step(dve.tensor_reduce(slot_f[:, k, :], w[:, :, :], AX, ALU.add))
                step(dve.tensor_copy(slot[:, :, :], slot_f[:, :, :]))
                tt = t_f[:, :].rearrange("p (t o) -> p t o", o=1).broadcast_to([1, NT, E])
                ee = end[0:1, :].rearrange("p (o e) -> p o e", o=1).broadcast_to([1, NT, E])
                step(dve.tensor_tensor(te[:, :, :], tt, ee, ALU.is_ge))
                step(dve.tensor_reduce(te_s[:, :], te[:, :, :], AX, ALU.add))
                step(dve.tensor_scalar(tile_expert[:, lead_tiles:], te_s[:, :], float(E - 1), None, ALU.min))

            @block.scalar
            def _(act):
                if softmax_gates:
                    act.wait_ge(top2, 1)
                    nc.scalar.activation(gate[:, 1, :], gate[:, 0, :], ACT.Exp).then_inc(exped, 1)

            @block.tensor
            def _(pe):
                pe.wait_ge(top2, 1)
                pe.matmul(rank[:, :, :], before[:, :], both[:, :, :], start=True, stop=True).then_inc(counted, 1)
                pe.matmul(total[:, :, :], ones[:, :], both[:, :, :], start=True, stop=True).then_inc(counted, 1)


class Combine:

    def __init__(self, room, X, slot, gate, dram, lead):
        self.X, self.slot, self.gate, self.dram, self.lead = X, slot, gate, dram, lead
        self.T, D = X.shape[1], X.shape[2]
        self.RING, self.GROUP = 8, 4
        self.got = room.sb("got", [P, self.RING, 2, D])
        self.head = room.sb("head", [P, 2, self.GROUP, D]) if lead else None
        self.arrived = [room.sem(f"arrived{r}") for r in range(self.RING)]
        self.first, self.second, self.head_in, self.head_done = (
            room.sem(s) for s in ("first", "second", "head_in", "head_done"))

    def gather(self, pool):
        for t in range(self.T):
            if t >= self.RING:
                pool.wait_ge(self.second, t - self.RING + 1)
            for k in range(2):
                pool.indirect_dma_start(self.got[:, t % self.RING, k, :], None, self.dram,
                                        bass.IndirectOffsetOnAxis(ap=self.slot[:, k, t:t + 1], axis=0)
                                        ).then_inc(self.arrived[t % self.RING], 16)

    def heads(self, queue):
        for g in range(self.T // self.GROUP):
            if g >= 2:
                queue.wait_ge(self.head_done, g - 1)
            if g >= 1:
                queue.wait_ge(self.head_in, 16 * g)
            queue.dma_start(self.head[:, g % 2, :, :], self.dram[g * self.GROUP * P:(g + 1) * self.GROUP * P, :]
                            .rearrange("(t p) d -> p t d", p=P)).then_inc(self.head_in, 16)

    def add(self, dve, tiles):
        X = self.X
        for t in tiles:
            if self.lead and t % self.GROUP == 0:
                g = t // self.GROUP
                dve.wait_ge(self.head_in, 16 * (g + 1))
                xs = X[:, t:t + self.GROUP, :]
                dve.tensor_tensor(xs, xs, self.head[:, g % 2, :, :], ALU.add).then_inc(self.head_done, 1)
                dve.wait_ge(self.head_done, g + 1)
            dve.wait_ge(self.arrived[t % self.RING], 32 * (t // self.RING + 1))
            for k, done in enumerate((self.first, self.second)):
                dve.scalar_tensor_tensor(out=X[:, t, :], in0=self.got[:, t % self.RING, k, :],
                                         scalar=self.gate[:, k, t:t + 1], in1=X[:, t, :],
                                         op0=ALU.mult, op1=ALU.add).then_inc(done, 1)
                dve.wait_ge(done, t + 1)


class Router:

    def __init__(self, room, weight, bias, score):
        self.weight, self.bias, self.score = weight, bias, score
        self.T, self.E = score.shape[1], score.shape[2]
        self.rw, self.bb = room.sb("rw", [P, self.E]), room.sb("bb", [P, self.E])
        self.lg = room.ps("lg", [P, self.T, self.E])
        self.loaded, self.made, self.scaled, self.done = (
            room.sem(s) for s in ("router_in", "made", "scaled", "done"))
        self.loads = 1 if bias is None else 2

    def load(self, queue):
        queue.dma_start(self.rw[:, :], self.weight).then_inc(self.loaded, 16)
        if self.bias is not None:
            queue.dma_start(self.bb[:, :], self.bias.rearrange("(o e) -> o e", o=1)
                            .broadcast_to([P, self.E])).then_inc(self.loaded, 16)

    def multiply(self, pe, HT, tiles):
        pe.wait_ge(self.loaded, 16 * self.loads)
        for t in tiles:
            last = pe.matmul(self.lg[:, t, :], HT[:, t * P:(t + 1) * P], self.rw[:, :], start=True, stop=True)
        last.then_inc(self.made, 1)

    def finish(self, nc):
        score, bias, lg, done, scaled = self.score, self.bias, self.lg, self.done, self.scaled
        with nc.Block() as block:
            @block.vector
            def _(dve):
                dve.wait_ge(self.made, self.T // 4)
                if bias is None:
                    dve.tensor_copy(score[:, :, :], lg[:, :, :]).then_inc(done, 1)
                else:
                    bw = self.bb[:, :].rearrange("p (o e) -> p o e", o=1).broadcast_to([P, self.T, self.E])
                    dve.wait_ge(self.loaded, 16 * self.loads)
                    dve.tensor_tensor(score[:, :, :], lg[:, :, :], bw, ALU.mult).then_inc(scaled, 1)

                    dve.wait_ge(scaled, 1)
                    dve.tensor_scalar(score[:, :, :], score[:, :, :], -1.0, 88.0, ALU.mult, ALU.min).then_inc(scaled, 1)
                    dve.wait_ge(done, 1)
                    dve.tensor_scalar(score[:, :, :], score[:, :, :], 1.0, None, ALU.add).then_inc(done, 1)
                    dve.wait_ge(done, 2)
                    dve.reciprocal(score[:, :, :], score[:, :, :]).then_inc(done, 1)

            if bias is not None:
                @block.scalar
                def _(act):
                    act.wait_ge(scaled, 2)
                    nc.scalar.activation(score[:, :, :], score[:, :, :], ACT.Exp).then_inc(done, 1)


class LnExperts:

    def __init__(self, room, shape):
        self.E, self.D, self.H = E, D, H = shape
        self.HC = H // P
        sb = room.sb
        self.w1, self.w2, self.wo = sb("w1", [P, E, H]), sb("w2", [P, E, H]), sb("wo", [P, E, self.HC * D])
        self.bias1, self.bias2, self.biaso = sb("bias1", [P, E, H]), sb("bias2", [P, E, H]), sb("biaso", [P, E, D])
        self.egT, self.ebT = sb("egT", [P, E]), sb("ebT", [P, E])
        self.loaded, self.loads = room.sem("weights_in"), 7 + E

    def load(self, nc, sp, eg, eb, W1, b1, W2, b2, Wo, bo):
        E, D, H = self.E, self.D, self.H
        for dst, src in ((self.w1[:, :, :], W1.rearrange("e p h -> p e h")),
                         (self.w2[:, :, :], W2.rearrange("e p h -> p e h")),
                         (self.egT[:, :], eg.rearrange("e p -> p e")), (self.ebT[:, :], eb.rearrange("e p -> p e")),
                         (self.biaso[:, :, :], bo.rearrange("(o e) d -> o e d", o=1).broadcast_to([P, E, D])),
                         (self.bias1[:, :, :], b1.rearrange("(o e) d -> o e d", o=1).broadcast_to([P, E, H])),
                         (self.bias2[:, :, :], b2.rearrange("(o e) d -> o e d", o=1).broadcast_to([P, E, H]))):
            with nc.allow_non_contiguous_dma(reason="two small matrices are transposed"):
                sp.dma_start(dst, src).then_inc(self.loaded, 16)
        for e in range(E):
            sp.dma_start(self.wo[:, e, :].rearrange("p (c d) -> p c d", c=self.HC),
                         Wo[e].rearrange("(c p) d -> p c d", p=P)).then_inc(self.loaded, 16)


class FoldAndDispatch:

    def __init__(self, room, experts, rows, slot, buffer):
        self.experts, self.rows, self.slot, self.buffer, self.dram = experts, rows, slot, buffer, buffer.dram
        self.ebW = room.sb("ebW", [P, experts.E, P])
        self.A, self.B = room.ps("A", [P, 2, 512]), room.ps("B", [P, 2, 512])
        self.sent, self.wide_ok, self.bias_mm, self.bias_ok, self.scaled = (
            room.sem(n) for n in ("sent", "wide_ok", "bias_mm", "bias_ok", "scaled"))

    def scatter(self, pool, normed, tiles):
        T = self.rows.shape[1]
        self.buffer.wait(pool)
        for t in range(T):
            if t % tiles == 0:
                pool.wait_ge(normed, t // tiles + 1)
            for k in range(2):
                pool.indirect_dma_start(self.dram, bass.IndirectOffsetOnAxis(ap=self.slot[:, k, t:t + 1], axis=0),
                                        self.rows[:, t, :], None).then_inc(self.sent, 16)
        pool.wait_ge(self.sent, 16 * 2 * T)

    def spread_bias(self, pe):
        experts = self.experts
        pe.wait_ge(experts.loaded, 16 * experts.loads)
        pe.wait_ge(self.wide_ok, 1)
        for e in range(experts.E):
            if e >= 2:
                pe.wait_ge(self.bias_ok, 2 * (e - 1))
            for ps, w in ((self.A, experts.w1), (self.B, experts.w2)):
                pe.matmul(ps[:, e % 2, :], self.ebW[:, e, :], w[:, e, :], start=True, stop=True).then_inc(self.bias_mm, 1)

    def fold(self, dve):
        experts, E = self.experts, self.experts.E
        dve.wait_ge(experts.loaded, 16 * experts.loads)
        dve.tensor_copy(self.ebW[:, :, :], experts.ebT[:, :].rearrange("p (e o) -> p e o", o=1)
                        .broadcast_to([P, E, P])).then_inc(self.wide_ok, 1)
        for e in range(E):
            for k, (ps, b) in enumerate(((self.A, experts.bias1), (self.B, experts.bias2))):
                dve.wait_ge(self.bias_mm, 2 * e + k + 1)
                dve.tensor_tensor(b[:, e, :], ps[:, e % 2, :], b[:, e, :], ALU.add).then_inc(self.bias_ok, 1)
            for w in (experts.w1, experts.w2):
                dve.tensor_scalar(w[:, e, :], w[:, e, :], experts.egT[:, e:e + 1], None,
                                  ALU.mult).then_inc(self.scaled, 1)
        dve.wait_ge(self.scaled, 2 * E)


def experts_ln(nc, Zs, Os, tile_expert, ident, experts):
    E, D, H, HC = experts.E, experts.D, experts.H, experts.HC
    w1, w2, wo = experts.w1, experts.w2, experts.wo
    bias1, bias2, biaso = experts.bias1, experts.bias2, experts.biaso
    NT = tile_expert.shape[1]
    CLIP2, CLIP = 20.0, 10000.0
    with Room(nc, "e0") as room:
        sb, sem = room.sb, room.sem
        xs, xT = sb("xs", [P, 2, D]), sb("xT", [P, 2, P])
        t1, t2, sl = sb("t1", [P, 2, H]), sb("t2", [P, 2, H]), sb("sl", [P, 2, H])
        hid, hT = sb("hid", [P, 2, H]), sb("hT", [P, 2, HC * P])
        o = sb("o", [P, 2, D])
        warm = sb("warm", [P, 1])
        A, B, HP, XO = (room.ps(n, [P, 2, 512]) for n in ("A", "B", "HP", "XO"))
        names = ("x_in0", "x_in1", "x_turned", "xT_ok", "A_ok", "B_ok",
                 "t2_ok", "clip_ok", "silu_ok", "t1_ok", "h_ok", "h_turned", "hT_ok", "O_ok", "o_add", "o_ok",
                 "stored0", "stored1")
        s = {n: sem(n) for n in names}
        x_in = [s["x_in0"], s["x_in1"]]
        stored = [s["stored0"], s["stored1"]]
        with nc.Block() as block:
            @block.sync
            def _(sp):
                with sp.Fori(0, NT // 2) as j:
                    for q in range(2):
                        T = j * 2 + q
                        sp.wait_ge(s["o_ok"], T + 1)
                        sp.dma_start(Os[ds(T * P, P), :], o[:, q, :]).then_inc(stored[q], 16)
                for q in range(2):
                    sp.wait_ge(stored[q], 16 * (NT // 2) + 1)

            @block.tensor
            def _(pe):
                def turn_x(T, q, j1, early=False):
                    pe.wait_ge(x_in[q], j1 * 16)
                    if not early:
                        pe.wait_ge(s["o_add"], T - 2)
                    pe.transpose(XO[:, q, 0:P], xs[:, q, :], ident[:, :]).then_inc(s["x_turned"], 1)

                def up(T, q, e, early, also=None):
                    pe.wait_ge(s["xT_ok"], T + 1)
                    if not early:
                        pe.wait_ge(s["t1_ok"], T - 1)
                    pe.matmul(B[:, q, 0:H], xT[:, q, :], w2[:, ds(e, 1), :], start=True, stop=True).then_inc(s["B_ok"], 1)
                    e_also = None if also is None else expert(also)
                    pe.matmul(A[:, q, 0:H], xT[:, q, :], w1[:, ds(e, 1), :], start=True, stop=True).then_inc(s["A_ok"], 1)
                    return e_also

                def turn_h(T, q):
                    pe.wait_ge(s["h_ok"], T + 1)
                    for c in range(HC):
                        last = pe.transpose(HP[:, q, c * P:(c + 1) * P], hid[:, q, c * P:(c + 1) * P], ident[:, :])
                    last.then_inc(s["h_turned"], 1)

                def down(T, q, e):
                    pe.wait_ge(s["hT_ok"], T + 1)
                    for c in range(HC):
                        last = pe.matmul(XO[:, q, 256:256 + D], hT[:, q, c * P:(c + 1) * P],
                                         wo[:, ds(e, 1), c * D:(c + 1) * D], start=(c == 0), stop=(c == HC - 1))
                    last.then_inc(s["O_ok"], 1)

                def expert(T):
                    return pe.value_load(tile_expert[0:1, ds(T, 1)], min_val=0, max_val=E - 1)

                turn_x(0, 0, 1, True)
                up(0, 0, expert(0), True)
                turn_x(1, 1, 1, True)
                up(1, 1, expert(1), True)
                turn_x(2, 0, 2, True)
                turn_h(0, 0)
                with pe.Fori(0, NT // 2 - 2) as j:
                    for q in range(2):
                        T = j * 2 + (q + 2)
                        e_out = up(T, q, expert(T), False, T - 2)
                        turn_x(T + 1, 1 - q, j + (2 + q))
                        down(T - 2, q, e_out)
                        turn_h(T - 1, 1 - q)
                for T in (NT - 2, NT - 1):
                    q = T % 2
                    up(T, q, expert(T), False)
                    if T + 1 < NT:
                        turn_x(T + 1, 1 - q, NT // 2)
                    down(T - 2, q, expert(T - 2))
                    turn_h(T - 1, 1 - q)
                down(NT - 2, 0, expert(NT - 2))
                turn_h(NT - 1, 1)
                down(NT - 1, 1, expert(NT - 1))

            @block.scalar
            def _(act):
                def load(T, q):
                    act.dma_start(xs[:, q, :], Zs[ds(T * P, P), :]).then_inc(x_in[q], 16)

                def turn(T, q, more=True):
                    act.wait_ge(s["x_turned"], T + 1)
                    if more:
                        load(T + 2, q)
                    nc.scalar.activation(xT[:, q, :], XO[:, q, 0:P], ACT.Copy).then_inc(s["xT_ok"], 1)

                def silu(T, q):
                    act.wait_ge(s["clip_ok"], T + 1)
                    nc.scalar.activation(sl[:, q, :], t2[:, q, :], ACT.Silu).then_inc(s["silu_ok"], 1)

                load(0, 0)
                load(1, 1)
                act.wait_ge(x_in[0], 16)
                nc.scalar.activation(warm[:, :], ident[:, 0:1], ACT.Silu).then_inc(s["o_add"], 1)
                turn(0, 0)
                with act.Fori(0, NT // 2 - 2) as j:
                    for q in range(2):
                        turn(j * 2 + (q + 1), 1 - q)
                        silu(j * 2 + q, q)
                turn(NT - 3, 1)
                silu(NT - 4, 0)
                turn(NT - 2, 0, False)
                silu(NT - 3, 1)
                turn(NT - 1, 1, False)
                silu(NT - 2, 0)
                silu(NT - 1, 1)

            @block.gpsimd
            def _(pool):
                with pool.Fori(0, NT // 2) as j:
                    for q in range(2):
                        T = j * 2 + q
                        pool.wait_ge(s["silu_ok"], T + 1)
                        pool.wait_ge(s["t1_ok"], T + 1)
                        pool.tensor_tensor(hid[:, q, :], t1[:, q, :], sl[:, q, :], ALU.mult).then_inc(s["h_ok"], 1)

            @block.vector
            def _(dve):
                def act_in(T, q):
                    e = dve.value_load(tile_expert[0:1, ds(T, 1)], min_val=0, max_val=E - 1)
                    dve.wait_ge(s["B_ok"], T + 1)
                    dve.tensor_tensor(t2[:, q, :], B[:, q, 0:H], bias2[:, ds(e, 1), :], ALU.add).then_inc(s["t2_ok"], 1)
                    dve.wait_ge(s["t2_ok"], T + 1)
                    dve.tensor_scalar(t2[:, q, :], t2[:, q, :], CLIP2, -CLIP2, ALU.min, ALU.max).then_inc(s["clip_ok"], 1)
                    dve.wait_ge(s["A_ok"], T + 1)
                    dve.tensor_tensor(t1[:, q, :], A[:, q, 0:H], bias1[:, ds(e, 1), :], ALU.add).then_inc(s["t1_ok"], 1)

                def hidden(T, q):
                    dve.wait_ge(s["h_turned"], T + 1)
                    dve.tensor_scalar(hT[:, q, :], HP[:, q, 0:HC * P], CLIP, -CLIP, ALU.min, ALU.max
                                      ).then_inc(s["hT_ok"], 1)

                def out(T, q, j0):
                    e = dve.value_load(tile_expert[0:1, ds(T, 1)], min_val=0, max_val=E - 1)
                    dve.wait_ge(s["O_ok"], T + 1)
                    dve.wait_ge(stored[q], j0 * 16 + 1)
                    dve.tensor_tensor(o[:, q, :], XO[:, q, 256:256 + D], biaso[:, ds(e, 1), :], ALU.add
                                      ).then_inc(s["o_add"], 1)
                    dve.wait_ge(s["o_add"], T + 2)
                    dve.tensor_scalar(o[:, q, :], o[:, q, :], CLIP, -CLIP, ALU.min, ALU.max).then_inc(s["o_ok"], 1)

                for q in range(2):
                    dve.memset(o[:, q, :], 0.0).then_inc(stored[q], 1)
                act_in(0, 0)
                act_in(1, 1)
                hidden(0, 0)
                with dve.Fori(0, NT // 2 - 1) as j:
                    for q in range(2):
                        T = j * 2 + (q + 2)
                        act_in(T, q)
                        out(T - 2, q, j)
                        hidden(T - 1, 1 - q)
                out(NT - 2, 0, NT // 2 - 1)
                hidden(NT - 1, 1)
                out(NT - 1, 1, NT // 2 - 1)


def ffn0(nc, outer, buffer, X, XN, XT, ident, ln_g, ln_b, router_w, eg, eb, W1, b1, W2, b2, Wo, bo):
    T, D, E = X.shape[1], X.shape[2], router_w.shape[1]
    NT = buffer.NT
    Os = nc.dram_tensor("ffn0_outs", (NT * P, D), F32, kind="Internal").ap()
    slot, gate = outer.sb("slot", [P, 2, T], U32), outer.sb("gate", [P, 2, T])
    with Room(nc, "f0") as room:
        gb = room.sb("gb", [P, 2, D])
        loaded = room.sem("gb_in")
        score = room.sb("score", [P, T, E])
        tile_expert = room.sb("tile_expert", [1, NT], I32)
        experts = LnExperts(room, W1.shape)
        with nc.Block() as block:
            @block.sync
            def _(sp):
                for k, v in enumerate((ln_g, ln_b)):
                    sp.dma_start(gb[:, k, :], v.rearrange("(o d) -> o d", o=1).broadcast_to([P, D])).then_inc(loaded, 16)

        def start_loads(queue):
            router.load(queue)
            experts.load(nc, queue, eg, eb, W1, b1, W2, b2, Wo, bo)

        with Room(nc, "rs0") as inner:
            router = Router(inner, router_w, None, score)
            layernorm(nc, "ln1", X, XN, XT, ident, var_scale=1.0 + EPS, var_bias=EPS * EPS,
                      gb=(gb[:, 0, :], gb[:, 1, :]), gb_in=(loaded, 32), loads=start_loads, router=router)
            router.finish(nc)
        route(nc, "rt0", score, True, slot, gate, tile_expert, 0, 0)
        Z = XT[:, :].rearrange("p (t d) -> p t d", d=D)
        with Room(nc, "fd") as inner:
            layernorm(nc, "ln2", XN, Z, None, ident, after=FoldAndDispatch(inner, experts, Z, slot, buffer))
        experts_ln(nc, buffer.dram, Os, tile_expert, ident, experts)
    return Combine(outer, X, slot, gate, Os, False)


class SwigluExperts:

    def __init__(self, room, D, H, routed):
        self.E, self.D, self.H = E, D, H = routed + 1, D, H
        self.cuts = [(lo, min(lo + P, H)) for lo in range(0, H, P)]
        HC = len(self.cuts)
        self.wg, self.wu, self.wd = room.sb("wg", [P, E, H]), room.sb("wu", [P, E, H]), room.sb("wd", [P, E, HC * D])
        self.loaded, self.loads = room.sem("weights_in"), 4 + 2 * HC

    def load(self, sp, shared, routed):
        E, D = self.E, self.D
        for dst, sh, ro in ((self.wg, shared[0], routed[0]), (self.wu, shared[1], routed[1])):
            sp.dma_start(dst[:, E - 1, :], sh).then_inc(self.loaded, 16)
            sp.dma_start(dst[:, 0:E - 1, :], ro.rearrange("e p h -> p e h")).then_inc(self.loaded, 16)
        for c, (lo, hi) in enumerate(self.cuts):
            sp.dma_start(self.wd[0:hi - lo, E - 1, c * D:(c + 1) * D], shared[2][lo:hi, :]).then_inc(self.loaded, 16)
            sp.dma_start(self.wd[0:hi - lo, 0:E - 1, c * D:(c + 1) * D],
                         routed[2][:, lo:hi, :].rearrange("e p d -> p e d")).then_inc(self.loaded, 16)


def experts_swiglu(nc, buffer, Os, tile_expert, ident, experts, rows, slot, lead_copied):
    E, D, H, cuts = experts.E, experts.D, experts.H, experts.cuts
    wg, wu, wd = experts.wg, experts.wu, experts.wd
    NT, LEAD, Zs = tile_expert.shape[1], rows.shape[1], buffer.dram
    HC = len(cuts)
    with Room(nc, "e1") as room:
        sb, sem = room.sb, room.sem
        xs, xT = sb("xs", [P, 2, D]), sb("xT", [P, 2, P])
        sl, hid, hT = sb("sl", [P, 2, H]), sb("hid", [P, 2, H]), sb("hT", [P, 2, HC * P])
        o = sb("o", [P, 2, D])
        warm = sb("warm", [P, 1])
        A, B, HP, XO = (room.ps(n, [P, 2, 512]) for n in ("A", "B", "HP", "XO"))
        names = ("sent", "x_in0", "x_in1", "x_turned", "xT_ok", "A_ok", "B_ok", "silu_ok", "h_ok", "h_turned",
                 "hT_ok", "O_ok", "o_ok", "stored0", "stored1")
        s = {n: sem(n) for n in names}
        x_in, stored = [s["x_in0"], s["x_in1"]], [s["stored0"], s["stored1"]]
        with nc.Block() as block:
            @block.sync
            def _(sp):
                with sp.Fori(0, NT // 2) as j:
                    for q in range(2):
                        T = j * 2 + q
                        sp.wait_ge(s["o_ok"], T + 2)
                        sp.dma_start(Os[ds(T * P, P), :], o[:, q, :]).then_inc(stored[q], 16)
                for q in range(2):
                    sp.wait_ge(stored[q], 16 * (NT // 2) + 1)

            @block.tensor
            def _(pe):
                pe.wait_ge(experts.loaded, 16 * experts.loads)

                def turn_x(T, q, j1):
                    pe.wait_ge(x_in[q], j1 * 16)
                    pe.transpose(XO[:, q, 0:P], xs[:, q, :], ident[:, :]).then_inc(s["x_turned"], 1)

                def up(T, q, e, early, also=None):
                    pe.wait_ge(s["xT_ok"], T + 1)
                    if not early:
                        pe.wait_ge(s["h_ok"], T - 1)
                    pe.matmul(A[:, q, 0:H], xT[:, q, :], wg[:, ds(e, 1), :], start=True, stop=True).then_inc(s["A_ok"], 1)
                    e_also = None if also is None else expert(also)
                    pe.matmul(B[:, q, 0:H], xT[:, q, :], wu[:, ds(e, 1), :], start=True, stop=True).then_inc(s["B_ok"], 1)
                    return e_also

                def turn_h(T, q):
                    pe.wait_ge(s["h_ok"], T + 1)
                    for c, (lo, hi) in enumerate(cuts):
                        last = pe.transpose(HP[0:hi - lo, q, c * P:(c + 1) * P], hid[:, q, lo:hi], ident[:, :])
                    last.then_inc(s["h_turned"], 1)

                def down(T, q, e):
                    pe.wait_ge(s["hT_ok"], T + 1)
                    for c, (lo, hi) in enumerate(cuts):
                        last = pe.matmul(XO[:, q, 256:256 + D], hT[0:hi - lo, q, c * P:(c + 1) * P],
                                         wd[0:hi - lo, ds(e, 1), c * D:(c + 1) * D], start=(c == 0),
                                         stop=(c == HC - 1))
                    last.then_inc(s["O_ok"], 1)

                def expert(T):
                    return pe.value_load(tile_expert[0:1, ds(T, 1)], min_val=0, max_val=E - 1)

                turn_x(0, 0, 1)
                up(0, 0, expert(0), True)
                turn_x(1, 1, 1)
                up(1, 1, expert(1), True)
                turn_x(2, 0, 2)
                turn_h(0, 0)
                for lo, hi in ((0, LEAD // 2 - 1), (LEAD // 2 - 1, NT // 2 - 2)):
                    with pe.Fori(lo, hi) as j:
                        for q in range(2):
                            T = j * 2 + (q + 2)
                            if lo == 0:
                                up(T, q, E - 1, False)
                                e_out = E - 1
                            else:
                                e_out = up(T, q, expert(T), False, T - 2)
                            pe.wait_ge(s["o_ok"], j * 2 + (q + 1))
                            turn_x(T + 1, 1 - q, j + (2 + q))
                            down(T - 2, q, e_out)
                            turn_h(T - 1, 1 - q)
                for T in (NT - 2, NT - 1):
                    q = T % 2
                    up(T, q, expert(T), False)
                    if T + 1 < NT:
                        pe.wait_ge(s["o_ok"], T - 1)
                        turn_x(T + 1, 1 - q, NT // 2)
                    down(T - 2, q, expert(T - 2))
                    turn_h(T - 1, 1 - q)
                down(NT - 2, 0, expert(NT - 2))
                turn_h(NT - 1, 1)
                down(NT - 1, 1, expert(NT - 1))

            @block.scalar
            def _(act):
                def load(T, q):
                    act.dma_start(xs[:, q, :], Zs[ds(T * P, P), :]).then_inc(x_in[q], 16)

                def turn(T, q, more=True):
                    act.wait_ge(s["x_turned"], T + 1)
                    if more:
                        load(T + 2, q)
                    nc.scalar.activation(xT[:, q, :], XO[:, q, 0:P], ACT.Copy).then_inc(s["xT_ok"], 1)

                def silu(T, q):
                    act.wait_ge(s["A_ok"], T + 1)
                    nc.scalar.activation(sl[:, q, :], A[:, q, 0:H], ACT.Silu).then_inc(s["silu_ok"], 1)

                act.wait_ge(lead_copied, 16)
                load(0, 0)
                load(1, 1)
                act.wait_ge(x_in[0], 16)
                nc.scalar.activation(warm[:, :], ident[:, 0:1], ACT.Silu).then_inc(s["o_ok"], 1)
                turn(0, 0)
                lead_steps = LEAD // 2 - 2
                for lo, hi in ((0, lead_steps), (lead_steps, NT // 2 - 2)):
                    if lo:
                        act.wait_ge(s["sent"], 16 * 2 * LEAD)
                    with act.Fori(lo, hi) as j:
                        for q in range(2):
                            turn(j * 2 + (q + 1), 1 - q)
                            silu(j * 2 + q, q)
                turn(NT - 3, 1)
                silu(NT - 4, 0)
                turn(NT - 2, 0, False)
                silu(NT - 3, 1)
                turn(NT - 1, 1, False)
                silu(NT - 2, 0)
                silu(NT - 1, 1)

            @block.gpsimd
            def _(pool):
                buffer.wait(pool)
                for t in range(LEAD):
                    for k in range(2):
                        pool.indirect_dma_start(Zs, bass.IndirectOffsetOnAxis(ap=slot[:, k, t:t + 1], axis=0),
                                                rows[:, t, :], None).then_inc(s["sent"], 16)
                pool.wait_ge(s["sent"], 16 * 2 * LEAD)

            @block.vector
            def _(dve):
                def gate_up(T, q):
                    dve.wait_ge(s["silu_ok"], T + 1)
                    dve.wait_ge(s["B_ok"], T + 1)
                    dve.tensor_tensor(hid[:, q, :], B[:, q, 0:H], sl[:, q, :], ALU.mult).then_inc(s["h_ok"], 1)

                def hidden(T, q):
                    dve.wait_ge(s["h_turned"], T + 1)
                    full = (H // P) * P
                    dve.tensor_copy(hT[:, q, 0:full], HP[:, q, 0:full])
                    last = H - full
                    dve.tensor_copy(hT[0:last, q, full:full + P], HP[0:last, q, full:full + P]).then_inc(s["hT_ok"], 1)

                def out(T, q, j0):
                    dve.wait_ge(s["O_ok"], T + 1)
                    dve.wait_ge(stored[q], j0 * 16 + 1)
                    dve.tensor_copy(o[:, q, :], XO[:, q, 256:256 + D]).then_inc(s["o_ok"], 1)

                for q in range(2):
                    dve.memset(o[:, q, :], 0.0).then_inc(stored[q], 1)
                gate_up(0, 0)
                gate_up(1, 1)
                hidden(0, 0)
                with dve.Fori(0, NT // 2 - 1) as j:
                    for q in range(2):
                        T = j * 2 + (q + 2)
                        gate_up(T, q)
                        out(T - 2, q, j)
                        hidden(T - 1, 1 - q)
                out(NT - 2, 0, NT // 2 - 1)
                hidden(NT - 1, 1)
                out(NT - 1, 1, NT // 2 - 1)


def ffn1(nc, buffer, X, XN, XT, ident, shared, routed, Wr, routing_bias, out):
    T, D, E = X.shape[1], X.shape[2], Wr.shape[1]
    NT, Zs = buffer.NT, buffer.dram
    Os = nc.dram_tensor("ffn1_outs", (NT * P, D), F32, kind="Internal").ap()
    with Room(nc, "f1") as room:
        slot, gate = room.sb("slot", [P, 2, T], U32), room.sb("gate", [P, 2, T])
        score = room.sb("score", [P, T, E])
        tile_expert = room.sb("tile_expert", [1, NT], I32)
        experts = SwigluExperts(room, D, shared[0].shape[1], E)
        lead_copied = room.sem("lead_copied")

        def start_loads(queue):
            router.load(queue)
            experts.load(queue, shared, routed)

        with Room(nc, "rs1") as inner:
            router = Router(inner, Wr, routing_bias, score)
            layernorm(nc, "ln4", X, XN, XT, ident, loads=start_loads, router=router)
            router.finish(nc)
        with nc.Block() as block:
            @block.scalar
            def _(act):
                act.dma_start(Zs[0:T * P, :].rearrange("(t p) d -> p t d", p=P), XN[:, :, :]).then_inc(lead_copied, 16)
        route(nc, "rt1", score, False, slot, gate, tile_expert, T, E)
        experts_swiglu(nc, buffer, Os, tile_expert, ident, experts, XN, slot, lead_copied)
        combine, stored = Combine(room, X, slot, gate, Os, True), room.sem("stored")
        STEP = 2 * combine.GROUP
        with nc.Block() as block:
            @block.gpsimd
            def _(pool):
                combine.gather(pool)

            @block.scalar
            def _(act):
                combine.heads(act)

            @block.vector
            def _(dve):
                combine.add(dve, range(T))

            @block.sync
            def _(sp):
                for t in range(0, T, STEP):
                    sp.wait_ge(combine.second, t + STEP)
                    sp.dma_start(out[:, t:t + STEP, :], X[:, t:t + STEP, :]).then_inc(stored, 16)
                sp.wait_ge(stored, 16 * (T // STEP))


HEADS, HD, GROUP = 16, 8, 4
LEFT, RIGHT = 64, 8
BAND = LEFT + P + RIGHT
PITCH = BAND + P
ROW = GROUP * PITCH + 8
QPARTS, KPARTS = (0, 0, 1, 0, 1, 2), (0, 1, 0, 2, 1, 0)
STACK = HD * len(QPARTS)


class AttentionWeights:

    def __init__(self, room):
        self.wraw, self.bias, self.E0, self.E72, self.et, self.bvb = (
            room.sb("wraw", [P, 4, P]), room.sb("bias", [P, 3]), room.sb("E0", [P, 1]), room.sb("E72", [P, 1]),
            room.sb("et", [HD, LEFT + RIGHT + 1]), room.sb("bvb", [P, P]))
        self.bob = room.sb("bob", [P, P])
        self.loaded, self.loads = room.sem("weights_in"), 4 + 2 + 2 * HEADS + 3

    def load(self, nc, queue, Wq, bq, Wk, bk, Wv, bv, Wo, bo, dist_emb):
        with nc.allow_non_contiguous_dma(reason="small vectors and the embedding's transpose"):
            for k, w in enumerate((Wq, Wk, Wv, Wo)):
                queue.dma_start(self.wraw[:, k, :], w).then_inc(self.loaded, 16)
            for k, v in enumerate((bq, bk)):
                queue.dma_start(self.bias[:, k:k + 1], v.rearrange("(p o) -> p o", o=1)).then_inc(self.loaded, 16)
            for dst, row in ((self.E0, 0), (self.E72, LEFT + RIGHT)):
                for h in range(HEADS):
                    queue.dma_start(dst[HD * h:HD * (h + 1), :],
                                    dist_emb[row:row + 1, :].rearrange("o d -> d o")).then_inc(self.loaded, 16)
            queue.dma_start(self.et[:, :], dist_emb.rearrange("p d -> d p")).then_inc(self.loaded, 16)
            for dst, v in ((self.bvb, bv), (self.bob, bo)):
                queue.dma_start(dst[:, :], v.rearrange("(o d) -> o d", o=1).broadcast_to([P, P])).then_inc(self.loaded, 16)


def attention_inputs(nc, XT, ident, weights, V, ES, parts, skew, skew_bufs):
    NTOK = XT.shape[1]
    SC = 1.0 / float(HD) ** 0.5
    with Room(nc, "ai") as room:
        sb, sem = room.sb, room.sem
        wraw, bias, E0, E72, et, bvb = (weights.wraw, weights.bias, weights.E0, weights.E72, weights.et, weights.bvb)
        wT = sb("wT", [P, 3, P])
        CT, RING = 1024, 3
        NCT = NTOK // CT
        steps = [(a, c) for a in range(3) for c in range(NCT)]
        val, split = sb("val", [P, 2, CT]), sb("split", [P, RING, 3, CT], BF16)
        de = sb("de", [HD, BAND])
        der, ep = sb("der", [HD, BAND]), sb("ep", [HD, 3, BAND], BF16)
        zero = sb("zero", [P, ROW])
        G = room.ps("G", [P, 8, 512])
        turned, wT_ok, step_s, bias_ok, proj, evac, hi_ok, rest_ok, mid_ok, lo_ok, e_sent, vproj, v_ok, zs, zw = (
            sem(n) for n in ("turned", "wT_ok", "dve_step", "bias_ok", "proj", "evac", "hi_ok", "rest_ok",
                             "mid_ok", "lo_ok", "e_sent", "vproj", "v_ok", "zs", "zw"))
        sent = [sem(f"sent{r}") for r in range(RING)]
        sent_by = [16 * sum(2 if steps[m][1] == 0 else 1 for m in range(n % RING, n + 1, RING))
                   for n in range(len(steps))]
        NCH = NTOK // 512
        biases = [bias[:, 0:1], E0[:, :], E72[:, :]]
        with nc.Block() as block:
            @block.sync
            def _(sp):
                sp.wait_ge(zs, 1)
                for k in range(skew_bufs):
                    sp.dma_start(skew[k * P * ROW:(k + 1) * P * ROW].rearrange("(p w) -> p w", p=P),
                                 zero[:, :]).then_inc(zw, 16)
                for n, (a, c) in enumerate(steps):
                    sp.wait_ge(mid_ok, n + 1)
                    sp.wait_ge(lo_ok, n + 1)
                    for at in ((c, NCT) if c == 0 else (c,)):
                        sp.dma_start(parts[a][:, :, at * CT:(at + 1) * CT].rearrange("k p t -> p k t"),
                                     split[:, n % RING, :, :]).then_inc(sent[n % RING], 16)
                for n in range(len(steps) - RING, len(steps)):
                    sp.wait_ge(sent[n % RING], sent_by[n])
                sp.wait_ge(zw, 16 * skew_bufs)
                sp.wait_ge(e_sent, 16 * 6)

            @block.gpsimd
            def _(pool):
                pool.memset(zero[:, :], 0.0).then_inc(zs, 1)
                pool.wait_ge(bias_ok, 1)
                for i, p in enumerate(KPARTS):
                    pool.dma_start(ES[i * HD:(i + 1) * HD, :], ep[:, p, :]).then_inc(e_sent, 16)
                for n in range(len(steps)):
                    pool.wait_ge(mid_ok, n + 1)
                    pool.tensor_tensor(split[:, n % RING, 2, :], val[:, n % 2, :], split[:, n % RING, 1, :],
                                       ALU.subtract).then_inc(lo_ok, 1)
                pool.wait_ge(e_sent, 96)

            @block.tensor
            def _(pe):
                pe.wait_ge(weights.loaded, 16 * weights.loads)
                for k in range(3):
                    last = pe.transpose(G[:, 0, k * P:(k + 1) * P], wraw[:, k, :], ident[:, :])
                last.then_inc(turned, 1)
                pe.wait_ge(wT_ok, 1)
                for n, (a, c) in enumerate(steps):
                    if n >= 3:
                        pe.wait_ge(evac, n - 2)
                    for k in range(2):
                        last = pe.matmul(G[:, 2 * (n % 3) + k, :], wT[:, min(a, 1), :],
                                         XT[:, c * CT + 512 * k:c * CT + 512 * (k + 1)], start=True, stop=True)
                    last.then_inc(proj, 1)
                for g in range(NCH):
                    if g >= 2:
                        pe.wait_ge(v_ok, g - 1)
                    for t in range(4):
                        last = pe.matmul(G[:, 6 + g % 2, t * P:(t + 1) * P], XT[:, (4 * g + t) * P:(4 * g + t + 1) * P],
                                         wT[:, 2, :], start=True, stop=True)
                    last.then_inc(vproj, 1)

            @block.scalar
            def _(act):
                act.wait_ge(bias_ok, 1)
                for n, (a, c) in enumerate(steps):
                    act.wait_ge(proj, n + 1)
                    if n >= 2:
                        act.wait_ge(lo_ok, n - 1)
                    nc.scalar.activation(val[:, n % 2, :], G[:, 2 * (n % 3):2 * (n % 3) + 2, :], ACT.Identity,
                                         bias=biases[a], scale=SC if a == 0 else 1.0).then_inc(evac, 1)
                    act.wait_ge(evac, n + 1)
                    if n >= RING:
                        act.wait_ge(sent[n % RING], sent_by[n - RING])
                    nc.scalar.activation(split[:, n % RING, 0, :], val[:, n % 2, :], ACT.Copy).then_inc(hi_ok, 1)

            @block.vector
            def _(dve):
                step = Steps(dve, step_s)
                dve.wait_ge(weights.loaded, 16 * weights.loads)
                dve.wait_ge(turned, 1)
                dve.tensor_copy(wT[:, :, :], G[:, 0, 0:3 * P].rearrange("p (k m) -> p k m", k=3)).then_inc(wT_ok, 1)
                step(dve.tensor_scalar(bias[:, 0:1], bias[:, 0:1], SC, None, ALU.mult))
                step(dve.tensor_tensor(E0[:, :], E0[:, :], bias[:, 1:2], ALU.add))
                step(dve.tensor_tensor(E72[:, :], E72[:, :], bias[:, 1:2], ALU.add))
                NP = LEFT + RIGHT + 1
                step(dve.tensor_scalar(de[:, 0:NP], et[:, :], et[:, 0:1], None, ALU.subtract))
                step(dve.tensor_copy(de[:, NP:], de[:, NP - 1:NP].broadcast_to([HD, BAND - NP])))
                step(dve.tensor_copy(ep[:, 0, :], de[:, :]))
                step(dve.tensor_tensor(der[:, :], de[:, :], ep[:, 0, :], ALU.subtract))
                step(dve.tensor_copy(ep[:, 1, :], der[:, :]))
                dve.tensor_tensor(ep[:, 2, :], der[:, :], ep[:, 1, :], ALU.subtract).then_inc(bias_ok, 1)
                for n in range(len(steps)):
                    dve.wait_ge(hi_ok, n + 1)
                    dve.tensor_tensor(val[:, n % 2, :], val[:, n % 2, :], split[:, n % RING, 0, :],
                                      ALU.subtract).then_inc(rest_ok, 1)
                    dve.wait_ge(rest_ok, n + 1)
                    dve.tensor_copy(split[:, n % RING, 1, :], val[:, n % 2, :]).then_inc(mid_ok, 1)
                bw = bvb[:, :].rearrange("p (o d) -> p o d", o=1).broadcast_to([P, 4, P])
                for g in range(NCH):
                    dve.wait_ge(vproj, g + 1)
                    dve.tensor_tensor(V[:, 4 * g:4 * g + 4, :], G[:, 6 + g % 2, :].rearrange("p (t d) -> p t d", t=4),
                                      bw, ALU.add).then_inc(v_ok, 1)


def attention(nc, ident, V, ES, parts, skew, O):
    LT = 8
    NL, NU = 2 * LT, 2 * LT * GROUP
    IN = 16 * 3 * len(QPARTS)
    PAIRS = V.shape[1] // LT * (HEADS // GROUP) // 2
    with Room(nc, "at") as room:
        sb, sem = room.sb, room.sem
        st = [[sb(f"stack{s}{a}", [STACK, GROUP, 1024], BF16) for a in range(3)] for s in range(2)]
        Vg = sb("Vg", [P, 2, LT, GROUP, 32])
        qe, band = sb("qe", [P, 2, GROUP, BAND]), sb("band", [P, 4, GROUP, BAND])
        nmax, prob = sb("nmax", [P, 4]), sb("prob", [P, 4, 1024])
        pT = sb("pT", [P, 8, LT, P])
        credit = sb("credit", [P, 3])
        acc_sb, rden = sb("acc_sb", [P, 2, P]), sb("rden", [P, GROUP])
        S = room.ps("S", [P, 2, 1024])
        TP = room.ps("TP", [P, 2, 4, P])
        QE = room.ps("QE", [P, 512])
        AC = room.ps("AC", [P, 512])
        TURNED = 2 * BAND
        turned = sb("turned", [P, 2, GROUP, HD + 1])
        picks = ident[:, :].rearrange("p (h c) -> p h c", h=GROUP)[:, :, 0:HD + 1]
        names = ("v_const", "v_ok", "set0_in", "set1_in", "S_ok", "max_ok", "exp_ok", "ta_ok", "tb_ok", "ea_ok", "eb_ok",
                 "qe_mm", "qe_ok", "skew_out", "band_in0", "band_in1", "band_ok", "av_ok", "acc_ok",
                 "at_ok", "tu_ok", "rd_ok", "out_ok")
        s = {n: sem(n) for n in names}
        set_in = [s["set0_in"], s["set1_in"]]
        band_in = [s["band_in0"], s["band_in1"]]

        with nc.Block() as block:
            @block.gpsimd
            def _(pool):
                def load(k, batch, group):
                    for a, order in enumerate((QPARTS, KPARTS, KPARTS)):
                        for i, which in enumerate(order):
                            src = parts[a][which, ds(group * (GROUP * HD), GROUP * HD), ds(batch * 1024, 1024)]
                            pool.dma_start(st[k][a][i * HD:(i + 1) * HD, :, :],
                                           src.rearrange("(h d) t -> d h t", d=HD)).then_inc(set_in[k], 16)

                pool.memset(Vg[:, :, :, :, :], 0.0).then_inc(s["v_const"], 1)
                pool.wait_ge(s["v_const"], 1)
                pool.memset(Vg[:, :, :, :, HD:HD + 1], 1.0).then_inc(s["v_const"], 1)
                pool.wait_ge(s["v_const"], 2)
                for k, n in enumerate(("av_ok", "ea_ok", "eb_ok")):
                    pool.memset(credit[:, k:k + 1], 0.0).then_inc(s[n], 1)
                load(0, 0, 0)
                with pool.Fori(0, PAIRS) as j:
                    pool.wait_ge(s["av_ok"], j * NL + 1)
                    for k in range(2):
                        b8 = j // 2 * LT
                        hg = (j % 2) * 2 + k
                        pool.tensor_copy(Vg[:, k, :, :, 0:HD],
                                         V[:, ds(b8, LT), ds(hg * GROUP * HD, GROUP * HD)]
                                         .rearrange("p t (h d) -> p t h d", d=HD)).then_inc(s["v_ok"], 1)
                    load(1, j // 2, (j % 2) * 2 + 1)
                    pool.wait_ge(s["S_ok"], j * NU + NU // 2 + 1)
                    load(0, (j + 1) // 2, ((j + 1) % 2) * 2)
                pool.wait_ge(set_in[0], IN * (PAIRS + 1))
                pool.wait_ge(set_in[1], IN * PAIRS)

            @block.sync
            def _(sp):
                def skew_tile(lam, base):
                    sp.wait_ge(s["qe_ok"], (base + lam + 1) * 2)
                    buf = skew[(lam % 4) * P * ROW:(lam % 4 + 1) * P * ROW]
                    rows = buf.rearrange("(p w) -> p w", p=P)[:, 0:GROUP * PITCH].rearrange("p (h w) -> p h w", h=GROUP)
                    sp.dma_start(rows[:, :, 0:BAND], qe[:, lam % 2, :, :]).then_inc(s["skew_out"], 16)
                    sp.wait_ge(s["skew_out"], (base + lam + 1) * 16)
                    skewed = buf[0:P * (ROW - 1)].rearrange("(p w) -> p w", p=P)[:, 0:GROUP * PITCH]
                    sp.dma_start(band[:, lam % 4, :, :], skewed.rearrange("p (h w) -> p h w", h=GROUP)[:, :, 0:BAND]
                                 ).then_inc(band_in[lam % 2], 16)

                skew_tile(0, 0)
                skew_tile(1, 0)
                with sp.Fori(0, PAIRS) as j:
                    for lam in range(2, NL + 2):
                        skew_tile(lam, j * NL)
                for q in range(2):
                    sp.wait_ge(band_in[q], (PAIRS * NL // 2 + 1) * 16)

            @block.tensor
            def _(pe):
                def q_dot_e(lam, half):
                    k, L = (lam // LT) % 2, lam % LT
                    for h in range(2):
                        last = pe.matmul(QE[:, h * BAND:(h + 1) * BAND], st[k][0][:, 2 * half + h, L * P:(L + 1) * P],
                                         ES[:, :], start=True, stop=True)
                    last.then_inc(s["qe_mm"], 1)

                def scores(m):
                    h, k, L = m % GROUP, (m // GROUP // LT) % 2, m // GROUP % LT
                    q = st[k][0][:, h, L * P:(L + 1) * P]
                    cut = min(L * P + P + RIGHT, 1024)
                    for a, (lo, hi) in ((1, (0, cut)), (2, (cut, 1024))):
                        for bank in (0, 512):
                            x, y = max(lo, bank), min(hi, bank + 512)
                            if x < y:
                                last = pe.matmul(S[:, m % 2, x:y], q, st[k][a][:, h, x:y], start=True, stop=True)
                    last.then_inc(s["S_ok"], 1)

                def turn(m, base_u):
                    for half, (ok, out) in enumerate((("ea_ok", "ta_ok"), ("eb_ok", "tb_ok"))):
                        pe.wait_ge(s[ok], base_u + (m + 1))
                        for r in range(4):
                            c = (4 * half + r) * P
                            last = pe.transpose(TP[:, half, r, :], prob[:, m % 4, c:c + P], ident[:, :])
                        last.then_inc(s[out], 1)

                def weigh(lam, j, part):
                    if part == 0:
                        if lam % LT == 0:
                            pe.wait_ge(s["v_ok"], j * 2 + (lam // LT + 1))
                        pe.wait_ge(s["ea_ok"], j * NU + ((lam + 1) * GROUP + 1))
                        pe.wait_ge(s["eb_ok"], j * NU + ((lam + 1) * GROUP + 1))
                        if lam:
                            pe.wait_ge(s["acc_ok"], j * NL + lam)
                    for r in range(3 * part, min(3 * part + 3, LT)):
                        for h in range(GROUP):
                            last = pe.matmul(AC[32 * h:32 * (h + 1), 0:P], Vg[:, lam // LT, r, h, :],
                                             pT[:, (lam * GROUP + h) % 8, r, :], start=(r == 0), stop=(r == LT - 1),
                                             skip_group_check=True)
                    if part == 2:
                        last.then_inc(s["av_ok"], 1)

                def turn_out(lam, j):
                    pe.wait_ge(s["acc_ok"], j * NL + (lam + 1))
                    pe.matmul(QE[:, TURNED:TURNED + GROUP * (HD + 1)], acc_sb[:, lam % 2, :], picks, start=True,
                              stop=True, skip_group_check=True).then_inc(s["at_ok"], 1)

                pe.wait_ge(set_in[0], IN)
                for lam in range(2):
                    for half in range(2):
                        if lam + half:
                            pe.wait_ge(s["qe_ok"], lam * 2 + half)
                        q_dot_e(lam, half)
                scores(0)
                scores(1)
                with pe.Fori(0, PAIRS) as j:
                    for m in range(NU):
                        lam, h = m // GROUP, m % GROUP
                        if h in (0, 2):
                            pe.wait_ge(s["qe_ok"], j * (2 * NL) + ((lam + 2) * 2 + h // 2))
                            if h == 0 and (lam == 0 or lam > 2):
                                pe.wait_ge(s["tu_ok"], j * NL + (max(lam - 2, 0) + 1))
                            if h == 2 and lam >= 2:
                                turn_out(lam - 2, j)
                            if lam + 2 == LT and h == 0:
                                pe.wait_ge(set_in[1], j * IN + IN)
                            if lam + 2 == NL and h == 0:
                                pe.wait_ge(set_in[0], j * IN + 2 * IN)
                            q_dot_e(lam + 2, h // 2)
                        pe.wait_ge(s["exp_ok"], j * NU + (m + 1))
                        scores(m + 2)
                        if lam >= 1 and h:
                            weigh(lam - 1, j, h - 1)
                        turn(m, j * NU)
                    for part in range(3):
                        weigh(NL - 1, j, part)
                    pe.wait_ge(s["qe_ok"], j * (2 * NL) + (NL + 2) * 2)
                    turn_out(NL - 2, j)
                    pe.wait_ge(s["tu_ok"], j * NL + NL)
                    turn_out(NL - 1, j)

            @block.scalar
            def _(act):
                def qe_copy(lam, half, base, wait):
                    act.wait_ge(s["qe_mm"], base * 2 + (lam * 2 + half + 1))
                    if wait:
                        act.wait_ge(s["skew_out"], (base + lam - 1) * 16)
                    nc.scalar.activation(qe[:, lam % 2, 2 * half:2 * half + 2, :],
                                         QE[:, 0:2 * BAND].rearrange("p (h u) -> p h u", h=2),
                                         ACT.Copy).then_inc(s["qe_ok"], 1)

                def copy_turned(m, base_u):
                    act.wait_ge(s["ta_ok"], base_u + (m + 1))
                    nc.scalar.activation(pT[:, m % 8, 0:4, :], TP[:, 0, :, :], ACT.Copy).then_inc(s["ea_ok"], 1)
                    if m % 2:
                        act.wait_ge(s["tb_ok"], base_u + (m + 1))
                        nc.scalar.activation(pT[:, m % 8, 4:8, :], TP[:, 1, :, :], ACT.Copy).then_inc(s["eb_ok"], 1)

                def copy_acc(lam, j):
                    act.wait_ge(s["av_ok"], j * NL + (lam + 2))
                    nc.scalar.activation(acc_sb[:, lam % 2, :], AC[:, 0:P], ACT.Copy).then_inc(s["acc_ok"], 1)

                def copy_output(lam, j):
                    act.wait_ge(s["at_ok"], j * NL + (lam + 1))
                    act.wait_ge(s["out_ok"], j * NL + (lam + 1))
                    nc.scalar.activation(turned[:, lam % 2, :, :], QE[:, TURNED:TURNED + GROUP * (HD + 1)]
                                         .rearrange("p (h c) -> p h c", h=GROUP), ACT.Copy).then_inc(s["tu_ok"], 1)

                for lam in range(2):
                    for half in range(2):
                        qe_copy(lam, half, 0, False)
                with act.Fori(0, PAIRS) as j:
                    for m in range(NU):
                        lam, h = m // GROUP, m % GROUP
                        act.wait_ge(s["max_ok"], j * NU + (m + 1))
                        nc.scalar.activation(prob[:, m % 4, :], S[:, m % 2, :], ACT.Exp,
                                             bias=nmax[:, m % 4:m % 4 + 1]).then_inc(s["exp_ok"], 1)
                        if m:
                            copy_turned(m - 1, j * NU)
                        if h in (1, 3):
                            qe_copy(lam + 2, h // 2, j * NL, True)
                        if lam >= 2 and h == 3:
                            copy_output(lam - 2, j)
                        if lam >= 2 and h == 0:
                            copy_acc(lam - 2, j)
                    copy_turned(NU - 1, j * NU)
                    copy_acc(NL - 2, j)
                    copy_output(NL - 2, j)
                    copy_acc(NL - 1, j)
                    copy_output(NL - 1, j)

            @block.vector
            def _(dve):
                def copy_turned(m, base_u):
                    if m % 2:
                        return
                    dve.wait_ge(s["tb_ok"], base_u + (m + 1))
                    dve.tensor_copy(pT[:, m % 8, 4:8, :], TP[:, 1, :, :]).then_inc(s["eb_ok"], 1)

                def out(lam, j):
                    k, L = lam // LT, lam % LT
                    dve.wait_ge(s["tu_ok"], j * NL + (lam + 2))
                    v = turned[:, lam % 2, :, :]
                    dve.wait_ge(s["out_ok"], j * NL + (lam + 1))
                    dve.reciprocal(rden[:, :], v[:, :, HD]).then_inc(s["rd_ok"], 1)
                    dve.wait_ge(s["rd_ok"], j * NL + (lam + 1))
                    dst = O[:, ds(j // 2 * LT + L, 1), ds(((j % 2) * 2 + k) * GROUP * HD, GROUP * HD)]
                    dve.tensor_tensor(dst.rearrange("p o (h d) -> p (o h) d", d=HD), v[:, :, 0:HD],
                                      rden[:, :].rearrange("p (h o) -> p h o", o=1).broadcast_to([P, GROUP, HD]),
                                      ALU.mult).then_inc(s["out_ok"], 1)

                def negated_max(m, j):
                    lam, h = m // GROUP, m % GROUP
                    L = lam % LT
                    dve.wait_ge(s["S_ok"], j * NU + (m + 1))
                    if h == 0:
                        dve.wait_ge(band_in[lam % 2], j * (NL // 2 * 16) + (lam // 2 + 1) * 16)
                    lo = L * P - LEFT
                    x, y = max(lo, 0), min(lo + BAND, 1024)
                    dve.tensor_tensor(S[:, m % 2, x:y], S[:, m % 2, x:y], band[:, lam % 4, h, x - lo:y - lo],
                                      ALU.add).then_inc(s["band_ok"], 1)
                    dve.wait_ge(s["band_ok"], j * NU + (m + 1))
                    dve.tensor_reduce(nmax[:, m % 4:m % 4 + 1], S[:, m % 2, :], AX, ALU.max,
                                      negate=True).then_inc(s["max_ok"], 1)

                dve.memset(rden[:, :], 0.0).then_inc(s["out_ok"], 1)
                dve.memset(turned[:, :, :, :], 0.0).then_inc(s["tu_ok"], 1)
                negated_max(0, 0)
                with dve.Fori(0, PAIRS) as j:
                    for m in range(NU):
                        lam, h = m // GROUP, m % GROUP
                        negated_max(m + 1, j)
                        if m:
                            copy_turned(m - 1, j * NU)
                        if lam >= 3 and h == 0:
                            out(lam - 3, j)
                    copy_turned(NU - 1, j * NU)
                    out(NL - 3, j)
                    out(NL - 2, j)
                    out(NL - 1, j)


def attention_output(nc, X, O, OT, ident, weights):
    wraw, bob = weights.wraw, weights.bob
    T = X.shape[1]
    with Room(nc, "ao") as room:
        wT = room.sb("wT", [P, P])
        G = room.ps("G", [P, 8, 4, P])
        w_turned, w_ok, turned, copied, made, added, biased = (
            room.sem(n) for n in ("w_turned", "w_ok", "turned", "copied", "made", "added", "biased"))
        NG = T // 4
        with nc.Block() as block:
            @block.tensor
            def _(pe):
                pe.transpose(G[:, 0, 0, :], wraw[:, 3, :], ident[:, :]).then_inc(w_turned, 1)
                pe.wait_ge(w_ok, 1)
                for g in range(NG):
                    if g >= 4:
                        pe.wait_ge(copied, g - 3)
                    for t in range(4):
                        last = pe.transpose(G[:, g % 4, t, :], O[:, 4 * g + t, :], ident[:, :])
                    last.then_inc(turned, 1)
                for g in range(NG):
                    pe.wait_ge(copied, g + 1)
                    if g >= 4:
                        pe.wait_ge(added, g - 3)
                    for t in range(4):
                        tok = (4 * g + t) * P
                        last = pe.matmul(G[:, 4 + g % 4, t, :], OT[:, tok:tok + P], wT[:, :], start=True, stop=True)
                    last.then_inc(made, 1)

            @block.scalar
            def _(act):
                for g in range(NG):
                    act.wait_ge(turned, g + 1)
                    nc.scalar.activation(OT[:, 512 * g:512 * (g + 1)], G[:, g % 4, :, :], ACT.Copy).then_inc(copied, 1)

            @block.vector
            def _(dve):
                dve.wait_ge(w_turned, 1)
                dve.tensor_copy(wT[:, :], G[:, 0, 0, :]).then_inc(w_ok, 1)
                bw = bob[:, :].rearrange("p (o d) -> p o d", o=1).broadcast_to([P, T, P])
                dve.tensor_tensor(X[:, :, :], X[:, :, :], bw, ALU.add).then_inc(biased, 1)
                dve.wait_ge(biased, 1)
                for g in range(NG):
                    dve.wait_ge(made, g + 1)
                    xs = X[:, 4 * g:4 * g + 4, :]
                    dve.tensor_tensor(xs, xs, G[:, 4 + g % 4, :, :], ALU.add).then_inc(added, 1)


def attn1(nc, X, update, XN, XT, ident, Wq, bq, Wk, bk, Wv, bv, Wo, bo, dist_emb):
    T = X.shape[1]
    parts = [nc.dram_tensor(f"parts_{n}", (3, P, T * P + 1024), BF16, kind="Internal").ap()
             for n in ("q", "k_left", "k_right")]
    skew = nc.dram_tensor("skew", (4 * P * ROW,), F32, kind="Internal").ap()
    with Room(nc, "a1") as room:
        weights = AttentionWeights(room)
        layernorm(nc, "ln3", X, XN, XT, ident, update=update,
                  loads=lambda queue: weights.load(nc, queue, Wq, bq, Wk, bk, Wv, bv, Wo, bo, dist_emb))
        with Room(nc, "a2") as inner:
            V, ES = inner.sb("V", [P, T, P]), inner.sb("ES", [STACK, BAND], BF16)
            attention_inputs(nc, XT, ident, weights, V, ES, parts, skew, 4)
            attention(nc, ident, V, ES, parts, skew, XN)
        attention_output(nc, X, XN, XT, ident, weights)


def two_layers(nc, x, mamba_w, ffn0_w, attn_w, ffn1_w, out):
    tokens, D = x.shape[0] * x.shape[1], x.shape[2]
    with Room(nc, "all") as room:
        X, XN = room.sb("X", [P, tokens // P, D]), room.sb("XN", [P, tokens // P, D])
        XT = room.sb("XT", [P, tokens])
        ident, zero = room.sb("ident", [P, P]), room.sb("zero", [P, 8 * D])
        T = tokens // P
        buffers = [RowBuffer(nc, room, "ffn0", T, D, ffn0_w[2].shape[1], 0),
                   RowBuffer(nc, room, "ffn1", T, D, ffn1_w[6].shape[1], T)]
        with Room(nc, "mw") as inner:
            W_in, conv_w, _, W_x, W_dt, _, A_log, _, W_out = mamba_w
            weights = MambaWeights(inner, W_in, conv_w, W_x, W_dt, A_log, W_out)
            load_constants(nc, x, X, ident, zero)

            def start_transfers(queue):
                weights.load(nc, queue, *mamba_w)
                for buffer in buffers:
                    buffer.clear(queue, zero)

            layernorm(nc, "ln0", X, XN, XT, ident, loads=start_transfers)
            mamba(nc, X, XT, ident, weights)
        with Room(nc, "mo") as inner:
            update = ffn0(nc, inner, buffers[0], X, XN, XT, ident, *ffn0_w)
            attn1(nc, X, update, XN, XT, ident, *attn_w)
        ffn1(nc, buffers[1], X, XN, XT, ident, ffn1_w[0:3], ffn1_w[3:6], *ffn1_w[6:8],
             out.rearrange("b (t p) d -> p (b t) d", p=P))


_PARTS = [
    ["L0_attn_x"],
    ["L0_attn_" + n for n in ("W_in", "conv_w", "conv_b", "W_x", "W_dt", "b_dt", "A_log", "D", "W_out")],
    ["L0_ffn_" + n for n in ("ln_g", "ln_b", "router_w", "eg", "eb", "W1", "b1", "W2", "b2", "Wo", "bo")],
    ["L1_attn_" + n for n in ("Wq", "bq", "Wk", "bk", "Wv", "bv", "Wo", "bo", "dist_emb")],
    ["L1_ffn_" + n for n in ("shared_gate", "shared_up", "shared_down", "routed_gate", "routed_up", "routed_down", "Wr",
                             "routing_bias")],
]


def kernel(**inputs):
    import numpy as _np
    import concourse.bacc as _bacc
    from concourse import mybir as _mybir
    from concourse.bass_utils import run_bass_kernel_spmd as _run

    nc = _bacc.Bacc("TRN2", target_bir_lowering=False, num_devices=1)
    arrays, args = {}, []
    for part in _PARTS:
        args.append([])
        for name in part:
            a = _np.ascontiguousarray(inputs[name])
            arrays[f"in_{name}_dram"] = a
            args[-1].append(nc.dram_tensor(f"in_{name}_dram", a.shape, _mybir.dt.from_np(a.dtype),
                                           kind="ExternalInput").ap())
    out = nc.dram_tensor("out_0_dram", arrays["in_L0_attn_x_dram"].shape, _mybir.dt.float32,
                         kind="ExternalOutput").ap()
    two_layers(nc, args[0][0], *args[1:], out)
    r = _run(nc, [arrays], core_ids=[0])
    return r.results[0]["out_0_dram"]
```
